# Optimizing a Trainium2 kernel written in Bass

```python
import numpy as np
import jax
import jax.numpy as jnp

def _softmax(x, axis=-1):
    return jax.nn.softmax(x, axis=axis)

def _gelu(x):
    return jax.nn.gelu(x, approximate=True)

def _silu(x):
    return jax.nn.silu(x)

def _sigmoid(x):
    return jax.nn.sigmoid(x)

def _layernorm(x, axis=-1, eps=1e-05):
    m = jnp.mean(x, axis=axis, keepdims=True)
    v = jnp.var(x, axis=axis, keepdims=True)
    return (x - m) / jnp.sqrt(v + eps)

def _scatter_add(tgt, idx, src, axis=0):
    return tgt.at[idx].add(src)

def _segment_sum(src, seg, n):
    return jax.ops.segment_sum(src, seg, n)
kernel_name = 'mk_prb_d1_jaxref_r8_b76f73'

def setup_inputs(seed: int=0):
    np.random.seed(seed)
    _w = jnp.asarray

    def _L0_attn_setup():
        import jax, jax.numpy as jnp
        import numpy as np
        D_MODEL = 128
        D_STATE = 128
        EXPAND = 2
        HEADDIM = 64
        NGROUPS = 1
        D_INNER = EXPAND * D_MODEL
        NHEADS = D_INNER // HEADDIM
        N_ANGLES = D_STATE // 2 // 2
        CHUNK = 64
        DT_MIN, DT_MAX, DT_FLOOR, A_FLOOR = (0.001, 0.1, 0.0001, 0.0001)
        EPS = 1e-05
        BATCH, SEQLEN = (2, 256)

        def _rope(t, theta):
            na = theta.shape[-1]
            x1, x2, rest = (t[..., :na], t[..., na:2 * na], t[..., 2 * na:])
            c, s = (jnp.cos(theta), jnp.sin(theta))
            return jnp.concatenate([x1 * c - x2 * s, x1 * s + x2 * c, rest], axis=-1)

        def _rmsnorm(t, w):
            var = jnp.mean(t * t, axis=-1, keepdims=True)
            return t * jax.lax.rsqrt(var + EPS) * w

        def _forward(u, W_in, W_out, dt_bias, B_bias, C_bias, B_norm_w, C_norm_w, D):
            b, L, _ = u.shape
            proj = u @ W_in
            sizes = [D_INNER, D_INNER, D_STATE * NGROUPS, D_STATE * NGROUPS, NHEADS, NHEADS, NHEADS, N_ANGLES]
            z, x, Bg, Cg, dd_dt, dd_A, trap, angles = jnp.split(proj, np.cumsum(sizes)[:-1], axis=-1)
            z = z.reshape(b, L, NHEADS, HEADDIM)
            x = x.reshape(b, L, NHEADS, HEADDIM)
            a = jnp.minimum(-jax.nn.softplus(dd_A), -A_FLOOR)
            dt = jax.nn.softplus(dd_dt + dt_bias)
            adt = a * dt
            theta = jnp.cumsum(angles[:, :, None, :] * dt[..., None], axis=1)
            Bn = _rmsnorm(Bg, B_norm_w)
            Cn = _rmsnorm(Cg, C_norm_w)
            K = _rope(Bn[:, :, None, :] + B_bias, theta)
            Q = _rope(Cn[:, :, None, :] + C_bias, theta)
            beta = jax.nn.sigmoid(trap)
            g1 = beta * dt
            dt_prev = jnp.pad(dt[:, :-1], ((0, 0), (1, 0), (0, 0)))
            g2 = (1.0 - beta) * jnp.exp(adt) * dt_prev
            Kp = jnp.pad(K[:, :-1], ((0, 0), (1, 0), (0, 0), (0, 0)))
            xp = jnp.pad(x[:, :-1], ((0, 0), (1, 0), (0, 0), (0, 0)))
            nc = L // CHUNK
            ch = lambda t: t.reshape(b, nc, CHUNK, *t.shape[2:])
            Qc, Kc, Kpc, xc, xpc = (ch(Q), ch(K), ch(Kp), ch(x), ch(xp))
            g1c, g2c, adtc = (ch(g1), ch(g2), ch(adt))
            ell = jnp.cumsum(adtc, axis=2)
            decay = jnp.exp(ell[:, :, :, None, :] - ell[:, :, None, :, :])
            mask = jnp.tril(jnp.ones((CHUNK, CHUNK), bool))
            decay = jnp.where(mask[None, None, :, :, None], decay, 0.0)
            S1 = jnp.einsum('bcihn,bcjhn->bcijh', Qc, Kc) * g1c[:, :, None, :, :] * decay
            S2 = jnp.einsum('bcihn,bcjhn->bcijh', Qc, Kpc) * g2c[:, :, None, :, :] * decay
            y_intra = jnp.einsum('bcijh,bcjhp->bcihp', S1, xc) + jnp.einsum('bcijh,bcjhp->bcihp', S2, xpc)
            dec_end = jnp.exp(ell[:, :, -1:, :] - ell)
            Wsum = jnp.einsum('bcjh,bcjhp,bcjhn->bchpn', g1c * dec_end, xc, Kc) + jnp.einsum('bcjh,bcjhp,bcjhn->bchpn', g2c * dec_end, xpc, Kpc)
            chunk_decay = jnp.exp(ell[:, :, -1, :])

            def step(Hprev, inp):
                wc, cd = inp
                return (cd[:, :, None, None] * Hprev + wc, Hprev)
            H0 = jnp.zeros((b, NHEADS, HEADDIM, D_STATE), u.dtype)
            _, Hprevs = jax.lax.scan(step, H0, (jnp.moveaxis(Wsum, 1, 0), jnp.moveaxis(chunk_decay, 1, 0)))
            Hprevs = jnp.moveaxis(Hprevs, 0, 1)
            y_inter = jnp.einsum('bcihn,bcih,bchpn->bcihp', Qc, jnp.exp(ell), Hprevs)
            y = (y_intra + y_inter).reshape(b, L, NHEADS, HEADDIM)
            y = y + D[None, None, :, None] * x
            y = y * jax.nn.silu(z)
            return y.reshape(b, L, D_INNER) @ W_out
        key = jax.random.key(seed)
        ks = jax.random.split(key, 4)
        d_in_proj = 2 * D_INNER + 2 * D_STATE * NGROUPS + 3 * NHEADS + N_ANGLES
        u = jax.random.normal(ks[0], (BATCH, SEQLEN, D_MODEL), jnp.float32)
        W_in = jax.random.normal(ks[1], (D_MODEL, d_in_proj), jnp.float32) * 0.02
        W_out = jax.random.normal(ks[2], (D_INNER, D_MODEL), jnp.float32) * 0.02
        _dt = jnp.exp(jax.random.uniform(ks[3], (NHEADS,), jnp.float32) * (np.log(DT_MAX) - np.log(DT_MIN)) + np.log(DT_MIN))
        _dt = jnp.maximum(_dt, DT_FLOOR)
        dt_bias = _dt + jnp.log(-jnp.expm1(-_dt))
        return dict(u=u, W_in=W_in, W_out=W_out, dt_bias=dt_bias, B_bias=jnp.ones((NHEADS, D_STATE), jnp.float32), C_bias=jnp.ones((NHEADS, D_STATE), jnp.float32), B_norm_w=jnp.ones((D_STATE,), jnp.float32), C_norm_w=jnp.ones((D_STATE,), jnp.float32), D=jnp.ones((NHEADS,), jnp.float32))
    _L0_attn_in = _L0_attn_setup()

    def _L0_ffn_setup():
        import jax, jax.numpy as jnp
        import numpy as np
        B, N, D, F, E, K = (4, 256, 128, 512, 16, 2)
        EPS = 1e-05
        key = jax.random.key(seed)
        ks = jax.random.split(key, 6)
        scaled = lambda k, shape, fan: jax.random.normal(k, shape, jnp.float32) / np.float32(np.sqrt(fan))
        return {'x': jax.random.normal(ks[0], (B, N, D), jnp.float32), 'Wr': scaled(ks[1], (D, E), D), 'br': jnp.zeros((E,), jnp.float32), 'W1': scaled(ks[2], (E, D, F), D), 'W3': scaled(ks[3], (E, D, F), D), 'W2': scaled(ks[4], (E, F, D), F), 'gamma': jnp.ones((E, D), jnp.float32), 'beta': jnp.zeros((E, D), jnp.float32)}
    _L0_ffn_in = _L0_ffn_setup()
    _d = {'L0_attn_u': _L0_attn_in['u'], 'L0_attn_W_in': _L0_attn_in['W_in'], 'L0_attn_W_out': _L0_attn_in['W_out'], 'L0_attn_dt_bias': _L0_attn_in['dt_bias'], 'L0_attn_B_bias': _L0_attn_in['B_bias'], 'L0_attn_C_bias': _L0_attn_in['C_bias'], 'L0_attn_B_norm_w': _L0_attn_in['B_norm_w'], 'L0_attn_C_norm_w': _L0_attn_in['C_norm_w'], 'L0_attn_D': _L0_attn_in['D'], 'L0_ffn_Wr': _L0_ffn_in['Wr'], 'L0_ffn_br': _L0_ffn_in['br'], 'L0_ffn_W1': _L0_ffn_in['W1'], 'L0_ffn_W3': _L0_ffn_in['W3'], 'L0_ffn_W2': _L0_ffn_in['W2'], 'L0_ffn_gamma': _L0_ffn_in['gamma'], 'L0_ffn_beta': _L0_ffn_in['beta']}
    _x0 = _d['L0_attn_u']
    _d['L0_attn_u'] = jax.random.normal(jax.random.fold_in(jax.random.key(seed), 1), (4, 512, 128), dtype=_x0.dtype)
    del _x0
    return _d

def reference(L0_attn_u, L0_attn_W_in, L0_attn_W_out, L0_attn_dt_bias, L0_attn_B_bias, L0_attn_C_bias, L0_attn_B_norm_w, L0_attn_C_norm_w, L0_attn_D, L0_ffn_Wr, L0_ffn_br, L0_ffn_W1, L0_ffn_W3, L0_ffn_W2, L0_ffn_gamma, L0_ffn_beta):

    def _L0_attn_ref(u, W_in, W_out, dt_bias, B_bias, C_bias, B_norm_w, C_norm_w, D):
        import jax, jax.numpy as jnp
        import numpy as np
        D_MODEL = 128
        D_STATE = 128
        EXPAND = 2
        HEADDIM = 64
        NGROUPS = 1
        D_INNER = EXPAND * D_MODEL
        NHEADS = D_INNER // HEADDIM
        N_ANGLES = D_STATE // 2 // 2
        CHUNK = 64
        DT_MIN, DT_MAX, DT_FLOOR, A_FLOOR = (0.001, 0.1, 0.0001, 0.0001)
        EPS = 1e-05
        BATCH, SEQLEN = (2, 256)

        def _rope(t, theta):
            na = theta.shape[-1]
            x1, x2, rest = (t[..., :na], t[..., na:2 * na], t[..., 2 * na:])
            c, s = (jnp.cos(theta), jnp.sin(theta))
            return jnp.concatenate([x1 * c - x2 * s, x1 * s + x2 * c, rest], axis=-1)

        def _rmsnorm(t, w):
            var = jnp.mean(t * t, axis=-1, keepdims=True)
            return t * jax.lax.rsqrt(var + EPS) * w

        def _forward(u, W_in, W_out, dt_bias, B_bias, C_bias, B_norm_w, C_norm_w, D):
            b, L, _ = u.shape
            proj = u @ W_in
            sizes = [D_INNER, D_INNER, D_STATE * NGROUPS, D_STATE * NGROUPS, NHEADS, NHEADS, NHEADS, N_ANGLES]
            z, x, Bg, Cg, dd_dt, dd_A, trap, angles = jnp.split(proj, np.cumsum(sizes)[:-1], axis=-1)
            z = z.reshape(b, L, NHEADS, HEADDIM)
            x = x.reshape(b, L, NHEADS, HEADDIM)
            a = jnp.minimum(-jax.nn.softplus(dd_A), -A_FLOOR)
            dt = jax.nn.softplus(dd_dt + dt_bias)
            adt = a * dt
            theta = jnp.cumsum(angles[:, :, None, :] * dt[..., None], axis=1)
            Bn = _rmsnorm(Bg, B_norm_w)
            Cn = _rmsnorm(Cg, C_norm_w)
            K = _rope(Bn[:, :, None, :] + B_bias, theta)
            Q = _rope(Cn[:, :, None, :] + C_bias, theta)
            beta = jax.nn.sigmoid(trap)
            g1 = beta * dt
            dt_prev = jnp.pad(dt[:, :-1], ((0, 0), (1, 0), (0, 0)))
            g2 = (1.0 - beta) * jnp.exp(adt) * dt_prev
            Kp = jnp.pad(K[:, :-1], ((0, 0), (1, 0), (0, 0), (0, 0)))
            xp = jnp.pad(x[:, :-1], ((0, 0), (1, 0), (0, 0), (0, 0)))
            nc = L // CHUNK
            ch = lambda t: t.reshape(b, nc, CHUNK, *t.shape[2:])
            Qc, Kc, Kpc, xc, xpc = (ch(Q), ch(K), ch(Kp), ch(x), ch(xp))
            g1c, g2c, adtc = (ch(g1), ch(g2), ch(adt))
            ell = jnp.cumsum(adtc, axis=2)
            decay = jnp.exp(ell[:, :, :, None, :] - ell[:, :, None, :, :])
            mask = jnp.tril(jnp.ones((CHUNK, CHUNK), bool))
            decay = jnp.where(mask[None, None, :, :, None], decay, 0.0)
            S1 = jnp.einsum('bcihn,bcjhn->bcijh', Qc, Kc) * g1c[:, :, None, :, :] * decay
            S2 = jnp.einsum('bcihn,bcjhn->bcijh', Qc, Kpc) * g2c[:, :, None, :, :] * decay
            y_intra = jnp.einsum('bcijh,bcjhp->bcihp', S1, xc) + jnp.einsum('bcijh,bcjhp->bcihp', S2, xpc)
            dec_end = jnp.exp(ell[:, :, -1:, :] - ell)
            Wsum = jnp.einsum('bcjh,bcjhp,bcjhn->bchpn', g1c * dec_end, xc, Kc) + jnp.einsum('bcjh,bcjhp,bcjhn->bchpn', g2c * dec_end, xpc, Kpc)
            chunk_decay = jnp.exp(ell[:, :, -1, :])

            def step(Hprev, inp):
                wc, cd = inp
                return (cd[:, :, None, None] * Hprev + wc, Hprev)
            H0 = jnp.zeros((b, NHEADS, HEADDIM, D_STATE), u.dtype)
            _, Hprevs = jax.lax.scan(step, H0, (jnp.moveaxis(Wsum, 1, 0), jnp.moveaxis(chunk_decay, 1, 0)))
            Hprevs = jnp.moveaxis(Hprevs, 0, 1)
            y_inter = jnp.einsum('bcihn,bcih,bchpn->bcihp', Qc, jnp.exp(ell), Hprevs)
            y = (y_intra + y_inter).reshape(b, L, NHEADS, HEADDIM)
            y = y + D[None, None, :, None] * x
            y = y * jax.nn.silu(z)
            return y.reshape(b, L, D_INNER) @ W_out
        return _forward(u, W_in, W_out, dt_bias, B_bias, C_bias, B_norm_w, C_norm_w, D)

    def _L0_ffn_ref(x, Wr, br, W1, W3, W2, gamma, beta):
        import jax, jax.numpy as jnp
        import numpy as np
        B, N, D, F, E, K = (4, 256, 128, 512, 16, 2)
        EPS = 1e-05
        b, n, d = x.shape
        e = Wr.shape[1]
        xf = x.reshape(-1, d)
        logits = xf @ Wr + br
        probs = jax.nn.softmax(logits, axis=-1)
        vals, idx = jax.lax.top_k(probs, K)
        w = vals / vals.sum(axis=-1, keepdims=True)
        combine = jnp.zeros((xf.shape[0], e), x.dtype)
        for k in range(K):
            combine = combine + w[:, k:k + 1] * jax.nn.one_hot(idx[:, k], e, dtype=x.dtype)
        out = jnp.zeros_like(xf)
        for ei in range(e):
            h = jax.nn.silu(xf @ W1[ei]) * (xf @ W3[ei])
            y = h @ W2[ei]
            mu = y.mean(axis=-1, keepdims=True)
            var = ((y - mu) ** 2).mean(axis=-1, keepdims=True)
            y = (y - mu) * jax.lax.rsqrt(var + EPS) * gamma[ei] + beta[ei]
            out = out + combine[:, ei:ei + 1] * y
        return out.reshape(b, n, d)
    x = L0_attn_u
    xn = _layernorm(x, axis=-1)
    x = x + _L0_attn_ref(xn, L0_attn_W_in, L0_attn_W_out, L0_attn_dt_bias, L0_attn_B_bias, L0_attn_C_bias, L0_attn_B_norm_w, L0_attn_C_norm_w, L0_attn_D) + _L0_ffn_ref(xn, L0_ffn_Wr, L0_ffn_br, L0_ffn_W1, L0_ffn_W3, L0_ffn_W2, L0_ffn_gamma, L0_ffn_beta)
    return x

_drawn_inputs = setup_inputs


def setup_inputs(seed=0):
    import zlib

    import numpy as np

    out = dict(_drawn_inputs(seed))
    spreads = {'L0_attn_B_bias': (1.0, 0.6),
     'L0_attn_C_bias': (1.0, 0.6),
     'L0_attn_B_norm_w': (1.0, 0.6),
     'L0_attn_C_norm_w': (1.0, 0.6),
     'L0_attn_D': (1.0, 0.6),
     'L0_ffn_br': (0.0, 0.1),
     'L0_ffn_gamma': (1.0, 0.2),
     'L0_ffn_beta': (0.0, 0.1)}
    factors = {}
    for name, (base, spread) in spreads.items():
        noise = np.random.default_rng([zlib.crc32(name.encode()), seed]).standard_normal(out[name].shape)
        drawn = base * np.exp(spread * noise) if base else spread * noise
        out[name] = jnp.asarray(drawn.astype(out[name].dtype))
    for name, factor in factors.items():
        out[name] = (out[name] * factor).astype(out[name].dtype)
    return out
```

```python
import concourse.bass as bass
from concourse import mybir
from contextlib import ExitStack


def build(nc, A_u, A_Win, A_Wout, A_dtb, A_Bb, A_Cb, A_Bw, A_Cw, A_D, A_Wr, A_br, A_W1, A_W3, A_W2,
          A_gamma, A_beta, A_out):
    fp32, bf16, i32 = mybir.dt.float32, mybir.dt.bfloat16, mybir.dt.int32
    ALU = mybir.AluOpType
    ACT = mybir.ActivationFunctionType
    X = mybir.AxisListType.X

    P = 128
    NBATCH, SEQ, DM = A_u.shape
    NT = NBATCH * SEQ // P
    TB = SEQ // P
    T = NT * P
    NH, DS = A_Bb.shape
    DI = A_Wout.shape[0]
    HD = DI // NH
    NA = (A_Win.shape[1] - 2 * DI - 2 * DS - 3 * NH)
    NE, _, F = A_W1.shape
    FC = F // P
    TOPK = 2
    ZX, BC = 2 * DI, 2 * DS
    NARROW = 3 * NH + NA + NE
    WIDE = ZX + BC
    NB = (TOPK * T - NE) // P + NE
    NROWS = NB * P
    ROW = DM + 2
    SOLO = 4
    JOINT = NT - SOLO
    SLOTS = 4
    LAST = NB - 1 - SLOTS * (JOINT - 1)
    assert 0 < LAST <= SLOTS and NA == 32
    EPS = 1e-5
    A_FLOOR = 1e-4
    MAGIC = 1.5 * 2.0 ** 23
    INV_2PI = 0.15915494309189535
    TWO_PI = 6.2831845
    NEG = -1e30

    rows_dram = nc.dram_tensor("rows_dram", [NROWS, ROW], fp32, kind="Internal").ap()
    res_dram = nc.dram_tensor("res_dram", [TOPK * T + NROWS, DM], fp32, kind="Internal").ap()

    ctx = ExitStack()
    with ctx:
        def sb(name, shape, dt=fp32):
            return ctx.enter_context(nc.sbuf_tensor(name, shape, dt))

        def sem(name):
            return ctx.enter_context(nc.semaphore(name))

        def sems(name, n):
            return [sem(f"{name}{j}") for j in range(n)]

        bank = [ctx.enter_context(nc.psum_tensor(f"bank{i}", [P, 512], fp32)) for i in range(8)]

        w1 = sb("w1", [P, NE, F])
        w3 = sb("w3", [P, NE, F])
        w2 = sb("w2", [P, NE, FC, DM])
        w_in = sb("w_in", [P, WIDE + NARROW])
        w_out = sb("w_out", [P, 2, DM])
        gam = sb("gam", [P, NE, DM])
        beta_e = sb("beta_e", [NE, DM])
        bias_kq = sb("bias_kq", [P, 2, NH, DS])
        nw_kq = sb("nw_kq", [P, 2, DS])
        br = sb("br", [P, NE])
        dtb = sb("dtb", [P, NH])
        dskip = sb("dskip", [P, NH])
        ident = sb("ident", [P, P])
        iota_e = sb("iota_e", [P, NE])
        iota_b = sb("iota_b", [1, NB])
        mhalf = sb("mhalf", [P, NT])

        acc = sb("acc", [P, NT, DM])
        xnT = sb("xnT", [P, T])
        xrow = sb("xrow", [P, NT, ROW])
        theta = sb("theta", [P, NT, NH * NA])
        decay = sb("decay", [P, NT, NH * P])
        rows0 = decay[:, :, :].rearrange("p t c -> p (t c)")[:, 0:NB * ROW]\
            .rearrange("p (b c) -> p b c", c=ROW)
        eL = sb("eL", [P, 3, NT, NH])
        coefG = sb("coefG", [P, NT, NH])
        coefH = sb("coefH", [P, NT, NH])
        wstate = sb("wstate", [P, NT, NH])
        slots_f = sb("slots_f", [P, TOPK, NT])
        slots = sb("slots", [P, TOPK, NT], i32)
        wtop = sb("wtop", [P, TOPK, NT])
        blk_e = sb("blk_e", [1, NB], i32)

        xt_s = sb("xt_s", [P, P])
        ms = sb("ms", [P, 2])
        rms = sb("rms", [P, 2])
        kq = sb("kq", [P, 2, NH, DS])
        ang = sb("ang", [P, 2, NH * NA])
        angk = sb("angk", [P, 2, NH * NA])
        trig = sb("trig", [P, 2, NH, NA])
        rot = sb("rot", [P, 4, 2, NH, NA])
        kqT = sb("kqT", [P, 2, NH * P])
        qkp = rot[:, 0:2].rearrange("p r q h n -> p (r q h n)").rearrange("p (h n) -> p h n", n=DS)
        qk = sb("qk", [P, NH])
        coef = sb("coef", [P, NH])
        sd = sb("sd", [P, NH, P])
        bn_kq = sd[:, 0:2, :]
        xg_w = sb("xg_w", [P, NH, HD])
        xs_w = sb("xs_w", [P, NH, HD])
        xc_w = angk[:, :, :].rearrange("p a (b d) -> p (a b) d", d=HD)
        gate = sb("gate", [P, DI])
        ysum = sb("ysum", [P, NH, HD])
        yT = xg_w[:, :, :].rearrange("p h d -> p (h d)")
        state = sb("state", [P, NH, HD])

        blk = sb("blk", [P, SLOTS, ROW])
        blkT = sb("blkT", [P, 2, P])
        rows_end = xrow[:, :, :].rearrange("p t c -> p (t c)")
        gl, hm, hT = (rows_end[:, n * F:(n + 1) * F] for n in range(3))
        res = rows_end[:, 3 * F:3 * F + SLOTS * DM].rearrange("p (j d) -> p j d", d=DM)
        st6 = sb("st6", [P, 6])
        mv = sb("mv", [P, 2])
        rstd = sb("rstd", [P, 1])
        rw = sb("rw", [P, 1])
        yc = sb("yc", [P, DM])

        used = [0]

        def scratch(shape, dt=fp32):
            n = 1
            for s in shape[1:]:
                n *= s
            flat = w2[:, :, :, :].rearrange("p a b c -> p (a b c)")
            words = n if dt != bf16 else (n + 1) // 2
            v = flat[:, used[0]:used[0] + words]
            used[0] += words
            if dt != fp32:
                v = v.bitcast(dt)
            if len(shape) == 3:
                v = v.rearrange("p (a b) -> p a b", b=shape[2])
            if len(shape) == 4:
                v = v.rearrange("p (a b c) -> p a b c", b=shape[2], c=shape[3])
            return v

        tri = scratch([P, P])
        low = scratch([P, P])
        ones = scratch([P, P])
        shift = scratch([P, P])
        wrap = scratch([P, P])
        ident_h = scratch([P, P], bf16)
        tri_h = scratch([P, P], bf16)
        ones_h = scratch([P, P], bf16)
        neg_h = scratch([P, NH, P], bf16)
        stats = scratch([P, NT, 6])
        mvx = scratch([P, NT, 2])
        vx = scratch([P, NT])
        rx = scratch([P, NT])
        nar = scratch([P, NT, NARROW])
        turns = scratch([P, NT, NH * NA])
        tpre = scratch([P, NBATCH, TB - 1, NH * NA])
        lg, rt, sc1, posb, pick = (
            tpre.rearrange("p b j c -> p (b j c)")[:, n * NT * NE:(n + 1) * NT * NE]
            .rearrange("p (t e) -> p t e", e=NE) for n in range(5))
        cmpb = turns.rearrange("p t c -> p (t c)")[0:1, 0:NB * NE].rearrange("p (b e) -> p b e", e=NE)
        sp_x = scratch([P, 2, NT * NH])
        sp_e = scratch([P, 2, NT * NH])
        sp_u = scratch([P, 2, NT * NH])
        sp_l = scratch([P, 2, NT * NH])
        sp_r = scratch([P, 2, NT * NH])
        sp_t = scratch([P, 2, NT * NH])
        sp = scratch([P, 2, NT, NH])
        adt = scratch([P, NT, NH])
        bet = scratch([P, NT, NH])
        bet_e = scratch([P, NT, NH])
        dtp = scratch([P, NT, NH])
        g_t = scratch([P, NT, NH])
        m1 = scratch([P, NT])
        m2 = scratch([P, NT])
        e2 = scratch([P, NT])
        oh1 = scratch([P, NT, NE])
        oh2 = scratch([P, NT, NE])
        comb = scratch([P, NT, NE])
        cnt_b = scratch([P, NE])
        ends = scratch([P, NE])
        base = scratch([P, NE])
        zer = scratch([P, NE])
        blkf = scratch([P, NB])[0:1]
        both_h = scratch([P, NT, NE], bf16)
        assert used[0] <= NE * FC * DM
        arm = sd
        combT = xs_w

        x_in = sems("x_in", NBATCH)
        win_in, small_in, gam_in, w1_in, w2_in = (sem(n) for n in (
            "win_in", "small_in", "gam_in", "w1_in", "w2_in"))
        rows0_set, rows0_out, consts_set, pool_step, dve_step = (sem(n) for n in (
            "rows0_set", "rows0_out", "consts_set", "pool_step", "dve_step"))
        var_ready, rstd_ready, xn_ready, xnT_psum, xnT_ready, nar_psum, nar_ready = (sem(n) for n in (
            "var_ready", "rstd_ready", "xn_ready", "xnT_psum", "xnT_ready", "nar_psum", "nar_ready"))
        e_in, e_out, l_in, l_out = (sem(n) for n in ("e_in", "e_out", "l_in", "l_out"))
        adt_ready, L_psum, L_exp, bet_ready, betn_psum, turns_ready, theta_psum, theta_ready = (sem(n) for n in (
            "adt_ready", "L_psum", "L_exp", "bet_ready", "betn_psum", "turns_ready", "theta_psum", "theta_ready"))
        top_in, top_out, both_ready, pos_psum, pos_used, slots_ready = (sem(n) for n in (
            "top_in", "top_out", "both_ready", "pos_psum", "pos_used", "slots_ready"))
        row_meta, sent, comb_ready, combT_psum, combT_ready, beta_psum, acc_ready, betn_used = (sem(n) for n in (
            "row_meta", "sent", "comb_ready", "combT_psum", "combT_ready", "beta_psum", "acc_ready", "betn_used"))
        arm_ready, arm_psum, decay_ready, coefs_ready, scratch_free, blk_e_ready = (sem(n) for n in (
            "arm_ready", "arm_psum", "decay_ready", "coefs_ready", "scratch_free", "blk_e_ready"))
        names = ("xt_ready zx_psum bc_psum sq_done ms_ready rms_ready bn_ready kq0_ready ang_ready angk_ready"
                 " angr_ready trig_ready rot_dve rot_pool k_rot kT_psum qT_psum kT_ready qT_ready"
                 " score_psum sd_ready xg_ready xs_ready gate_ready inter_psum intra_psum state_psum state_dec"
                 " state_ready qkp_ready qk_ready qkh_ready coef_ready xc_ready y1_ready y2_ready y3_ready y_ready"
                 " yT_psum yT_ready out_psum acc_done")
        s = {n: sem(n) for n in names.split()}
        fnames = ("blkT_psum blkT_ready h1_psum h3_psum gl_ready hm_ready hT_psum hT_ready y_psum"
                  " st_ready mv_ready ve_ready rstd_ready rw_ready yc_ready res_ready")
        f = {n: [sem("f_" + n)] * SLOTS for n in fnames.split()}
        f["blk_in"], f["res_out"] = sems("f_blk_in", SLOTS), sems("f_res_out", SLOTS)
        res_in = sems("res_in", 4)
        fin_a, fin_ready, out_done = (sem(n) for n in ("fin_a", "fin_ready", "out_done"))

        block = ctx.enter_context(nc.Block())

        def bc(ap, n, k):
            v = ap.unsqueeze(k + 1)
            shape = list(v.shape)
            shape[k + 1] = n
            return v.to_broadcast(shape)

        def nth(j, i):
            return i + 2 if j == SLOTS - 1 else i + 1

        def cnt(j, i):
            return SLOTS * i + (j + 2)

        def prev(j, i):
            return (SLOTS - 1, i - 1) if j == 0 else (j - 1, i)

        def ahead(j, i):
            return (0, i + 1) if j == SLOTS - 1 else (j + 1, i)

        def again(eng, sem_, v):
            if not isinstance(v, int) or v > 0:
                eng.wait_ge(sem_, v)

        def joint(eng, pieces, slot_steps, first, last):
            def body(t, i, nslots):
                for j, steps in enumerate(pieces):
                    for step in steps:
                        step(t)
                    if j < nslots:
                        slot_steps(j, i, j == nslots - 1 and nslots < SLOTS)
            body(0, 0, 0)
            with eng.Fori(1, SOLO) as t:
                body(t, 0, 0)
            first()
            with eng.Fori(SOLO, NT - 1) as t:
                body(t, t - SOLO, SLOTS)
            body(NT - 1, JOINT - 1, LAST)
            last()

        def combT4(q):
            return (kq[0:NE, 0].rearrange("p h n -> p (h n)"), kq[0:NE, 1].rearrange("p h n -> p (h n)"),
                    kqT[0:NE, 0], kqT[0:NE, 1])[q]

        @block.sync
        def _(sp):
            x_v = A_u.rearrange("b (j p) d -> p (b j) d", p=P)
            for b in range(NBATCH):
                sp.dma_start(acc[:, b * TB:(b + 1) * TB, :], x_v[:, b * TB:(b + 1) * TB, :])\
                    .then_inc(x_in[b], 16)
            sp.dma_start(w_in[:, 0:WIDE + NARROW - NE], A_Win).then_inc(win_in, 16)
            sp.dma_start(w_in[:, WIDE + NARROW - NE:], A_Wr).then_inc(win_in, 16)
            sp.dma_start(w_out[:, :, :], A_Wout.rearrange("(c p) d -> p c d", p=P)).then_inc(small_in, 16)
            sp.dma_start(beta_e[:, :], A_beta).then_inc(small_in, 16)

            def spread(dst, src):
                sp.dma_start(dst, src.rearrange("(o n) -> o n", o=1).to_broadcast([P, src.shape[0]]))\
                    .then_inc(small_in, 16)
            spread(br[:, :], A_br)
            spread(dtb[:, :], A_dtb)
            spread(dskip[:, :], A_D)
            spread(bias_kq[:, 0, :, :].rearrange("p h n -> p (h n)"), A_Bb.rearrange("h n -> (h n)"))
            spread(bias_kq[:, 1, :, :].rearrange("p h n -> p (h n)"), A_Cb.rearrange("h n -> (h n)"))
            spread(nw_kq[:, 0, :], A_Bw)
            spread(nw_kq[:, 1, :], A_Cw)
            sp.wait_ge(rows0_set, 2)
            sp.dma_start(rows_dram.rearrange("(b p) c -> p b c", p=P), rows0).then_inc(rows0_out, 16)
            flat = A_gamma.rearrange("e d -> (e d)")
            sp.dma_start(gam[:, :, :].rearrange("p e d -> p (e d)"),
                         flat.rearrange("(o n) -> o n", o=1).to_broadcast([P, NE * DM])).then_inc(gam_in, 16)
            for q in range(4):
                e0, e1 = q * NE // 4, (q + 1) * NE // 4
                sp.dma_start(w1[:, e0:e1, :], A_W1[e0:e1].rearrange("e d f -> d e f")).then_inc(w1_in, 16)
                sp.dma_start(w3[:, e0:e1, :], A_W3[e0:e1].rearrange("e d f -> d e f")).then_inc(w1_in, 16)
            sp.wait_ge(scratch_free, 1)
            for q in range(4):
                e0, e1 = q * NE // 4, (q + 1) * NE // 4
                sp.dma_start(w2[:, e0:e1, :, :], A_W2[e0:e1].rearrange("e (c p) d -> p e c d", p=P))\
                    .then_inc(w2_in, 16)

            def load(j, b):
                sp.dma_start(blk[:, j, :], rows_dram[bass.ds(b * P, P), :]).then_inc(f["blk_in"][j], 16)

            sp.wait_ge(sent, 16 * TOPK * NT)
            load(SLOTS - 1, 0)
            for j in range(SLOTS - 1):
                load(j, 1 + j)
            def refill(j, i):
                sp.wait_ge(f["rw_ready"][j], cnt(j, i - 1))
                sp.wait_ge(f["res_out"][j], 16 * nth(j, i - 1))
                load(j, 1 + SLOTS * i + j)
            with sp.Fori(0, JOINT - 2) as i:
                refill(SLOTS - 1, i)
                for j in range(SLOTS - 1):
                    refill(j, i + 1)
            refill(SLOTS - 1, JOINT - 2)
            for j in range(min(LAST, SLOTS - 1)):
                refill(j, JOINT - 1)
            for q in range(4):
                n = NT // 4
                if q == 0:
                    for j in range(SLOTS):
                        sp.wait_ge(f["res_out"][j], 16 * (nth(j, JOINT - 1) - (0 if j < LAST else 1)))
                    sp.wait_ge(s["sd_ready"], NT)
                    sp.wait_ge(s["acc_done"], NT)
                for k in range(TOPK):
                    rv = res_dram[k * T:(k + 1) * T, :].rearrange("(t p) d -> p t d", p=P)
                    dst = decay[:, :, :].rearrange("p t c -> p (t c)")[:, k * T:(k + 1) * T]\
                        .rearrange("p (t d) -> p t d", d=DM)
                    sp.dma_start(dst[:, q * n:(q + 1) * n, :], rv[:, q * n:(q + 1) * n, :])\
                        .then_inc(res_in[q], 16)
            out_v = A_out.rearrange("b (j p) d -> p (b j) d", p=P)
            for q in range(4):
                n = NT // 4
                sp.wait_ge(fin_ready, q + 1)
                sp.dma_start(out_v[:, q * n:(q + 1) * n, :], acc[:, q * n:(q + 1) * n, :]).then_inc(out_done, 16)
            sp.wait_ge(out_done, 64)

        @block.gpsimd
        def _(pool):
            g = nc.gpsimd
            flat0 = decay[:, :, :].rearrange("p t c -> p (t c)")[:, 0:NB * ROW]
            g.memset(flat0, 0.0).then_inc(rows0_set, 1)
            for m, v in ((ident, 0.0), (ones, 1.0), (tri, 1.0), (low, 1.0), (shift, 0.0), (wrap, 0.0),
                         (mhalf, -0.5), (ident_h, 0.0), (ones_h, 1.0), (tri_h, 1.0)):
                g.memset(m[:, :], v).then_inc(pool_step, 1)
            g.memset(neg_h[:, :, :], 0.0).then_inc(pool_step, 1)
            g.iota(iota_e[:, :], [[1, NE]], base=0, channel_multiplier=0,
                   allow_small_or_imprecise_dtypes=True).then_inc(pool_step, 1)
            g.iota(iota_b[:, :], [[1, NB]], base=0, channel_multiplier=0,
                   allow_small_or_imprecise_dtypes=True).then_inc(pool_step, 1)
            pool.wait_ge(rows0_set, 1)
            g.iota(rows0[:, :, ROW - 1:ROW].bitcast(i32), [[P, NB], [1, 1]], base=TOPK * T,
                   channel_multiplier=1).then_inc(rows0_set, 1)
            pool.wait_ge(pool_step, 13)
            for m, cmp, fill, b0, cm, step in (
                    (ident, ALU.not_equal, 1.0, 0, 1, -1), (ident_h, ALU.not_equal, 1.0, 0, 1, -1),
                    (tri, ALU.is_ge, 0.0, 0, -1, 1), (tri_h, ALU.is_ge, 0.0, 0, -1, 1),
                    (low, ALU.is_gt, 0.0, 0, 1, -1), (shift, ALU.not_equal, 1.0, -1, 1, -1),
                    (wrap, ALU.not_equal, 1.0, P - 1, P, -1)):
                g.affine_select(out=m[:, :], in_=m[:, :], compare_op=cmp, fill=fill, base=b0,
                                pattern=[[step, P]], channel_multiplier=cm).then_inc(consts_set, 1)
            g.affine_select(out=neg_h[:, :, :], in_=neg_h[:, :, :], compare_op=ALU.is_ge, fill=NEG, base=0,
                            pattern=[[0, NH], [1, P]], channel_multiplier=-1).then_inc(consts_set, 1)
            pool.wait_ge(var_ready, 1)
            g.tensor_tensor(rx, vx, mhalf[:, :], ALU.pow).then_inc(rstd_ready, 1)
            g.iota(xrow[:, :, ROW - 1:ROW].bitcast(i32), [[P, NT], [1, 1]], base=0, channel_multiplier=1)\
                .then_inc(row_meta, 1)
            pool.wait_ge(row_meta, 2)
            pool.wait_ge(slots_ready, 1)
            pool.wait_ge(xn_ready, NT)
            pool.wait_ge(rows0_out, 16)
            for k in range(TOPK):
                if k:
                    pool.wait_ge(sent, 16 * NT)
                    g.iota(xrow[:, :, ROW - 1:ROW].bitcast(i32), [[P, NT], [1, 1]], base=k * T,
                           channel_multiplier=1).then_inc(row_meta, 1)
                    pool.wait_ge(row_meta, 4)
                for t in range(NT):
                    g.indirect_dma_start(out=rows_dram, in_=xrow[:, t, :], in_offset=None,
                                         out_offset=bass.IndirectOffsetOnAxis(ap=slots[:, k, t:t + 1], axis=0))\
                        .then_inc(sent, 16)

            def rms_pow(t):
                pool.wait_ge(s["ms_ready"], t + 1)
                again(pool, s["bn_ready"], t)
                g.tensor_tensor(rms[:, :], ms[:, :], mhalf[:, 0:2], ALU.pow).then_inc(s["rms_ready"], 1)

            def rot_sine(t):
                pool.wait_ge(s["kq0_ready"], t + 1)
                pool.wait_ge(s["trig_ready"], t + 1)
                again(pool, s["k_rot"], 2 * t)
                again(pool, s["qk_ready"], t)
                sn = bc(trig[:, 0, :, :], 2, 0)
                x1, x2 = kq[:, :, :, 0:NA], kq[:, :, :, NA:2 * NA]
                g.tensor_tensor(rot[:, 1], x2, sn, ALU.mult).then_inc(s["rot_pool"], 1)
                g.tensor_tensor(rot[:, 3], x1, sn, ALU.mult).then_inc(s["rot_pool"], 1)

            def qk_prod(t):
                pool.wait_ge(s["k_rot"], 2 * (t + 1))
                again(pool, s["qk_ready"], t)
                g.tensor_tensor(qkp[:, :, :], kq[:, 0], kq[:, 1], ALU.mult).then_inc(s["qkp_ready"], 1)

            def finish(j, i):
                pool.wait_ge(f["ve_ready"][j], cnt(j, i))
                pj, pi = prev(j, i)
                if isinstance(cnt(pj, pi), int) and cnt(pj, pi) < 1:
                    pass
                else:
                    pool.wait_ge(f["rw_ready"][pj], cnt(pj, pi))
                g.tensor_tensor(rstd[:, :], mv[:, 1:2], mhalf[:, 0:1], ALU.pow).then_inc(f["rstd_ready"][j], 1)

            def store(j, i):
                pool.wait_ge(f["blk_in"][j], 16)
                pool.wait_ge(f["res_ready"][j], cnt(j, i))
                g.indirect_dma_start(out=res_dram, in_=res[:, j, :], in_offset=None,
                                     out_offset=bass.IndirectOffsetOnAxis(
                                         ap=blk[:, j, ROW - 1:ROW].bitcast(i32), axis=0))\
                    .then_inc(f["res_out"][j], 16)

            def slot(j, i, last):
                finish(*prev(j, i))
                store(*prev(j, i))

            def ending():
                finish(LAST - 1, JOINT - 1)
                store(LAST - 1, JOINT - 1)
            joint(pool, [[], [rms_pow], [rot_sine, qk_prod], [], []], slot, lambda: None, ending)

        @block.tensor
        def _(pe):
            m = nc.tensor.matmul
            pe.wait_ge(consts_set, 8)
            for b in range(NBATCH):
                for j in range(TB):
                    t = b * TB + j
                    pe.wait_ge(xn_ready, t + 1)
                    nc.tensor.transpose(bank[b][:, j * P:(j + 1) * P], xrow[:, t, 0:DM], ident[:, :])\
                        .then_inc(xnT_psum, 1)
            pe.wait_ge(win_in, 32)
            per = NT // 2
            for t in range(NT):
                if t % TB == 0:
                    pe.wait_ge(xnT_ready, t // TB + 1)
                c = (t % per) * NARROW
                m(bank[4 + t // per][:, c:c + NARROW], xnT[:, t * P:(t + 1) * P], w_in[:, WIDE:],
                  start=True, stop=True).then_inc(nar_psum, 1)
            pe.wait_ge(both_ready, 1)
            m(bank[0][:, 0:NT * NE], tri_h[:, :], both_h.rearrange("p t e -> p (t e)"),
              start=True, stop=False)
            for d in range(1, NT):
                m(bank[0][:, d * NE:NT * NE], ones_h[:, :],
                  both_h[:, 0:NT - d, :].rearrange("p t e -> p (t e)"), start=False, stop=(d == NT - 1))
            for t in range(NT):
                last = m(bank[1][:, 0:NE], ones_h[:, :], both_h[:, t, :], start=(t == 0), stop=(t == NT - 1))
            last.then_inc(pos_psum, 1)
            pe.wait_ge(adt_ready, 1)
            a_v = adt.rearrange("p t h -> p (t h)")
            W = NT * NH
            m(bank[2][:, 0:W], tri, a_v, start=True, stop=True)
            m(bank[2][:, W:2 * W], low, a_v, start=True, stop=True)
            m(bank[2][:, 2 * W:3 * W], ones, a_v, start=True, stop=True).then_inc(L_psum, 1)
            pe.wait_ge(bet_ready, 1)
            b4 = bet.rearrange("p (b j) h -> p b j h", j=TB)
            o4 = bank[3][:, 0:W].rearrange("p (b j h) -> p b j h", j=TB, h=NH)
            m(bank[3][:, 0:W], shift[:, :], bet.rearrange("p t h -> p (t h)"), start=True, stop=False)
            m(o4[:, :, 0:TB - 1, :], wrap[:, :], b4[:, :, 1:TB, :], start=False, stop=True).then_inc(betn_psum, 1)
            pe.wait_ge(turns_ready, 1)
            pe.wait_ge(nar_ready, 2)
            for b in range(NBATCH):
                v = turns[:, b * TB:(b + 1) * TB, :].rearrange("p j c -> p (j c)")
                q = tpre[:, b].rearrange("p j c -> p (j c)")
                m(bank[4 + b][:, :], tri, v, start=True, stop=False)
                m(bank[4 + b][:, P:], ones, q, start=False, stop=True).then_inc(theta_psum, 1)
            pe.wait_ge(comb_ready, 1)
            pe.wait_ge(pos_used, 1)
            for t in range(NT):
                q, c = divmod(t, TB)
                if t and t % (2 * TB) == 0:
                    pe.wait_ge(combT_ready, t // TB)
                nc.tensor.transpose(bank[q % 2][0:NE, c * P:(c + 1) * P], comb[:, t, :], ident[:, :])\
                    .then_inc(combT_psum, 1)
            pe.wait_ge(small_in, 16 * 9)
            pe.wait_ge(L_exp, 1)
            pe.wait_ge(betn_used, 1)
            for t in range(NT):
                q, c = divmod(t, TB)
                if c == 0:
                    pe.wait_ge(combT_ready, q + 1)
                    if q >= 2:
                        pe.wait_ge(acc_ready, q - 1)
                cT = combT4(q)
                m(bank[2 + q % 2][:, c * DM:(c + 1) * DM], cT[:, c * P:(c + 1) * P], beta_e[:, :],
                  start=True, stop=True).then_inc(beta_psum, 1)
            pe.wait_ge(combT_ready, NBATCH)
            for t in range(NT):
                pe.wait_ge(arm_ready, t + 1)
                if t >= 2:
                    pe.wait_ge(decay_ready, t - 1)
                for h in range(NH):
                    m(bank[t % 2][:, h * P:(h + 1) * P], arm[:, h, :], tri, start=(h == 0), stop=False)
                m(bank[t % 2][:, :], ident_h[:, :], neg_h[:, :, :].rearrange("p h i -> p (h i)"),
                  start=False, stop=True).then_inc(arm_psum, 1)
            pe.wait_ge(theta_ready, NBATCH)
            pe.wait_ge(acc_ready, NBATCH)
            pe.wait_ge(decay_ready, NT)

            def project(t):
                pe.wait_ge(s["xt_ready"], t + 1)
                again(pe, s["acc_done"], t)
                again(pe, s["state_ready"], t)
                m(bank[1][:, 0:BC], xt_s[:, :], w_in[:, ZX:WIDE], start=True, stop=True).then_inc(s["bc_psum"], 1)
                m(bank[0][:, :], xt_s[:, :], w_in[:, 0:ZX], start=True, stop=True).then_inc(s["zx_psum"], 1)

            def turn_kq(t):
                pe.wait_ge(s["k_rot"], 2 * (t + 1))
                again(pe, s["y2_ready"], t)
                for h in range(NH):
                    last = nc.tensor.transpose(bank[2][:, h * P:(h + 1) * P], kq[:, 0, h, :], ident[:, :])
                last.then_inc(s["kT_psum"], 1)
                for h in range(NH):
                    last = nc.tensor.transpose(bank[3][:, h * P:(h + 1) * P], kq[:, 1, h, :], ident[:, :])
                last.then_inc(s["qT_psum"], 1)

            def scores(t):
                pe.wait_ge(s["kT_ready"], t + 1)
                pe.wait_ge(s["qT_ready"], t + 1)
                for h in range(NH):
                    last = m(bank[2][:, h * P:(h + 1) * P], kqT[:, 0, h * P:(h + 1) * P],
                             kqT[:, 1, h * P:(h + 1) * P], start=True, stop=True)
                last.then_inc(s["score_psum"], 1)
                for h in range(NH):
                    last = m(bank[3][:, DI + h * HD:DI + (h + 1) * HD], kqT[:, 1, h * P:(h + 1) * P],
                             state[:, h, :], start=True, stop=True)
                last.then_inc(s["inter_psum"], 1)
                pe.wait_ge(s["xs_ready"], t + 1)
                for h in range(NH):
                    last = m(bank[1][:, h * HD:(h + 1) * HD], kq[:, 0, h, :], xs_w[:, h, :], start=True, stop=True)
                last.then_inc(s["state_psum"], 1)

            def intra(t):
                pe.wait_ge(s["sd_ready"], t + 1)
                pe.wait_ge(s["xg_ready"], t + 1)
                pe.wait_ge(s["y1_ready"], t + 1)
                for h in range(NH):
                    last = m(bank[3][:, h * HD:(h + 1) * HD], sd[:, h, :], xg_w[:, h, :], start=True, stop=True)
                last.then_inc(s["intra_psum"], 1)

            def turn_y(t):
                pe.wait_ge(s["y_ready"], t + 1)
                for c in range(2):
                    last = nc.tensor.transpose(
                        bank[0][:, c * P:(c + 1) * P],
                        ysum[:, :, :].rearrange("p h d -> p (h d)")[:, c * P:(c + 1) * P], ident[:, :])
                last.then_inc(s["yT_psum"], 1)

            def project_out(t):
                pe.wait_ge(s["yT_ready"], t + 1)
                for c in range(2):
                    last = m(bank[0][:, DI:DI + DM], yT[:, c * P:(c + 1) * P], w_out[:, c, :],
                             start=(c == 0), stop=(c == 1))
                last.then_inc(s["out_psum"], 1)

            def turn_block(j, i):
                pe.wait_ge(f["blk_in"][j], 16 * nth(j, i))
                nc.tensor.transpose(bank[6][:, 0:P], blk[:, j, 0:DM], ident[:, :]).then_inc(f["blkT_psum"][j], 1)

            def expert_of(b):
                return pe.value_load(blk_e[0:1, bass.ds(b, 1)], min_val=0, max_val=NE - 1)

            def up(j, i, e, w, out, done, side):
                m(bank[out][:, :], blkT[:, side, :], w[:, bass.ds(e, 1), :].rearrange("p o f -> p (o f)"),
                  start=True, stop=True).then_inc(f[done][j], 1)

            def turn_h(j, i):
                pe.wait_ge(f["hm_ready"][j], cnt(j, i))
                for c in range(FC):
                    last = nc.tensor.transpose(bank[6][:, c * P:(c + 1) * P], hm[:, c * P:(c + 1) * P], ident[:, :])
                last.then_inc(f["hT_psum"][j], 1)

            def down(j, i, e):
                pe.wait_ge(f["hT_ready"][j], cnt(j, i))
                w = w2[:, bass.ds(e, 1), :, :].rearrange("p o c d -> p (o c) d")
                for c in range(FC):
                    last = m(bank[7][:, 0:DM], hT[:, c * P:(c + 1) * P], w[:, c, :],
                             start=(c == 0), stop=(c == FC - 1))
                last.then_inc(f["y_psum"][j], 1)

            def slot(j, i, last):
                b = 1 + SLOTS * i + j
                pj, pi = prev(j, i)
                side = (j + 1) % 2
                e, ep = expert_of(b), expert_of(b - 1)
                pe.wait_ge(f["blkT_ready"][j], cnt(j, i))
                pe.wait_ge(f["gl_ready"][pj], cnt(pj, pi))
                up(j, i, e, w1, 4, "h1_psum", side)
                turn_h(pj, pi)
                pe.wait_ge(f["hm_ready"][pj], cnt(pj, pi))
                up(j, i, e, w3, 5, "h3_psum", side)
                pe.wait_ge(f["yc_ready"][0], cnt(pj, pi))
                down(pj, pi, ep)
                if not last:
                    turn_block(*ahead(j, i))

            def first():
                pe.wait_ge(w1_in, 16 * 8)
                pe.wait_ge(w2_in, 16 * 4)
                pe.wait_ge(blk_e_ready, 1)
                turn_block(SLOTS - 1, -1)
                pe.wait_ge(f["blkT_ready"][SLOTS - 1], 1)
                e = expert_of(0)
                up(SLOTS - 1, -1, e, w1, 4, "h1_psum", 0)
                up(SLOTS - 1, -1, e, w3, 5, "h3_psum", 0)
                turn_block(0, 0)

            def ending():
                j, i = LAST - 1, JOINT - 1
                e = expert_of(NB - 1)
                turn_h(j, i)
                pe.wait_ge(f["yc_ready"][0], cnt(j, i))
                down(j, i, e)
            joint(pe, [[], [project], [], [turn_kq, scores], [intra, turn_y, project_out]], slot, first, ending)

        @block.scalar
        def _(act):
            a = nc.scalar.activation
            nc.scalar.preload_act_table_set("natural_log_exp_and_others")
            for b in range(NBATCH):
                act.wait_ge(xnT_psum, TB * (b + 1))
                a(xnT[:, b * SEQ:(b + 1) * SEQ], bank[b][:, :], ACT.Copy).then_inc(xnT_ready, 1)
            per = NT // 2
            for q in range(2):
                act.wait_ge(nar_psum, per * (q + 1))
                a(nar[:, q * per:(q + 1) * per, :].rearrange("p t c -> p (t c)"), bank[4 + q][:, 0:per * NARROW],
                  ACT.Copy).then_inc(nar_ready, 1)
            act.wait_ge(top_in, 1)
            a(e2, m2, ACT.Exp).then_inc(top_out, 1)
            act.wait_ge(e_in, 1)
            a(sp_e, sp_x, ACT.Exp, scale=-1.0).then_inc(e_out, 1)
            a(bet_e, nar[:, :, 2 * NH:3 * NH], ACT.Exp, scale=-1.0).then_inc(e_out, 1)
            act.wait_ge(l_in, 1)
            a(sp_l, sp_u, ACT.Ln).then_inc(l_out, 1)
            act.wait_ge(L_psum, 1)
            a(eL[:, :, :, :].rearrange("p a t h -> p (a t h)"), bank[2][:, 0:3 * NT * NH], ACT.Exp)\
                .then_inc(L_exp, 1)
            for b in range(NBATCH):
                act.wait_ge(theta_psum, b + 1)
                a(theta[:, b * TB:(b + 1) * TB, :].rearrange("p j c -> p (j c)"), bank[4 + b][:, :], ACT.Copy)\
                    .then_inc(theta_ready, 1)
            for q in range(NBATCH):
                act.wait_ge(combT_psum, TB * (q + 1))
                a(combT4(q), bank[q % 2][0:NE, :], ACT.Copy).then_inc(combT_ready, 1)
            act.wait_ge(rows0_out, 16)
            for t in range(NT):
                act.wait_ge(arm_psum, t + 1)
                a(decay[:, t, :], bank[t % 2][:, :], ACT.Exp).then_inc(decay_ready, 1)

            def squares(t):
                act.wait_ge(s["bc_psum"], t + 1)
                again(act, s["kT_ready"], t)
                for n in range(2):
                    a(kqT[:, n, 0:DS], bank[1][:, n * DS:(n + 1) * DS], ACT.Square,
                      accum_out=ms[:, n:n + 1]).then_inc(s["sq_done"], 1)

            def sines(t):
                act.wait_ge(s["angr_ready"], t + 1)
                again(act, s["k_rot"], 2 * t)
                a(trig[:, :, :, :].rearrange("p a h n -> p (a h n)"), ang[:, :, :].rearrange("p a c -> p (a c)"),
                  ACT.Sin, scale=TWO_PI).then_inc(s["trig_ready"], 1)

            def gates(t):
                act.wait_ge(s["zx_psum"], t + 1)
                again(act, s["y_ready"], t)
                a(gate[:, :], bank[0][:, 0:DI], ACT.Silu).then_inc(s["gate_ready"], 1)

            def out_kq(t):
                act.wait_ge(s["kT_psum"], t + 1)
                a(kqT[:, 0, :], bank[2][:, :], ACT.Copy).then_inc(s["kT_ready"], 1)
                act.wait_ge(s["qT_psum"], t + 1)
                a(kqT[:, 1, :], bank[3][:, :], ACT.Copy).then_inc(s["qT_ready"], 1)

            def out_y(t):
                act.wait_ge(s["yT_psum"], t + 1)
                a(yT[:, :], bank[0][:, 0:DI], ACT.Copy).then_inc(s["yT_ready"], 1)

            def out_block(j, i, side):
                act.wait_ge(f["blkT_psum"][j], cnt(j, i))
                a(blkT[:, side, :], bank[6][:, 0:P], ACT.Copy).then_inc(f["blkT_ready"][j], 1)

            def silu(j, i):
                act.wait_ge(f["h1_psum"][j], cnt(j, i))
                pj, pi = prev(j, i)
                if not isinstance(cnt(pj, pi), int) or cnt(pj, pi) > 0:
                    act.wait_ge(f["hm_ready"][pj], cnt(pj, pi))
                a(gl[:, :], bank[4][:, :], ACT.Silu).then_inc(f["gl_ready"][j], 1)

            def out_h(j, i):
                act.wait_ge(f["hT_psum"][j], cnt(j, i))
                a(hT[:, :], bank[6][:, :], ACT.Copy).then_inc(f["hT_ready"][j], 1)

            def scale_y(j, i):
                act.wait_ge(f["rw_ready"][j], cnt(j, i))
                act.wait_ge(f["yc_ready"][j], cnt(j, i) + 1)
                a(res[:, j, :], yc[:, :], ACT.Copy, scale=rw[:, 0:1]).then_inc(f["res_ready"][j], 1)

            def slot(j, i, last):
                out_h(*prev(j, i))
                silu(j, i)
                if not last:
                    jj, ii = ahead(j, i)
                    out_block(jj, ii, (jj + 1) % 2)
                scale_y(*prev(j, i))

            def first():
                out_block(SLOTS - 1, -1, 0)
                silu(SLOTS - 1, -1)
                out_block(0, 0, 1)

            def ending():
                out_h(LAST - 1, JOINT - 1)
                scale_y(LAST - 1, JOINT - 1)
            joint(act, [[], [squares, sines, gates], [], [out_kq], [out_y]], slot, first, ending)

        @block.vector
        def _(dve):
            v = nc.vector
            tt, ts, stt = v.tensor_tensor, v.tensor_scalar, v.scalar_tensor_tensor
            n = [0]

            def link(ins):
                n[0] += 1
                ins.then_inc(dve_step, 1)
                dve.wait_ge(dve_step, n[0])

            v.memset(state[:, :, :], 0.0)
            v.memset(zer, 0.0)
            for t in range(NT):
                if t % TB == 0:
                    dve.wait_ge(x_in[t // TB], 16)
                last = v.bn_stats(stats[:, t, :], acc[:, t, :])
            link(last)
            for t in range(NT):
                last = v.bn_aggr(mvx[:, t, :], stats[:, t, :])
            link(last)
            ts(vx, mvx[:, :, 1], EPS, None, ALU.add).then_inc(var_ready, 1)
            dve.wait_ge(rstd_ready, 1)
            for t in range(NT):
                ts(xrow[:, t, 0:DM], acc[:, t, :], mvx[:, t, 0:1], rx[:, t:t + 1], ALU.subtract, ALU.mult)\
                    .then_inc(xn_ready, 1)
            dve.wait_ge(small_in, 16 * 9)
            dve.wait_ge(nar_ready, 2)
            link(tt(lg, nar[:, :, NARROW - NE:], bc(br[:, :], NT, 0), ALU.add))
            link(v.tensor_reduce(m1, lg, X, ALU.max))

            def pick_top(src, mx, onehot):
                link(tt(rt, src, bc(mx, NE, 1), ALU.is_equal))
                link(stt(sc1, rt, -float(NE), bc(iota_e[:, :], NT, 0), ALU.mult, ALU.add))
                link(v.tensor_reduce(posb[:, 0, :], sc1, X, ALU.min))
                link(tt(onehot, sc1, bc(posb[:, 0, :], NE, 1), ALU.is_equal))
            pick_top(lg, m1, oh1)
            link(stt(lg, oh1, NEG, lg, ALU.mult, ALU.add))
            link(v.tensor_reduce(m2, lg, X, ALU.max))
            pick_top(lg, m2, oh2)
            tt(both_h, oh1, oh2, ALU.add).then_inc(both_ready, 1)
            tt(m2, m2, m1, ALU.subtract).then_inc(top_in, 1)
            sp4 = sp_t.rearrange("p a (t h) -> p a t h", h=NH)
            tt(sp4[:, 0], nar[:, :, 0:NH], bc(dtb[:, :], NT, 0), ALU.add)
            link(v.tensor_copy(sp4[:, 1], nar[:, :, NH:2 * NH]))
            stt(sp_x, sp_t, -1.0, sp_t, ALU.mult, ALU.max).then_inc(e_in, 1)
            dve.wait_ge(top_out, 1)
            link(ts(e2, e2, 1.0, None, ALU.add) if False else ts(m1, e2, 1.0, None, ALU.add))
            link(v.reciprocal(wtop[:, 0, :], m1))
            link(tt(wtop[:, 1, :], wtop[:, 0, :], e2, ALU.mult))
            dve.wait_ge(pos_psum, 1)
            link(ts(cnt_b, bank[1][:, 0:NE], 1.0 / P, (P - 1) / P - (P - 1) / (2.0 * P), ALU.mult, ALU.add))
            link(ts(cnt_b, cnt_b, MAGIC, -MAGIC, ALU.add, ALU.add))
            link(v.tensor_tensor_scan(ends, cnt_b, zer, 0.0, ALU.add, ALU.add))
            link(tt(base, ends, cnt_b, ALU.subtract))
            link(ts(base, base, float(P), -1.0, ALU.mult, ALU.add))
            link(tt(posb, bank[0][:, 0:NT * NE].rearrange("p (t e) -> p t e", e=NE), bc(base, NT, 0), ALU.add))
            for k, oh in enumerate((oh1, oh2)):
                link(tt(pick, oh, posb, ALU.mult))
                link(v.tensor_reduce(slots_f[:, k, :], pick, X, ALU.add))
            v.tensor_copy(slots[:, :, :], slots_f[:, :, :]).then_inc(slots_ready, 1)
            v.tensor_copy(xrow[:, :, DM:DM + 1].rearrange("p t o -> p (t o)"), wtop[:, 0, :]).then_inc(row_meta, 1)
            link(tt(cmpb, bc(ends[0:1, :], NB, 0), bc(iota_b[:, :], NE, 1), ALU.is_le))
            link(v.tensor_reduce(blkf, cmpb, X, ALU.add))
            ts(blk_e[:, :], blkf, float(NE - 1), None, ALU.min).then_inc(blk_e_ready, 1)
            link(tt(comb, oh1, bc(wtop[:, 0, :], NE, 1), ALU.mult))
            link(tt(pick, oh2, bc(wtop[:, 1, :], NE, 1), ALU.mult))
            tt(comb, comb, pick, ALU.add).then_inc(comb_ready, 1)
            dve.wait_ge(comb_ready, 1)
            v.memset(base[0:1, 0:1], 0.0).then_inc(pos_used, 1)
            dve.wait_ge(e_out, 2)
            link(ts(sp_u, sp_e, 1.0, None, ALU.add))
            ts(sp_x, sp_u, 1.0, None, ALU.subtract).then_inc(l_in, 1)
            dve.wait_ge(l_in, 1)
            link(tt(sp_e, sp_e, sp_x, ALU.subtract))
            link(v.reciprocal(sp_r, sp_u))
            link(tt(sp_e, sp_e, sp_r, ALU.mult))
            link(stt(sp_e, sp_t, 0.0, sp_e, ALU.max, ALU.add))
            link(ts(bet_e, bet_e, 1.0, None, ALU.add))
            v.reciprocal(bet, bet_e).then_inc(bet_ready, 1)
            dve.wait_ge(bet_ready, 1)
            dve.wait_ge(l_out, 1)
            link(tt(sp.rearrange("p a t h -> p a (t h)"), sp_l, sp_e, ALU.add))
            dt_v = sp[:, 0]
            link(ts(g_t, sp[:, 1], -1.0, -A_FLOOR, ALU.mult, ALU.min))
            tt(adt, g_t, dt_v, ALU.mult).then_inc(adt_ready, 1)
            link(ts(dtp, dt_v, INV_2PI, None, ALU.mult))
            for t in range(NT):
                last = tt(turns[:, t, :].rearrange("p (h n) -> p h n", n=NA),
                          bc(nar[:, t, 3 * NH:3 * NH + NA], NH, 0), bc(dtp[:, t, :], NA, 1), ALU.mult)
            link(last)
            u4 = turns.rearrange("p (b j) c -> p b j c", j=TB)
            link(v.tensor_copy(tpre[:, :, 0], u4[:, :, 0]))
            for j in range(1, TB - 1):
                last = tt(tpre[:, :, j], tpre[:, :, j - 1], u4[:, :, j], ALU.add)
                if j < TB - 2:
                    link(last)
            last.then_inc(turns_ready, 1)
            dve.wait_ge(betn_psum, 1)
            link(ts(g_t, bank[3][:, 0:NT * NH].rearrange("p (t h) -> p t h", h=NH), -1.0, 1.0, ALU.mult, ALU.add))
            link(tt(coefH[:, :, :], g_t, dt_v, ALU.mult))
            link(tt(g_t, bet, dt_v, ALU.mult))
            link(tt(coefG[:, :, :], g_t, coefH[:, :, :], ALU.add))
            dve.wait_ge(L_exp, 1)
            link(tt(wstate[:, :, :], coefG[:, :, :], eL[:, 1], ALU.mult))
            for z in (wstate[:, :, :], eL[:, 2]):
                for b in range(NBATCH):
                    last = v.memset(z[:, (b + 1) * TB - 1, :], 0.0)
            link(last)
            v.memset(base[0:1, 0:1], 0.0).then_inc(betn_used, 1)
            for q in range(NBATCH):
                dve.wait_ge(beta_psum, TB * (q + 1))
                a4 = acc[:, q * TB:(q + 1) * TB, :].rearrange("p t d -> p (t d)")
                tt(a4, a4, bank[2 + q % 2][:, :], ALU.add).then_inc(acc_ready, 1)
            for t in range(NT):
                if t:
                    dve.wait_ge(arm_psum, t)
                tt(arm[:, :, :], bc(low, NH, 0), bc(adt[:, t, :], P, 1), ALU.mult).then_inc(arm_ready, 1)
                if t == TB:
                    dve.wait_ge(sent, 16 * NT)
                    v.tensor_copy(xrow[:, :, DM:DM + 1].rearrange("p t o -> p (t o)"), wtop[:, 1, :])\
                        .then_inc(row_meta, 1)
            dve.wait_ge(row_meta, 3)
            dve.wait_ge(arm_psum, NT)
            dve.wait_ge(theta_ready, NBATCH)
            v.memset(zer[0:1, 0:1], 0.0).then_inc(scratch_free, 1)
            dve.wait_ge(scratch_free, 1)

            def token(t):
                again(dve, s["zx_psum"], t)
                ts(xt_s[:, :], xnT[:, bass.ds(t * P, P)], 1.0, None, ALU.mult).then_inc(s["xt_ready"], 1)
                again(dve, s["trig_ready"], t)
                th = theta[:, bass.ds(t, 1), :].rearrange("p o c -> p (o c)")
                ts(ang[:, 0, :], th, 0.0, None, ALU.add).then_inc(s["ang_ready"], 1)
                ts(ang[:, 1, :], th, 0.25, None, ALU.add).then_inc(s["ang_ready"], 1)
                dve.wait_ge(s["ang_ready"], 2 * (t + 1))
                ts(angk[:, :, :], ang[:, :, :], MAGIC, -MAGIC, ALU.add, ALU.add).then_inc(s["angk_ready"], 1)
                dve.wait_ge(s["angk_ready"], t + 1)
                tt(ang[:, :, :], ang[:, :, :], angk[:, :, :], ALU.subtract).then_inc(s["angr_ready"], 1)

            def norm_kq(t):
                dve.wait_ge(s["sq_done"], 2 * (t + 1))
                again(dve, s["rms_ready"], t)
                ts(ms[:, :], ms[:, :], 1.0 / DS, EPS, ALU.mult, ALU.add).then_inc(s["ms_ready"], 1)
                dve.wait_ge(s["rms_ready"], t + 1)
                for q in range(2):
                    last = stt(bn_kq[:, q, :], bank[1][:, q * DS:(q + 1) * DS], rms[:, q:q + 1], nw_kq[:, q, :],
                               ALU.mult, ALU.mult)
                last.then_inc(s["bn_ready"], 1)
                dve.wait_ge(s["bn_ready"], t + 1)
                again(dve, s["qkp_ready"], t)
                again(dve, s["state_psum"], t)
                for q in range(2):
                    last = tt(kq[:, q], bc(bn_kq[:, q, :], NH, 0), bias_kq[:, q], ALU.add)
                last.then_inc(s["kq0_ready"], 1)

            def at(tile, t, k=None):
                x = tile[:, bass.ds(t, 1), :] if k is None else tile[:, k, bass.ds(t, 1), :]
                return x.rearrange("p o h -> p (o h)")

            def weigh(t):
                dve.wait_ge(s["zx_psum"], t + 1)
                again(dve, s["intra_psum"], t)
                xv = bank[0][:, DI:2 * DI].rearrange("p (h d) -> p h d", d=HD)
                dve.wait_ge(s["gate_ready"], t + 1)
                tt(xg_w[:, :, :], xv, bc(at(coefG, t), HD, 1), ALU.mult).then_inc(s["xg_ready"], 1)
                again(dve, s["state_psum"], t)
                tt(xs_w[:, :, :], xv, bc(at(wstate, t), HD, 1), ALU.mult).then_inc(s["xs_ready"], 1)

            def rotate(t):
                dve.wait_ge(s["kq0_ready"], t + 1)
                dve.wait_ge(s["trig_ready"], t + 1)
                cs = bc(trig[:, 1, :, :], 2, 0)
                x1, x2 = kq[:, :, :, 0:NA], kq[:, :, :, NA:2 * NA]
                tt(rot[:, 0], x1, cs, ALU.mult).then_inc(s["rot_dve"], 1)
                tt(rot[:, 2], x2, cs, ALU.mult).then_inc(s["rot_dve"], 1)
                dve.wait_ge(s["rot_dve"], 2 * (t + 1))
                dve.wait_ge(s["rot_pool"], 2 * (t + 1))
                tt(x1, rot[:, 0], rot[:, 1], ALU.subtract).then_inc(s["k_rot"], 1)
                tt(x2, rot[:, 2], rot[:, 3], ALU.add).then_inc(s["k_rot"], 1)

            def mask(t):
                dve.wait_ge(s["score_psum"], t + 1)
                again(dve, s["intra_psum"], t)
                tt(sd[:, :, :].rearrange("p h i -> p (h i)"), bank[2][:, :],
                   decay[:, bass.ds(t, 1), :].rearrange("p o c -> p (o c)"), ALU.mult).then_inc(s["sd_ready"], 1)
                dve.wait_ge(s["inter_psum"], t + 1)
                tt(ysum[:, :, :], bank[3][:, DI:2 * DI].rearrange("p (h d) -> p h d", d=HD),
                   bc(at(eL, t, 0), HD, 1), ALU.mult).then_inc(s["y1_ready"], 1)

            def skip(t):
                dve.wait_ge(s["qkp_ready"], t + 1)
                v.tensor_reduce(qk[:, :], qkp[:, :, :], X, ALU.add).then_inc(s["qk_ready"], 1)
                dve.wait_ge(s["qk_ready"], t + 1)
                tt(qk[:, :], qk[:, :], at(coefH, t), ALU.mult).then_inc(s["qkh_ready"], 1)
                dve.wait_ge(s["qkh_ready"], t + 1)
                tt(coef[:, :], dskip[:, :], qk[:, :], ALU.subtract).then_inc(s["coef_ready"], 1)
                dve.wait_ge(s["coef_ready"], t + 1)
                tt(xc_w[:, :, :], bank[0][:, DI:2 * DI].rearrange("p (h d) -> p h d", d=HD),
                   bc(coef[:, :], HD, 1), ALU.mult).then_inc(s["xc_ready"], 1)

            def carry(t):
                dve.wait_ge(s["state_psum"], t + 1)
                tt(state[:, :, :], state[:, :, :], bc(at(eL, t, 2), HD, 1), ALU.mult).then_inc(s["state_dec"], 1)
                dve.wait_ge(s["state_dec"], t + 1)
                tt(state[:, :, :], state[:, :, :], bank[1][:, 0:DI].rearrange("p (h d) -> p h d", d=HD), ALU.add)\
                    .then_inc(s["state_ready"], 1)

            def join(t):
                dve.wait_ge(s["intra_psum"], t + 1)
                dve.wait_ge(s["y1_ready"], t + 1)
                tt(ysum[:, :, :], ysum[:, :, :], bank[3][:, 0:DI].rearrange("p (h d) -> p h d", d=HD), ALU.add)\
                    .then_inc(s["y2_ready"], 1)
                dve.wait_ge(s["y2_ready"], t + 1)
                dve.wait_ge(s["xc_ready"], t + 1)
                tt(ysum[:, :, :], ysum[:, :, :], xc_w[:, :, :], ALU.add).then_inc(s["y3_ready"], 1)
                dve.wait_ge(s["y3_ready"], t + 1)
                tt(ysum[:, :, :].rearrange("p h d -> p (h d)"), ysum[:, :, :].rearrange("p h d -> p (h d)"),
                   gate[:, :], ALU.mult).then_inc(s["y_ready"], 1)

            def add_out(t):
                dve.wait_ge(s["out_psum"], t + 1)
                o = acc[:, bass.ds(t, 1), :].rearrange("p o d -> p (o d)")
                tt(o, o, bank[0][:, DI:DI + DM], ALU.add).then_inc(s["acc_done"], 1)

            def product(j, i):
                dve.wait_ge(f["h3_psum"][j], cnt(j, i))
                dve.wait_ge(f["gl_ready"][j], cnt(j, i))
                pj, pi = prev(j, i)
                if not isinstance(cnt(pj, pi), int) or cnt(pj, pi) > 0:
                    dve.wait_ge(f["hT_psum"][pj], cnt(pj, pi))
                tt(hm[:, :], gl[:, :], bank[5][:, :], ALU.mult).then_inc(f["hm_ready"][j], 1)

            def norm_y(j, i, b):
                e = dve.value_load(blk_e[0:1, bass.ds(b, 1)], min_val=0, max_val=NE - 1)
                dve.wait_ge(f["y_psum"][j], cnt(j, i))
                v.bn_stats(st6[:, :], bank[7][:, 0:DM]).then_inc(f["st_ready"][j], 1)
                dve.wait_ge(gam_in, 16)
                dve.wait_ge(f["st_ready"][j], cnt(j, i))
                v.bn_aggr(mv[:, :], st6[:, :]).then_inc(f["mv_ready"][j], 1)
                dve.wait_ge(f["mv_ready"][j], cnt(j, i))
                ts(mv[:, 1:2], mv[:, 1:2], EPS, None, ALU.add).then_inc(f["ve_ready"][j], 1)
                pj, pi = prev(j, i)
                if not isinstance(cnt(pj, pi), int) or cnt(pj, pi) > 0:
                    dve.wait_ge(f["res_ready"][pj], cnt(pj, pi))
                stt(yc[:, :], bank[7][:, 0:DM], mv[:, 0:1], gam[:, bass.ds(e, 1), :].rearrange("p o d -> p (o d)"),
                    ALU.subtract, ALU.mult).then_inc(f["yc_ready"][j], 1)
                dve.wait_ge(f["rstd_ready"][j], cnt(j, i))
                tt(rw[:, :], rstd[:, :], blk[:, j, DM:DM + 1], ALU.mult).then_inc(f["rw_ready"][j], 1)

            def slot(j, i, last):
                product(j, i)
                norm_y(*prev(j, i), SLOTS * i + j)

            def first():
                dve.wait_ge(gam_in, 16)
                dve.wait_ge(blk_e_ready, 1)
                v.memset(yc[:, :], 0.0).then_inc(f["yc_ready"][0], 1)
                product(SLOTS - 1, -1)

            def ending():
                norm_y(LAST - 1, JOINT - 1, NB - 1)
            joint(dve, [[token], [norm_kq], [weigh, rotate], [mask, skip, carry], [join, add_out]], slot, first, ending)

            q4 = NT // 4
            flat = acc[:, :, :].rearrange("p t d -> p (t d)")
            d = decay[:, :, :].rearrange("p t c -> p (t c)")
            dve.wait_ge(s["acc_done"], NT)
            for q in range(4):
                dve.wait_ge(res_in[q], 16 * TOPK)
                c = q * q4 * DM
                w = q4 * DM
                tt(flat[:, c:c + w], flat[:, c:c + w], d[:, c:c + w], ALU.add).then_inc(fin_a, 1)
                dve.wait_ge(fin_a, q + 1)
                tt(flat[:, c:c + w], flat[:, c:c + w], d[:, T + c:T + c + w], ALU.add).then_inc(fin_ready, 1)


_INS = ['L0_attn_u', 'L0_attn_W_in', 'L0_attn_W_out', 'L0_attn_dt_bias', 'L0_attn_B_bias', 'L0_attn_C_bias',
        'L0_attn_B_norm_w', 'L0_attn_C_norm_w', 'L0_attn_D', 'L0_ffn_Wr', 'L0_ffn_br', 'L0_ffn_W1', 'L0_ffn_W3',
        'L0_ffn_W2', 'L0_ffn_gamma', 'L0_ffn_beta']


def kernel(**inputs):
    import numpy as _np
    import concourse.bacc as _bacc
    from concourse import mybir as _mybir
    from concourse.bass_utils import run_bass_kernel_spmd as _run

    nc = _bacc.Bacc("TRN2", target_bir_lowering=False, num_devices=1)
    arrays, args = {}, []
    for name in _INS:
        a = _np.ascontiguousarray(inputs[name])
        arrays[f"in_{name}_dram"] = a
        args.append(nc.dram_tensor(f"in_{name}_dram", a.shape, _mybir.dt.from_np(a.dtype), kind="ExternalInput").ap())
    u = inputs['L0_attn_u']
    out = nc.dram_tensor("out_0_dram", tuple(u.shape), _mybir.dt.float32, kind="ExternalOutput").ap()
    build(nc, *args, out)
    r = _run(nc, [arrays], core_ids=[0])
    return r.results[0]["out_0_dram"]
```

```python
import concourse.bass as bass
from concourse import mybir
from contextlib import ExitStack


def build(nc, A_u, A_Win, A_Wout, A_dtb, A_Bb, A_Cb, A_Bw, A_Cw, A_D, A_Wr, A_br, A_W1, A_W3, A_W2,
          A_gamma, A_beta, A_out):
    fp32, bf16, i32 = mybir.dt.float32, mybir.dt.bfloat16, mybir.dt.int32
    ALU = mybir.AluOpType
    ACT = mybir.ActivationFunctionType
    X = mybir.AxisListType.X

    P = 128
    NBATCH, SEQ, DM = A_u.shape
    NT = NBATCH * SEQ // P
    TB = SEQ // P
    T = NT * P
    NH, DS = A_Bb.shape
    DI = A_Wout.shape[0]
    HD = DI // NH
    NA = (A_Win.shape[1] - 2 * DI - 2 * DS - 3 * NH)
    NE, _, F = A_W1.shape
    FC = F // P
    TOPK = 2
    ZX, BC = 2 * DI, 2 * DS
    NARROW = 3 * NH + NA + NE
    WIDE = ZX + BC
    NB = (TOPK * T - NE) // P + NE
    LOADED = NB + 2
    NROWS = LOADED * P
    ROW = DM + 2
    HALF = 3
    SLOTS = 2 * HALF
    PAIRS = (NT - 2) // 2
    BEFORE = 2 + HALF
    assert NT % 2 == 0 and NA == 32
    assert BEFORE + SLOTS * PAIRS == NB
    EPS = 1e-5
    A_FLOOR = 1e-4
    MAGIC = 1.5 * 2.0 ** 23
    INV_2PI = 0.15915494309189535
    TWO_PI = 6.2831845
    HALF_PI = 1.5707963267948966
    TINY = 1e-37
    NEG = -1e30

    rows_dram = nc.dram_tensor("rows_dram", [NROWS, ROW], fp32, kind="Internal").ap()
    res_dram = nc.dram_tensor("res_dram", [TOPK * T + NROWS, DM], fp32, kind="Internal").ap()

    ctx = ExitStack()
    with ctx:
        def sb(name, shape, dt=fp32):
            return ctx.enter_context(nc.sbuf_tensor(name, shape, dt))

        def sem(name):
            return ctx.enter_context(nc.semaphore(name))

        def sems(name, n):
            return [sem(f"{name}{j}") for j in range(n)]

        bank = [ctx.enter_context(nc.psum_tensor(f"bank{i}", [P, 512], fp32)) for i in range(8)]

        w1 = sb("w1", [P, NE, F])
        w3 = sb("w3", [P, NE, F])
        w2 = sb("w2", [P, NE, FC, DM])
        w_in = sb("w_in", [P, WIDE + NARROW])
        w_out = sb("w_out", [P, 2, DM])
        gam = sb("gam", [P, NE, DM])
        bias_kq = sb("bias_kq", [P, 2, NH, DS])
        nw_kq = sb("nw_kq", [P, 2, DS])
        br = sb("br", [P, NE])
        dtb = sb("dtb", [P, NH])
        dskip = sb("dskip", [P, NH])
        ident = sb("ident", [P, P])
        iota_e = sb("iota_e", [P, NE])
        iota_b = sb("iota_b", [1, NB])
        mhalf = sb("mhalf", [P, NT])
        half_pi = sb("half_pi", [P, 1])

        acc = sb("acc", [P, NT, DM])
        xnT = sb("xnT", [P, T])
        xrow = sb("xrow", [P, NT, ROW])
        theta = sb("theta", [P, NT, NH * NA])
        decay = sb("decay", [P, NT, NH * P])
        rows0 = decay[:, :, :].rearrange("p t c -> p (t c)")[:, 0:LOADED * ROW]\
            .rearrange("p (b c) -> p b c", c=ROW)
        eL = sb("eL", [P, 3, NT, NH])
        own = sb("own", [P, NT, NH])
        lnw = sb("lnw", [P, NT, NH])
        wstate = sb("wstate", [P, NT, NH])
        slots_f = sb("slots_f", [P, TOPK, NT])
        slots = sb("slots", [P, TOPK, NT], i32)
        wtop = sb("wtop", [P, TOPK, NT])
        blk_e = sb("blk_e", [1, NB], i32)

        xt_s = sb("xt_s", [P, P])
        ms = sb("ms", [P, 2])
        rms = sb("rms", [P, 2])
        kq = sb("kq", [P, 2, NH, DS])
        ang = sb("ang", [P, NH * NA])
        trig = sb("trig", [P, 2, NH, NA])
        rot = sb("rot", [P, 4, 2, NH, NA])
        flat_rot = rot[:, :, :, :, :].rearrange("p r q h n -> p (r q h n)")
        kqT = sb("kqT", [P, 2, NH * P])
        sd = sb("sd", [P, NH, P])
        bn_kq = sd[:, 0:2, :]
        x_w = sb("x_w", [P, NH, HD])
        xs_w = sb("xs_w", [P, NH, HD])
        xd_w = sb("xd_w", [P, NH, HD])
        gate = sb("gate", [P, DI])
        ysum = sb("ysum", [P, NH, HD])
        yT = sb("yT", [P, DI])
        state = sb("state", [P, NH, HD])

        blk = sb("blk", [P, SLOTS, ROW])
        blkT = sb("blkT", [P, 2, P])
        rows_end = xrow[:, :, :].rearrange("p t c -> p (t c)")
        gl, hm, hT = (rows_end[:, n * F:(n + 1) * F] for n in range(3))
        res = rows_end[:, 3 * F:3 * F + HALF * DM].rearrange("p (j d) -> p j d", d=DM)
        st6 = sb("st6", [P, 6])
        mv = sb("mv", [P, 2])
        rstd = sb("rstd", [P, 1])
        rw = sb("rw", [P, 1])
        yc = rows_end[:, 3 * F + HALF * DM:3 * F + (HALF + 1) * DM]

        flat_sd = sd[:, :, :].rearrange("p h i -> p (h i)")
        tri = flat_sd[:, 0:P]
        adt = flat_sd[:, P:P + NT * NH].rearrange("p (t h) -> p t h", h=NH)
        ident_h = flat_sd[:, P + NT * NH:2 * P].bitcast(bf16)
        neg_h = flat_sd[:, 2 * P:4 * P].bitcast(bf16).rearrange("p (h i) -> p h i", i=P)
        assert NT * NH == P // 2

        used = [0]

        def scratch(shape, dt=fp32):
            n = 1
            for s in shape[1:]:
                n *= s
            flat = w2[:, :, :, :].rearrange("p a b c -> p (a b c)")
            words = n if dt != bf16 else (n + 1) // 2
            v = flat[:, used[0]:used[0] + words]
            used[0] += words
            if dt != fp32:
                v = v.bitcast(dt)
            if len(shape) == 3:
                v = v.rearrange("p (a b) -> p a b", b=shape[2])
            if len(shape) == 4:
                v = v.rearrange("p (a b c) -> p a b c", b=shape[2], c=shape[3])
            return v

        low = scratch([P, P])
        ones = scratch([P, P])
        shift = scratch([P, P])
        wrap = scratch([P, P])
        tri_h = scratch([P, P], bf16)
        ones_h = scratch([P, P], bf16)
        stats = scratch([P, NT, 6])
        mvx = scratch([P, NT, 2])
        vx = scratch([P, NT])
        rx = scratch([P, NT])
        nar = scratch([P, NT, NARROW])
        turns = scratch([P, NT, NH * NA])
        tpre = scratch([P, NBATCH, TB - 1, NH * NA])
        lg, rt, sc1, posb, pick = (
            tpre.rearrange("p b j c -> p (b j c)")[:, n * NT * NE:(n + 1) * NT * NE]
            .rearrange("p (t e) -> p t e", e=NE) for n in range(5))
        cmpb = turns.rearrange("p t c -> p (t c)")[0:1, 0:NB * NE].rearrange("p (b e) -> p b e", e=NE)
        beta_e = flat_rot[0:NE, TB * NH * NA:TB * NH * NA + DM]
        lnG = scratch([P, NT, NH])
        coefG = scratch([P, NT, NH])
        sp_x = scratch([P, 2, NT * NH])
        sp_e = scratch([P, 2, NT * NH])
        sp_u = scratch([P, 2, NT * NH])
        sp_l = scratch([P, 2, NT * NH])
        sp_r = scratch([P, 2, NT * NH])
        sp_t = scratch([P, 2, NT * NH])
        sp = scratch([P, 2, NT, NH])
        bet = scratch([P, NT, NH])
        bet_e = scratch([P, NT, NH])
        dtp = scratch([P, NT, NH])
        g_t = scratch([P, NT, NH])
        m1 = scratch([P, NT])
        m2 = scratch([P, NT])
        e2 = scratch([P, NT])
        oh1 = scratch([P, NT, NE])
        oh2 = scratch([P, NT, NE])
        comb = scratch([P, NT, NE])
        cnt_b = scratch([P, NE])
        ends = scratch([P, NE])
        base = scratch([P, NE])
        zer = scratch([P, NE])
        blkf = scratch([P, NB])[0:1]
        both_h = scratch([P, NT, NE], bf16)
        assert used[0] <= NE * FC * DM
        combT = xs_w

        x_in = sems("x_in", NBATCH)
        win_in, small_in, gam_in, w1_in, w2_in = (sem(n) for n in (
            "win_in", "small_in", "gam_in", "w1_in", "w2_in"))
        rows0_set, rows0_out, consts_set, pool_step, dve_step = (sem(n) for n in (
            "rows0_set", "rows0_out", "consts_set", "pool_step", "dve_step"))
        var_ready, rstd_ready, xn_ready, xnT_psum, xnT_ready, nar_psum, nar_ready = (sem(n) for n in (
            "var_ready", "rstd_ready", "xn_ready", "xnT_psum", "xnT_ready", "nar_psum", "nar_ready"))
        e_in, e_out, l_in, l_out = (sem(n) for n in ("e_in", "e_out", "l_in", "l_out"))
        adt_ready, L_psum, L_exp, bet_ready, betn_psum, turns_ready, theta_psum, theta_ready = (sem(n) for n in (
            "adt_ready", "L_psum", "L_exp", "bet_ready", "betn_psum", "turns_ready", "theta_psum", "theta_ready"))
        top_in, top_out, both_ready, pos_psum, pos_used, slots_ready = (sem(n) for n in (
            "top_in", "top_out", "both_ready", "pos_psum", "pos_used", "slots_ready"))
        row_meta, sent, comb_ready, combT_psum, combT_ready, beta_psum, acc_ready, turns_cut = (sem(n) for n in (
            "row_meta", "sent", "comb_ready", "combT_psum", "combT_ready", "beta_psum", "acc_ready", "turns_cut"))
        g_ready, lng_ready, lnw_ready, arm_psum, decay_ready, decay_done, scratch_free, blk_e_ready = (
            sem(n) for n in ("g_ready", "lng_ready", "lnw_ready", "arm_psum", "decay_ready", "decay_done",
                             "scratch_free", "blk_e_ready"))
        names = ("xt_ready zx_psum bc_psum sq_done ms_ready rms_ready bn_ready k0_ready q0_ready ang_ready"
                 " trig_ready rot_dve rot_pool k_rot kT_psum qT_psum kT_ready qT_ready"
                 " score_psum sd_ready x_ready xd_ready xs_ready gate_ready inter_psum intra_psum state_psum"
                 " state_dec state_ready y1_ready y2_ready y3_ready y_ready yT_psum yT_ready out_psum acc_done")
        s = {n: sem(n) for n in names.split()}
        fnames = ("blkT_psum blkT_ready h1_psum h3_psum gl_ready hm_ready hT_psum hT_ready y_psum"
                  " st_ready mv_ready ve_ready rstd_ready rw_ready yc_ready res_ready")
        f = {n: sem("f_" + n) for n in fnames.split()}
        blk_in, res_out = sems("f_blk_in", SLOTS), sems("f_res_out", SLOTS)
        res_in = sems("res_in", 4)
        fin_a, fin_ready, out_done = (sem(n) for n in ("fin_a", "fin_ready", "out_done"))

        block = ctx.enter_context(nc.Block())

        def bc(ap, n, k):
            v = ap.unsqueeze(k + 1)
            shape = list(v.shape)
            shape[k + 1] = n
            return v.to_broadcast(shape)

        def num(blk_):
            j, i = blk_
            return SLOTS * i + (j + BEFORE)

        def cnt(blk_):
            j, i = blk_
            return SLOTS * i + (j + BEFORE + 1)

        def nth(blk_):
            j, i = blk_
            return i + 2 if j >= SLOTS - BEFORE else i + 1

        def shift_by(blk_, n):
            j, i = blk_
            return ((j + n) % SLOTS, i + (j + n) // SLOTS)

        def exists(blk_):
            n = num(blk_)
            return not isinstance(n, int) or 0 <= n < NB

        def loaded(blk_):
            n = num(blk_)
            return not isinstance(n, int) or 0 <= n < LOADED

        def again(eng, sem_, v):
            if not isinstance(v, int) or v > 0:
                eng.wait_ge(sem_, v)

        def weave(eng, iteration):
            iteration(0, [None] + [(SLOTS - BEFORE + j, -1) for j in range(BEFORE - HALF)])
            iteration(1, [(SLOTS - HALF + j, -1) for j in range(HALF)])
            with eng.Fori(0, PAIRS) as i:
                iteration(2 * i + 2, [(j, i) for j in range(HALF)])
                iteration(2 * i + 3, [(HALF + j, i) for j in range(HALF)])
            iteration(NT, [(j, PAIRS) for j in range(HALF)])

        def parts(t, blocks):
            first = not (isinstance(t, int) and t == NT)
            second = not (isinstance(t, int) and t == 0)
            return first, second, blocks + [None] * (HALF - len(blocks))

        def combT4(q):
            return (kq[0:NE, 0].rearrange("p h n -> p (h n)"), kq[0:NE, 1].rearrange("p h n -> p (h n)"),
                    kqT[0:NE, 0], kqT[0:NE, 1])[q]

        @block.sync
        def _(sp):
            x_v = A_u.rearrange("b (j p) d -> p (b j) d", p=P)
            for b in range(NBATCH):
                sp.dma_start(acc[:, b * TB:(b + 1) * TB, :], x_v[:, b * TB:(b + 1) * TB, :])\
                    .then_inc(x_in[b], 16)
            sp.dma_start(w_in[:, 0:WIDE + NARROW - NE], A_Win).then_inc(win_in, 16)
            sp.dma_start(w_in[:, WIDE + NARROW - NE:], A_Wr).then_inc(win_in, 16)
            sp.dma_start(w_out[:, :, :], A_Wout.rearrange("(c p) d -> p c d", p=P)).then_inc(small_in, 16)
            sp.dma_start(beta_e[:, :], A_beta).then_inc(small_in, 16)

            def spread(dst, src):
                sp.dma_start(dst, src.rearrange("(o n) -> o n", o=1).to_broadcast([P, src.shape[0]]))\
                    .then_inc(small_in, 16)
            spread(br[:, :], A_br)
            spread(dtb[:, :], A_dtb)
            spread(dskip[:, :], A_D)
            spread(bias_kq[:, 0, :, :].rearrange("p h n -> p (h n)"), A_Bb.rearrange("h n -> (h n)"))
            spread(bias_kq[:, 1, :, :].rearrange("p h n -> p (h n)"), A_Cb.rearrange("h n -> (h n)"))
            spread(nw_kq[:, 0, :], A_Bw)
            spread(nw_kq[:, 1, :], A_Cw)
            def load_up(q):
                e0, e1 = q * NE // 4, (q + 1) * NE // 4
                sp.dma_start(w1[:, e0:e1, :], A_W1[e0:e1].rearrange("e d f -> d e f")).then_inc(w1_in, 16)
                sp.dma_start(w3[:, e0:e1, :], A_W3[e0:e1].rearrange("e d f -> d e f")).then_inc(w1_in, 16)
            load_up(0)
            sp.wait_ge(rows0_set, 2)
            sp.dma_start(rows_dram.rearrange("(b p) c -> p b c", p=P), rows0).then_inc(rows0_out, 16)
            for q in range(1, 4):
                load_up(q)
            flat = A_gamma.rearrange("e d -> (e d)")
            sp.dma_start(gam[:, :, :].rearrange("p e d -> p (e d)"),
                         flat.rearrange("(o n) -> o n", o=1).to_broadcast([P, NE * DM])).then_inc(gam_in, 16)
            sp.wait_ge(scratch_free, 1)
            for q in range(4):
                e0, e1 = q * NE // 4, (q + 1) * NE // 4
                sp.dma_start(w2[:, e0:e1, :, :], A_W2[e0:e1].rearrange("e (c p) d -> p e c d", p=P))\
                    .then_inc(w2_in, 16)

            def load(blk_):
                b = num(blk_)
                sp.dma_start(blk[:, blk_[0], :], rows_dram[bass.ds(b * P, P), :]).then_inc(blk_in[blk_[0]], 16)

            sp.wait_ge(sent, 16 * TOPK * NT)
            for b in range(SLOTS):
                load(shift_by((SLOTS - BEFORE, -1), b))

            def refill(blk_):
                if loaded(blk_):
                    old = (blk_[0], blk_[1] - 1)
                    sp.wait_ge(res_out[old[0]], 16 * nth(old))
                    load(blk_)
            rounds = LOADED // SLOTS - 1
            with sp.Fori(0, rounds) as i:
                for j in range(SLOTS):
                    refill(shift_by((SLOTS - BEFORE, i), j))
            for j in range(LOADED % SLOTS):
                refill(shift_by((SLOTS - BEFORE, rounds), j))
            for q in range(4):
                n = NT // 4
                if q == 0:
                    for b in range(NB - SLOTS, NB):
                        last_of = shift_by((SLOTS - BEFORE, -1), b)
                        sp.wait_ge(res_out[last_of[0]], 16 * nth(last_of))
                    sp.wait_ge(s["sd_ready"], NT)
                    sp.wait_ge(s["acc_done"], NT)
                for k in range(TOPK):
                    rv = res_dram[k * T:(k + 1) * T, :].rearrange("(t p) d -> p t d", p=P)
                    dst = decay[:, :, :].rearrange("p t c -> p (t c)")[:, k * T:(k + 1) * T]\
                        .rearrange("p (t d) -> p t d", d=DM)
                    sp.dma_start(dst[:, q * n:(q + 1) * n, :], rv[:, q * n:(q + 1) * n, :])\
                        .then_inc(res_in[q], 16)
            out_v = A_out.rearrange("b (j p) d -> p (b j) d", p=P)
            for q in range(4):
                n = NT // 4
                sp.wait_ge(fin_ready, q + 1)
                sp.dma_start(out_v[:, q * n:(q + 1) * n, :], acc[:, q * n:(q + 1) * n, :]).then_inc(out_done, 16)
            sp.wait_ge(out_done, 64)

        @block.gpsimd
        def _(pool):
            g = nc.gpsimd
            flat0 = decay[:, :, :].rearrange("p t c -> p (t c)")[:, 0:LOADED * ROW]
            for m, v in ((ident, 0.0), (ones, 1.0), (tri, 1.0), (low, 1.0), (shift, 0.0), (wrap, 0.0),
                         (mhalf, -0.5), (ident_h, 0.0), (ones_h, 1.0), (tri_h, 1.0), (half_pi, HALF_PI)):
                g.memset(m[:, :], v).then_inc(pool_step, 1)
            g.memset(neg_h[:, :, :], 0.0).then_inc(pool_step, 1)
            g.iota(iota_e[:, :], [[1, NE]], base=0, channel_multiplier=0,
                   allow_small_or_imprecise_dtypes=True).then_inc(pool_step, 1)
            g.iota(iota_b[:, :], [[1, NB]], base=0, channel_multiplier=0,
                   allow_small_or_imprecise_dtypes=True).then_inc(pool_step, 1)
            pool.wait_ge(pool_step, 14)
            for m, cmp, fill, b0, cm, step in (
                    (ident, ALU.not_equal, 1.0, 0, 1, -1), (ident_h, ALU.not_equal, 1.0, 0, 1, -1),
                    (tri, ALU.is_ge, 0.0, 0, -1, 1), (tri_h, ALU.is_ge, 0.0, 0, -1, 1),
                    (low, ALU.is_gt, 0.0, 0, 1, -1), (shift, ALU.not_equal, 1.0, -1, 1, -1),
                    (wrap, ALU.not_equal, 1.0, P - 1, P, -1)):
                g.affine_select(out=m[:, :], in_=m[:, :], compare_op=cmp, fill=fill, base=b0,
                                pattern=[[step, P]], channel_multiplier=cm).then_inc(consts_set, 1)
            g.affine_select(out=neg_h[:, :, :], in_=neg_h[:, :, :], compare_op=ALU.is_gt, fill=NEG, base=0,
                            pattern=[[0, NH], [1, P]], channel_multiplier=-1).then_inc(consts_set, 1)
            pool.wait_ge(var_ready, 1)
            g.tensor_tensor(rx, vx, mhalf[:, :], ALU.pow).then_inc(rstd_ready, 1)
            g.memset(flat0, 0.0).then_inc(rows0_set, 1)
            pool.wait_ge(rows0_set, 1)
            g.iota(rows0[:, :, ROW - 1:ROW].bitcast(i32), [[P, LOADED], [1, 1]], base=TOPK * T,
                   channel_multiplier=1).then_inc(rows0_set, 1)
            g.iota(xrow[:, :, ROW - 1:ROW].bitcast(i32), [[P, NT], [1, 1]], base=0, channel_multiplier=1)\
                .then_inc(row_meta, 1)
            pool.wait_ge(row_meta, 2)
            pool.wait_ge(slots_ready, 1)
            pool.wait_ge(xn_ready, NT)
            pool.wait_ge(rows0_out, 16)
            for k in range(TOPK):
                if k:
                    pool.wait_ge(sent, 16 * NT)
                    g.tensor_copy(xrow[:, :, DM:DM + 1].rearrange("p t o -> p (t o)"), wtop[:, 1, :])\
                        .then_inc(row_meta, 1)
                    g.iota(xrow[:, :, ROW - 1:ROW].bitcast(i32), [[P, NT], [1, 1]], base=k * T,
                           channel_multiplier=1).then_inc(row_meta, 1)
                    pool.wait_ge(row_meta, 4)
                    pool.wait_ge(slots_ready, 2)
                for t in range(NT):
                    g.indirect_dma_start(out=rows_dram, in_=xrow[:, t, :], in_offset=None,
                                         out_offset=bass.IndirectOffsetOnAxis(ap=slots[:, k, t:t + 1], axis=0))\
                        .then_inc(sent, 16)

            def skip_x(u):
                pool.wait_ge(s["x_ready"], u + 1)
                again(pool, s["y3_ready"], u)
                g.tensor_tensor(xd_w[:, :, :], x_w[:, :, :], bc(dskip[:, :], HD, 1), ALU.mult)\
                    .then_inc(s["xd_ready"], 1)

            def rms_pow(t):
                pool.wait_ge(s["ms_ready"], t + 1)
                again(pool, s["bn_ready"], t)
                g.tensor_tensor(rms[:, :], ms[:, :], mhalf[:, 0:2], ALU.pow).then_inc(s["rms_ready"], 1)

            def bias_k(t):
                pool.wait_ge(s["bn_ready"], t + 1)
                again(pool, s["state_psum"], t)
                g.tensor_tensor(kq[:, 0], bc(bn_kq[:, 0, :], NH, 0), bias_kq[:, 0], ALU.add)\
                    .then_inc(s["k0_ready"], 1)

            def rot_sine(t):
                pool.wait_ge(s["k0_ready"], t + 1)
                pool.wait_ge(s["q0_ready"], t + 1)
                pool.wait_ge(s["trig_ready"], t + 1)
                again(pool, s["k_rot"], 2 * t)
                sn = bc(trig[:, 0, :, :], 2, 0)
                x1, x2 = kq[:, :, :, 0:NA], kq[:, :, :, NA:2 * NA]
                g.tensor_tensor(rot[:, 1], x2, sn, ALU.mult).then_inc(s["rot_pool"], 1)
                g.tensor_tensor(rot[:, 3], x1, sn, ALU.mult).then_inc(s["rot_pool"], 1)

            def finish(b):
                if not exists(b):
                    return
                pool.wait_ge(blk_in[b[0]], 16)
                pool.wait_ge(f["ve_ready"], cnt(b))
                again(pool, f["rw_ready"], num(b))
                g.tensor_tensor(rstd[:, :], mv[:, 1:2], mhalf[:, 0:1], ALU.pow).then_inc(f["rstd_ready"], 1)
                pool.wait_ge(f["rstd_ready"], cnt(b))
                again(pool, f["res_ready"], num(b))
                g.tensor_tensor(rw[:, :], rstd[:, :], blk[:, b[0], DM:DM + 1], ALU.mult).then_inc(f["rw_ready"], 1)

            def store(b):
                if not exists(b):
                    return
                pool.wait_ge(blk_in[b[0]], 16)
                pool.wait_ge(f["res_ready"], cnt(b))
                g.indirect_dma_start(out=res_dram, in_=res[:, b[0] % HALF, :], in_offset=None,
                                     out_offset=bass.IndirectOffsetOnAxis(
                                         ap=blk[:, b[0], ROW - 1:ROW].bitcast(i32), axis=0))\
                    .then_inc(res_out[b[0]], 16)

            def iteration(t, blocks):
                first, second, (b0, b1, b2) = parts(t, blocks)
                if second:
                    skip_x(t - 1)
                if b0:
                    finish(shift_by(b0, -2))
                if first:
                    rms_pow(t)
                    bias_k(t)
                if b0:
                    store(shift_by(b0, -2))
                if first:
                    rot_sine(t)
                if b1:
                    finish(shift_by(b1, -2))
                if b1:
                    store(shift_by(b1, -2))
                if b2:
                    finish(shift_by(b2, -2))
                    store(shift_by(b2, -2))
            weave(pool, iteration)

        @block.tensor
        def _(pe):
            m = nc.tensor.matmul
            pe.wait_ge(consts_set, 8)
            per = NT // 2
            for b in range(NBATCH + 1):
                if b < NBATCH:
                    for j in range(TB):
                        t = b * TB + j
                        pe.wait_ge(xn_ready, t + 1)
                        nc.tensor.transpose(bank[b][:, j * P:(j + 1) * P], xrow[:, t, 0:DM], ident[:, :])\
                            .then_inc(xnT_psum, 1)
                if b:
                    pe.wait_ge(win_in, 32)
                    pe.wait_ge(xnT_ready, b)
                    for t in range((b - 1) * TB, b * TB):
                        c = (t % per) * NARROW
                        m(bank[4 + t // per][:, c:c + NARROW], xnT[:, t * P:(t + 1) * P], w_in[:, WIDE:],
                          start=True, stop=True).then_inc(nar_psum, 1)
            pe.wait_ge(both_ready, 1)
            m(bank[0][:, 0:NT * NE], tri_h[:, :], both_h.rearrange("p t e -> p (t e)"),
              start=True, stop=False)
            for d in range(1, NT):
                m(bank[0][:, d * NE:NT * NE], ones_h[:, :],
                  both_h[:, 0:NT - d, :].rearrange("p t e -> p (t e)"), start=False, stop=(d == NT - 1))
            for t in range(NT):
                last = m(bank[1][:, 0:NE], ones_h[:, :], both_h[:, t, :], start=(t == 0), stop=(t == NT - 1))
            last.then_inc(pos_psum, 1)
            pe.wait_ge(comb_ready, 1)
            pe.wait_ge(pos_used, 1)
            pe.wait_ge(nar_ready, 2)
            pe.wait_ge(small_in, 16 * 9)
            for q in range(NBATCH):
                if q >= 2:
                    pe.wait_ge(combT_ready, q - 1)
                for c in range(TB):
                    nc.tensor.transpose(bank[q % 2][0:NE, c * P:(c + 1) * P], comb[:, q * TB + c, :], ident[:, :])\
                        .then_inc(combT_psum, 1)
            pe.wait_ge(adt_ready, 1)
            a_v = adt.rearrange("p t h -> p (t h)")
            W = NT * NH
            m(bank[2][:, 0:W], tri, a_v, start=True, stop=True)
            m(bank[2][:, W:2 * W], low, a_v, start=True, stop=True)
            m(bank[2][:, 2 * W:3 * W], ones, a_v, start=True, stop=True).then_inc(L_psum, 1)
            pe.wait_ge(bet_ready, 1)
            b4 = bet.rearrange("p (b j) h -> p b j h", j=TB)
            o4 = bank[3][:, 0:W].rearrange("p (b j h) -> p b j h", j=TB, h=NH)
            m(bank[3][:, 0:W], shift[:, :], bet.rearrange("p t h -> p (t h)"), start=True, stop=False)
            m(o4[:, :, 0:TB - 1, :], wrap[:, :], b4[:, :, 1:TB, :], start=False, stop=True).then_inc(betn_psum, 1)
            def sum_turns(b):
                pe.wait_ge(turns_ready, 1)
                if b >= 2:
                    pe.wait_ge(theta_ready, b - 1)
                v = turns[:, b * TB:(b + 1) * TB, :].rearrange("p j c -> p (j c)")
                q = tpre[:, b].rearrange("p j c -> p (j c)")
                m(bank[b % 2][:, :], tri, v, start=True, stop=False)
                m(bank[b % 2][:, P:], ones, q, start=False, stop=True).then_inc(theta_psum, 1)

            def sum_decays(t):
                out = bank[4 + t % 4]
                if t >= 4:
                    pe.wait_ge(decay_ready, NH * (t - 3))
                for h in range(NH):
                    m(out[:, h * P:(h + 1) * P], adt[:, t, h:h + 1].to_broadcast([P, P]), tri,
                      start=(h == 0), stop=False)
                m(out[:, :], ident_h[:, :], neg_h[:, :, :].rearrange("p h i -> p (h i)"),
                  start=False, stop=True).then_inc(arm_psum, 1)

            def sum_betas(q):
                pe.wait_ge(combT_ready, q + 1)
                if q >= 2:
                    pe.wait_ge(acc_ready, q - 1)
                for c in range(TB):
                    m(bank[2 + q % 2][:, c * DM:(c + 1) * DM], combT4(q)[:, c * P:(c + 1) * P], beta_e[:, :],
                      start=True, stop=True).then_inc(beta_psum, 1)
            for t in range(NT):
                sum_decays(t)
                if t < NBATCH:
                    sum_turns(t)
                else:
                    if t == NBATCH:
                        pe.wait_ge(lnw_ready, 1)
                    if t < 2 * NBATCH:
                        sum_betas(t - NBATCH)
            pe.wait_ge(theta_ready, NBATCH)
            pe.wait_ge(acc_ready, NBATCH)
            pe.wait_ge(decay_ready, NH * NT)

            def project(t):
                pe.wait_ge(s["xt_ready"], t + 1)
                again(pe, s["yT_ready"], t - 1)
                again(pe, s["state_ready"], t - 1)
                m(bank[1][:, 0:BC], xt_s[:, :], w_in[:, ZX:WIDE], start=True, stop=True).then_inc(s["bc_psum"], 1)
                again(pe, s["x_ready"], t)
                again(pe, s["xs_ready"], t)
                m(bank[0][:, :], xt_s[:, :], w_in[:, 0:ZX], start=True, stop=True).then_inc(s["zx_psum"], 1)

            def turn_kq(t):
                pe.wait_ge(s["k_rot"], 2 * (t + 1))
                again(pe, s["sd_ready"], t)
                for h in range(NH):
                    last = nc.tensor.transpose(bank[2][:, h * P:(h + 1) * P], kq[:, 0, h, :], ident[:, :])
                last.then_inc(s["kT_psum"], 1)
                again(pe, s["y2_ready"], t)
                for h in range(NH):
                    last = nc.tensor.transpose(bank[3][:, h * P:(h + 1) * P], kq[:, 1, h, :], ident[:, :])
                last.then_inc(s["qT_psum"], 1)

            def state_product(t):
                pe.wait_ge(s["xs_ready"], t + 1)
                again(pe, s["state_ready"], t)
                again(pe, s["yT_ready"], t)
                for h in range(NH):
                    last = m(bank[1][:, DI + h * HD:DI + (h + 1) * HD], kq[:, 0, h, :], xs_w[:, h, :],
                             start=True, stop=True)
                last.then_inc(s["state_psum"], 1)

            def scores(u):
                pe.wait_ge(s["kT_ready"], u + 1)
                pe.wait_ge(s["qT_ready"], u + 1)
                for h in range(NH):
                    last = m(bank[2][:, h * P:(h + 1) * P], kqT[:, 0, h * P:(h + 1) * P],
                             kqT[:, 1, h * P:(h + 1) * P], start=True, stop=True)
                last.then_inc(s["score_psum"], 1)

            def inter(u):
                again(pe, s["state_ready"], u)
                again(pe, s["acc_done"], u)
                for h in range(NH):
                    last = m(bank[3][:, DI + h * HD:DI + (h + 1) * HD], kqT[:, 1, h * P:(h + 1) * P],
                             state[:, h, :], start=True, stop=True)
                last.then_inc(s["inter_psum"], 1)

            def intra(u):
                pe.wait_ge(s["sd_ready"], u + 1)
                pe.wait_ge(s["x_ready"], u + 1)
                for h in range(NH):
                    last = m(bank[3][:, h * HD:(h + 1) * HD], sd[:, h, :], x_w[:, h, :], start=True, stop=True)
                last.then_inc(s["intra_psum"], 1)

            def turn_y(u):
                pe.wait_ge(s["y_ready"], u + 1)
                if not isinstance(u, int) or u + 1 < NT:
                    pe.wait_ge(s["state_ready"], u + 1)
                for c in range(2):
                    last = nc.tensor.transpose(
                        bank[1][:, c * P:(c + 1) * P],
                        ysum[:, :, :].rearrange("p h d -> p (h d)")[:, c * P:(c + 1) * P], ident[:, :])
                last.then_inc(s["yT_psum"], 1)

            def project_out(u):
                pe.wait_ge(s["yT_ready"], u + 1)
                if not isinstance(u, int) or u + 1 < NT:
                    pe.wait_ge(s["qT_ready"], u + 2)
                for c in range(2):
                    last = m(bank[3][:, 0:DM], yT[:, c * P:(c + 1) * P], w_out[:, c, :],
                             start=(c == 0), stop=(c == 1))
                last.then_inc(s["out_psum"], 1)

            def turn_block(b):
                if loaded(b):
                    pe.wait_ge(blk_in[b[0]], 16 * nth(b))
                    again(pe, f["blkT_ready"], num(b))
                    nc.tensor.transpose(bank[6][:, 0:P], blk[:, b[0], 0:DM], ident[:, :])\
                        .then_inc(f["blkT_psum"], 1)

            def expert_of(b):
                return pe.value_load(blk_e[0:1, bass.ds(num(b), 1)], min_val=0, max_val=NE - 1)

            def up(b, e, w, out, done):
                m(bank[out][:, :], blkT[:, b[0] % 2, :], w[:, bass.ds(e, 1), :].rearrange("p o f -> p (o f)"),
                  start=True, stop=True).then_inc(f[done], 1)

            def turn_h(b):
                pe.wait_ge(f["hm_ready"], cnt(b))
                two = shift_by(b, 2)
                if loaded(two):
                    pe.wait_ge(f["blkT_ready"], cnt(two))
                for c in range(FC):
                    last = nc.tensor.transpose(bank[6][:, c * P:(c + 1) * P], hm[:, c * P:(c + 1) * P], ident[:, :])
                last.then_inc(f["hT_psum"], 1)

            def rise(b, e):
                before = shift_by(b, -1)
                if exists(b):
                    pe.wait_ge(f["blkT_ready"], cnt(b))
                    again(pe, f["gl_ready"], num(b))
                    up(b, e, w1, 4, "h1_psum")
                if exists(before):
                    turn_h(before)
                if exists(b):
                    again(pe, f["hm_ready"], num(b))
                    up(b, e, w3, 5, "h3_psum")

            def down(b, e):
                if not exists(b):
                    return
                pe.wait_ge(f["hT_ready"], cnt(b))
                again(pe, f["yc_ready"], num(b))
                w = w2[:, bass.ds(e, 1), :, :].rearrange("p o c d -> p (o c) d")
                for c in range(FC):
                    last = m(bank[7][:, 0:DM], hT[:, c * P:(c + 1) * P], w[:, c, :],
                             start=(c == 0), stop=(c == FC - 1))
                last.then_inc(f["y_psum"], 1)

            def begin(b):
                turn_block(b)
                turn_block(shift_by(b, 1))
                pe.wait_ge(blk_e_ready, 1)
                pe.wait_ge(w1_in, 16 * 8)
                pe.wait_ge(w2_in, 16 * 4)

            def iteration(t, blocks):
                first, second, (b0, b1, b2) = parts(t, blocks)
                e0 = expert_of(b0) if b0 and exists(b0) else None
                if first:
                    project(t)
                if b0:
                    rise(b0, e0)
                if second:
                    scores(t - 1)
                if b0:
                    before = shift_by(b0, -1)
                    down(before, expert_of(before))
                    turn_block(shift_by(b0, 2))
                if isinstance(t, int) and t == 0:
                    begin(b1)
                e1 = expert_of(b1) if b1 and exists(b1) else None
                if second:
                    inter(t - 1)
                if b1:
                    rise(b1, e1)
                if second:
                    intra(t - 1)
                e2 = expert_of(b2) if b2 and exists(b2) else None
                if b1:
                    down(shift_by(b1, -1), e0)
                    turn_block(shift_by(b1, 2))
                if first:
                    turn_kq(t)
                if b2:
                    rise(b2, e2)
                if second:
                    turn_y(t - 1)
                if b2:
                    down(shift_by(b2, -1), e1)
                    turn_block(shift_by(b2, 2))
                if first:
                    state_product(t)
                if second:
                    project_out(t - 1)
            weave(pe, iteration)

        @block.scalar
        def _(act):
            a = nc.scalar.activation
            nc.scalar.preload_act_table_set("natural_log_exp_and_others")
            for b in range(NBATCH):
                act.wait_ge(xnT_psum, TB * (b + 1))
                a(xnT[:, b * SEQ:(b + 1) * SEQ], bank[b][:, :], ACT.Copy).then_inc(xnT_ready, 1)
            per = NT // 2
            for q in range(2):
                act.wait_ge(nar_psum, per * (q + 1))
                a(nar[:, q * per:(q + 1) * per, :].rearrange("p t c -> p (t c)"), bank[4 + q][:, 0:per * NARROW],
                  ACT.Copy).then_inc(nar_ready, 1)
            act.wait_ge(top_in, 1)
            a(e2, m2, ACT.Exp).then_inc(top_out, 1)
            act.wait_ge(e_in, 1)
            a(sp_e, sp_x, ACT.Exp, scale=-1.0).then_inc(e_out, 1)
            a(bet_e, nar[:, :, 2 * NH:3 * NH], ACT.Exp, scale=-1.0).then_inc(e_out, 1)
            for q in range(NBATCH):
                act.wait_ge(combT_psum, TB * (q + 1))
                a(combT4(q), bank[q % 2][0:NE, :], ACT.Copy).then_inc(combT_ready, 1)
            act.wait_ge(l_in, 1)
            a(sp_l, sp_u, ACT.Ln).then_inc(l_out, 1)
            act.wait_ge(L_psum, 1)
            a(eL[:, :, :, :].rearrange("p a t h -> p (a t h)"), bank[2][:, 0:3 * NT * NH], ACT.Exp)\
                .then_inc(L_exp, 1)
            act.wait_ge(g_ready, 1)
            a(lnG, g_t, ACT.Ln).then_inc(lng_ready, 1)
            act.wait_ge(rows0_out, 16)
            act.wait_ge(lnw_ready, 1)
            for t in range(NT):
                act.wait_ge(arm_psum, t + 1)
                for h in range(NH):
                    a(decay[:, t, h * P:(h + 1) * P], bank[4 + t % 4][:, h * P:(h + 1) * P], ACT.Exp,
                      bias=lnw[:, t, h:h + 1]).then_inc(decay_ready, 1)

            def sines(t):
                act.wait_ge(consts_set, 8)
                act.wait_ge(s["ang_ready"], t + 1)
                again(act, s["k_rot"], 2 * t)
                again(act, s["rot_pool"], 2 * t)
                a(trig[:, 0, :, :].rearrange("p h n -> p (h n)"), theta[:, bass.ds(t, 1), :].rearrange("p o c -> p (o c)"),
                  ACT.Sin, scale=TWO_PI)
                a(trig[:, 1, :, :].rearrange("p h n -> p (h n)"), ang[:, :], ACT.Sin, scale=-TWO_PI,
                  bias=half_pi[:, 0:1]).then_inc(s["trig_ready"], 1)

            def squares(t):
                act.wait_ge(s["bc_psum"], t + 1)
                again(act, s["k_rot"], 2 * t)
                for n in range(2):
                    a(flat_rot[:, n * DS:(n + 1) * DS], bank[1][:, n * DS:(n + 1) * DS], ACT.Square,
                      accum_out=ms[:, n:n + 1]).then_inc(s["sq_done"], 1)

            def out_kq(t):
                act.wait_ge(s["kT_psum"], t + 1)
                a(kqT[:, 0, :], bank[2][:, :], ACT.Copy).then_inc(s["kT_ready"], 1)
                act.wait_ge(s["qT_psum"], t + 1)
                a(kqT[:, 1, :], bank[3][:, :], ACT.Copy).then_inc(s["qT_ready"], 1)

            def gates(t):
                act.wait_ge(s["zx_psum"], t + 1)
                act.wait_ge(s["xs_ready"], t + 1)
                again(act, s["y_ready"], t)
                a(gate[:, :], bank[0][:, 0:DI], ACT.Silu).then_inc(s["gate_ready"], 1)
                again(act, s["intra_psum"], t)
                again(act, s["xd_ready"], t)
                a(x_w[:, :, :].rearrange("p h d -> p (h d)"), bank[0][:, DI:2 * DI], ACT.Copy)\
                    .then_inc(s["x_ready"], 1)

            def out_y(u):
                act.wait_ge(s["yT_psum"], u + 1)
                again(act, s["out_psum"], u)
                a(yT[:, :], bank[1][:, 0:DI], ACT.Copy).then_inc(s["yT_ready"], 1)

            def out_block(b):
                if loaded(b):
                    act.wait_ge(f["blkT_psum"], cnt(b))
                    a(blkT[:, b[0] % 2, :], bank[6][:, 0:P], ACT.Copy).then_inc(f["blkT_ready"], 1)

            def silu(b):
                if exists(b):
                    act.wait_ge(f["h1_psum"], cnt(b))
                    again(act, f["hm_ready"], num(b))
                    a(gl[:, :], bank[4][:, :], ACT.Silu).then_inc(f["gl_ready"], 1)

            def out_h(b):
                if exists(b):
                    act.wait_ge(f["hT_psum"], cnt(b))
                    again(act, f["y_psum"], num(b))
                    a(hT[:, :], bank[6][:, :], ACT.Copy).then_inc(f["hT_ready"], 1)

            def scale_y(b):
                if exists(b):
                    old = shift_by(b, -HALF)
                    act.wait_ge(f["rw_ready"], cnt(b))
                    act.wait_ge(f["yc_ready"], cnt(b))
                    if exists(old):
                        act.wait_ge(res_out[old[0]], 16 * nth(old))
                    a(res[:, b[0] % HALF, :], yc[:, :], ACT.Copy, scale=rw[:, 0:1]).then_inc(f["res_ready"], 1)

            def iteration(t, blocks):
                first, second, (b0, b1, b2) = parts(t, blocks)
                if first:
                    sines(t)
                    squares(t)
                if isinstance(t, int) and t == 0:
                    out_block(b1)
                for b in (b0, b1):
                    if b:
                        out_block(shift_by(b, 1))
                        silu(b)
                        out_h(shift_by(b, -1))
                        scale_y(shift_by(b, -2))
                if b2:
                    out_block(shift_by(b2, 1))
                if first:
                    out_kq(t)
                if b2:
                    silu(b2)
                    out_h(shift_by(b2, -1))
                if second:
                    out_y(t - 1)
                if first:
                    gates(t)
                if b2:
                    scale_y(shift_by(b2, -2))
            weave(act, iteration)

        @block.vector
        def _(dve):
            v = nc.vector
            tt, ts, stt = v.tensor_tensor, v.tensor_scalar, v.scalar_tensor_tensor
            n = [0]

            def link(ins):
                n[0] += 1
                ins.then_inc(dve_step, 1)
                dve.wait_ge(dve_step, n[0])

            v.memset(state[:, :, :], 0.0)
            v.memset(zer, 0.0)
            for t in range(NT):
                if t % TB == 0:
                    dve.wait_ge(x_in[t // TB], 16)
                last = v.bn_stats(stats[:, t, :], acc[:, t, :])
            link(last)
            for t in range(NT):
                last = v.bn_aggr(mvx[:, t, :], stats[:, t, :])
            link(last)
            ts(vx, mvx[:, :, 1], EPS, None, ALU.add).then_inc(var_ready, 1)
            dve.wait_ge(rstd_ready, 1)
            for t in range(NT):
                ts(xrow[:, t, 0:DM], acc[:, t, :], mvx[:, t, 0:1], rx[:, t:t + 1], ALU.subtract, ALU.mult)\
                    .then_inc(xn_ready, 1)
            dve.wait_ge(small_in, 16 * 9)
            dve.wait_ge(nar_ready, 2)
            link(tt(lg, nar[:, :, NARROW - NE:], bc(br[:, :], NT, 0), ALU.add))
            link(v.tensor_reduce(m1, lg, X, ALU.max))

            def pick_top(src, mx, onehot):
                link(tt(rt, src, bc(mx, NE, 1), ALU.is_equal))
                link(stt(sc1, rt, -float(NE), bc(iota_e[:, :], NT, 0), ALU.mult, ALU.add))
                link(v.tensor_reduce(posb[:, 0, :], sc1, X, ALU.min))
                link(tt(onehot, sc1, bc(posb[:, 0, :], NE, 1), ALU.is_equal))
            pick_top(lg, m1, oh1)
            link(stt(lg, oh1, NEG, lg, ALU.mult, ALU.add))
            link(v.tensor_reduce(m2, lg, X, ALU.max))
            pick_top(lg, m2, oh2)
            tt(both_h, oh1, oh2, ALU.add).then_inc(both_ready, 1)
            tt(m2, m2, m1, ALU.subtract).then_inc(top_in, 1)
            sp4 = sp_t.rearrange("p a (t h) -> p a t h", h=NH)
            tt(sp4[:, 0], nar[:, :, 0:NH], bc(dtb[:, :], NT, 0), ALU.add)
            link(v.tensor_copy(sp4[:, 1], nar[:, :, NH:2 * NH]))
            stt(sp_x, sp_t, -1.0, sp_t, ALU.mult, ALU.max).then_inc(e_in, 1)
            dve.wait_ge(top_out, 1)
            link(ts(m1, e2, 1.0, None, ALU.add))
            link(v.reciprocal(wtop[:, 0, :], m1))
            link(tt(wtop[:, 1, :], wtop[:, 0, :], e2, ALU.mult))
            v.tensor_copy(xrow[:, :, DM:DM + 1].rearrange("p t o -> p (t o)"), wtop[:, 0, :]).then_inc(row_meta, 1)
            dve.wait_ge(pos_psum, 1)
            link(ts(cnt_b, bank[1][:, 0:NE], 1.0 / P, (P - 1) / P - (P - 1) / (2.0 * P), ALU.mult, ALU.add))
            link(ts(cnt_b, cnt_b, MAGIC, -MAGIC, ALU.add, ALU.add))
            link(v.tensor_tensor_scan(ends, cnt_b, zer, 0.0, ALU.add, ALU.add))
            link(tt(base, ends, cnt_b, ALU.subtract))
            link(ts(base, base, float(P), -1.0, ALU.mult, ALU.add))
            link(tt(posb, bank[0][:, 0:NT * NE].rearrange("p (t e) -> p t e", e=NE), bc(base, NT, 0), ALU.add))
            for k, oh in enumerate((oh1, oh2)):
                link(tt(pick, oh, posb, ALU.mult))
                link(v.tensor_reduce(slots_f[:, k, :], pick, X, ALU.add))
                v.tensor_copy(slots[:, k, :], slots_f[:, k, :]).then_inc(slots_ready, 1)
            link(tt(cmpb, bc(ends[0:1, :], NB, 0), bc(iota_b[:, :], NE, 1), ALU.is_le))
            link(v.tensor_reduce(blkf, cmpb, X, ALU.add))
            ts(blk_e[:, :], blkf, float(NE - 1), None, ALU.min).then_inc(blk_e_ready, 1)
            link(tt(comb, oh1, bc(wtop[:, 0, :], NE, 1), ALU.mult))
            link(tt(pick, oh2, bc(wtop[:, 1, :], NE, 1), ALU.mult))
            tt(comb, comb, pick, ALU.add).then_inc(comb_ready, 1)
            dve.wait_ge(comb_ready, 1)
            v.memset(base[0:1, 0:1], 0.0).then_inc(pos_used, 1)
            dve.wait_ge(e_out, 2)
            link(ts(sp_u, sp_e, 1.0, None, ALU.add))
            ts(sp_x, sp_u, 1.0, None, ALU.subtract).then_inc(l_in, 1)
            dve.wait_ge(l_in, 1)
            link(tt(sp_e, sp_e, sp_x, ALU.subtract))
            link(v.reciprocal(sp_r, sp_u))
            link(tt(sp_e, sp_e, sp_r, ALU.mult))
            link(stt(sp_e, sp_t, 0.0, sp_e, ALU.max, ALU.add))
            link(ts(bet_e, bet_e, 1.0, None, ALU.add))
            v.reciprocal(bet, bet_e).then_inc(bet_ready, 1)
            dve.wait_ge(bet_ready, 1)
            dve.wait_ge(l_out, 1)
            link(tt(sp.rearrange("p a t h -> p a (t h)"), sp_l, sp_e, ALU.add))
            dt_v = sp[:, 0]
            link(ts(g_t, sp[:, 1], -1.0, -A_FLOOR, ALU.mult, ALU.min))
            tt(adt, g_t, dt_v, ALU.mult).then_inc(adt_ready, 1)
            link(ts(dtp, dt_v, INV_2PI, None, ALU.mult))
            for t in range(NT):
                last = tt(turns[:, t, :].rearrange("p (h n) -> p h n", n=NA),
                          bc(nar[:, t, 3 * NH:3 * NH + NA], NH, 0), bc(dtp[:, t, :], NA, 1), ALU.mult)
            link(last)
            u4 = turns.rearrange("p (b j) c -> p b j c", j=TB)
            link(v.tensor_copy(tpre[:, :, 0], u4[:, :, 0]))
            for j in range(1, TB - 1):
                last = tt(tpre[:, :, j], tpre[:, :, j - 1], u4[:, :, j], ALU.add)
                if j < TB - 2:
                    link(last)
            last.then_inc(turns_ready, 1)
            dve.wait_ge(betn_psum, 1)
            link(ts(g_t, bank[3][:, 0:NT * NH].rearrange("p (t h) -> p t h", h=NH), -1.0, 1.0, ALU.mult, ALU.add))
            link(tt(g_t, g_t, dt_v, ALU.mult))
            link(tt(own[:, :, :], bet, dt_v, ALU.mult))
            link(tt(coefG, own[:, :, :], g_t, ALU.add))
            ts(g_t, coefG, TINY, None, ALU.max).then_inc(g_ready, 1)
            dve.wait_ge(L_exp, 1)
            link(tt(wstate[:, :, :], coefG, eL[:, 1], ALU.mult))
            for z in (wstate[:, :, :], eL[:, 2]):
                for b in range(NBATCH):
                    last = v.memset(z[:, (b + 1) * TB - 1, :], 0.0)
            link(last)
            dve.wait_ge(lng_ready, 1)
            tt(lnw[:, :, :], lnG, bank[2][:, 0:NT * NH].rearrange("p (t h) -> p t h", h=NH), ALU.subtract)\
                .then_inc(lnw_ready, 1)
            def diagonal(t):
                dve.wait_ge(decay_ready, NH * (t + 1))
                for h in range(NH):
                    d_h = decay[:, t, h * P:(h + 1) * P]
                    stt(d_h, ident[:, :], own[:, t, h:h + 1], d_h, ALU.mult, ALU.add).then_inc(decay_done, 1)
            def cut_turns(b):
                dve.wait_ge(theta_psum, b + 1)
                again(dve, theta_ready, b)
                cut_ = flat_rot[:, 0:TB * NH * NA]
                ts(cut_, bank[b % 2][:, :], MAGIC, -MAGIC, ALU.add, ALU.add).then_inc(turns_cut, 1)
                dve.wait_ge(turns_cut, b + 1)
                tt(theta[:, b * TB:(b + 1) * TB, :].rearrange("p j c -> p (j c)"), bank[b % 2][:, :], cut_,
                   ALU.subtract).then_inc(theta_ready, 1)

            def add_betas(q):
                dve.wait_ge(beta_psum, TB * (q + 1))
                a4 = acc[:, q * TB:(q + 1) * TB, :].rearrange("p t d -> p (t d)")
                tt(a4, a4, bank[2 + q % 2][:, :], ALU.add).then_inc(acc_ready, 1)

            for t in range(NT):
                if t < NBATCH:
                    cut_turns(t)
                diagonal(t)
                if t == NBATCH - 1:
                    dve.wait_ge(lnw_ready, 1)
                    dve.wait_ge(theta_ready, NBATCH)
                    v.memset(zer[0:1, 0:1], 0.0).then_inc(scratch_free, 1)
                if NBATCH <= t < 2 * NBATCH:
                    add_betas(t - NBATCH)

            def at(tile, t, k=None):
                x = tile[:, bass.ds(t, 1), :] if k is None else tile[:, k, bass.ds(t, 1), :]
                return x.rearrange("p o h -> p (o h)")

            def token(t):
                again(dve, s["zx_psum"], t)
                ts(xt_s[:, :], xnT[:, bass.ds(t * P, P)], 1.0, None, ALU.mult).then_inc(s["xt_ready"], 1)
                again(dve, s["trig_ready"], t)
                th = theta[:, bass.ds(t, 1), :].rearrange("p o c -> p (o c)")
                stt(ang[:, :], th, -1.0, th, ALU.mult, ALU.max).then_inc(s["ang_ready"], 1)

            def mean_square(t):
                dve.wait_ge(s["sq_done"], 2 * (t + 1))
                again(dve, s["rms_ready"], t)
                ts(ms[:, :], ms[:, :], 1.0 / DS, EPS, ALU.mult, ALU.add).then_inc(s["ms_ready"], 1)

            def weigh(t):
                dve.wait_ge(s["zx_psum"], t + 1)
                again(dve, s["state_psum"], t)
                tt(xs_w[:, :, :], bank[0][:, DI:2 * DI].rearrange("p (h d) -> p h d", d=HD),
                   bc(at(wstate, t), HD, 1), ALU.mult).then_inc(s["xs_ready"], 1)

            def norm_kq(t):
                dve.wait_ge(s["rms_ready"], t + 1)
                for q in range(2):
                    last = stt(bn_kq[:, q, :], bank[1][:, q * DS:(q + 1) * DS], rms[:, q:q + 1], nw_kq[:, q, :],
                               ALU.mult, ALU.mult)
                last.then_inc(s["bn_ready"], 1)
                dve.wait_ge(s["bn_ready"], t + 1)
                again(dve, s["state_psum"], t)
                tt(kq[:, 1], bc(bn_kq[:, 1, :], NH, 0), bias_kq[:, 1], ALU.add).then_inc(s["q0_ready"], 1)

            def rot_cosine(t):
                dve.wait_ge(s["k0_ready"], t + 1)
                dve.wait_ge(s["q0_ready"], t + 1)
                dve.wait_ge(s["trig_ready"], t + 1)
                cs = bc(trig[:, 1, :, :], 2, 0)
                x1, x2 = kq[:, :, :, 0:NA], kq[:, :, :, NA:2 * NA]
                tt(rot[:, 0], x1, cs, ALU.mult).then_inc(s["rot_dve"], 1)
                tt(rot[:, 2], x2, cs, ALU.mult).then_inc(s["rot_dve"], 1)

            def rotate(t):
                dve.wait_ge(s["rot_dve"], 2 * (t + 1))
                dve.wait_ge(s["rot_pool"], 2 * (t + 1))
                x1, x2 = kq[:, :, :, 0:NA], kq[:, :, :, NA:2 * NA]
                tt(x1, rot[:, 0], rot[:, 1], ALU.subtract).then_inc(s["k_rot"], 1)
                tt(x2, rot[:, 2], rot[:, 3], ALU.add).then_inc(s["k_rot"], 1)

            def mask(u):
                dve.wait_ge(decay_done, NH * NT)
                dve.wait_ge(s["score_psum"], u + 1)
                if not isinstance(u, int) or u + 1 < NT:
                    dve.wait_ge(s["k0_ready"], u + 2)
                    dve.wait_ge(s["q0_ready"], u + 2)
                tt(sd[:, :, :].rearrange("p h i -> p (h i)"), bank[2][:, :],
                   decay[:, bass.ds(u, 1), :].rearrange("p o c -> p (o c)"), ALU.mult).then_inc(s["sd_ready"], 1)

            def from_state(u):
                dve.wait_ge(s["inter_psum"], u + 1)
                dve.wait_ge(s["intra_psum"], u + 1)
                again(dve, s["yT_psum"], u)
                tt(ysum[:, :, :], bank[3][:, DI:2 * DI].rearrange("p (h d) -> p h d", d=HD),
                   bc(at(eL, u, 0), HD, 1), ALU.mult).then_inc(s["y1_ready"], 1)

            def fade(u):
                dve.wait_ge(s["inter_psum"], u + 1)
                tt(state[:, :, :], state[:, :, :], bc(at(eL, u, 2), HD, 1), ALU.mult).then_inc(s["state_dec"], 1)

            def carry(u):
                dve.wait_ge(s["state_psum"], u + 1)
                dve.wait_ge(s["state_dec"], u + 1)
                tt(state[:, :, :], state[:, :, :], bank[1][:, DI:2 * DI].rearrange("p (h d) -> p h d", d=HD), ALU.add)\
                    .then_inc(s["state_ready"], 1)

            def join(u):
                dve.wait_ge(s["intra_psum"], u + 1)
                dve.wait_ge(s["y1_ready"], u + 1)
                tt(ysum[:, :, :], ysum[:, :, :], bank[3][:, 0:DI].rearrange("p (h d) -> p h d", d=HD), ALU.add)\
                    .then_inc(s["y2_ready"], 1)

            def gate_y(u):
                dve.wait_ge(s["y2_ready"], u + 1)
                dve.wait_ge(s["xd_ready"], u + 1)
                tt(ysum[:, :, :], ysum[:, :, :], xd_w[:, :, :], ALU.add).then_inc(s["y3_ready"], 1)
                dve.wait_ge(s["y3_ready"], u + 1)
                dve.wait_ge(s["gate_ready"], u + 1)
                tt(ysum[:, :, :].rearrange("p h d -> p (h d)"), ysum[:, :, :].rearrange("p h d -> p (h d)"),
                   gate[:, :], ALU.mult).then_inc(s["y_ready"], 1)

            def add_out(u):
                dve.wait_ge(s["out_psum"], u + 1)
                o = acc[:, bass.ds(u, 1), :].rearrange("p o d -> p (o d)")
                tt(o, o, bank[3][:, 0:DM], ALU.add).then_inc(s["acc_done"], 1)

            def product(b):
                if not exists(b):
                    return
                dve.wait_ge(f["h3_psum"], cnt(b))
                dve.wait_ge(f["gl_ready"], cnt(b))
                again(dve, f["hT_psum"], num(b))
                tt(hm[:, :], gl[:, :], bank[5][:, :], ALU.mult).then_inc(f["hm_ready"], 1)

            def norm_y(b):
                if not exists(b):
                    return
                e = dve.value_load(blk_e[0:1, bass.ds(num(b), 1)], min_val=0, max_val=NE - 1)
                dve.wait_ge(f["y_psum"], cnt(b))
                v.bn_stats(st6[:, :], bank[7][:, 0:DM]).then_inc(f["st_ready"], 1)
                dve.wait_ge(gam_in, 16)
                dve.wait_ge(f["st_ready"], cnt(b))
                again(dve, f["rstd_ready"], num(b))
                v.bn_aggr(mv[:, :], st6[:, :]).then_inc(f["mv_ready"], 1)
                dve.wait_ge(f["mv_ready"], cnt(b))
                ts(mv[:, 1:2], mv[:, 1:2], EPS, None, ALU.add).then_inc(f["ve_ready"], 1)
                again(dve, f["res_ready"], num(b))
                stt(yc[:, :], bank[7][:, 0:DM], mv[:, 0:1], gam[:, bass.ds(e, 1), :].rearrange("p o d -> p (o d)"),
                    ALU.subtract, ALU.mult).then_inc(f["yc_ready"], 1)

            def iteration(t, blocks):
                first, second, (b0, b1, b2) = parts(t, blocks)
                if isinstance(t, int) and t == 1:
                    dve.wait_ge(blk_e_ready, 1)
                    dve.wait_ge(gam_in, 16)
                if first:
                    token(t)
                if b0:
                    norm_y(shift_by(b0, -2))
                if not isinstance(t, int) or t >= 2:
                    add_out(t - 2)
                if first:
                    mean_square(t)
                    weigh(t)
                    norm_kq(t)
                if b0:
                    product(b0)
                if second:
                    mask(t - 1)
                if b1:
                    norm_y(shift_by(b1, -2))
                if first:
                    rot_cosine(t)
                if second and first:
                    fade(t - 1)
                if first:
                    rotate(t)
                if second:
                    from_state(t - 1)
                    join(t - 1)
                if b1:
                    product(b1)
                if second:
                    gate_y(t - 1)
                if second and first:
                    carry(t - 1)
                if b2:
                    norm_y(shift_by(b2, -2))
                    product(b2)
            weave(dve, iteration)
            add_out(NT - 1)

            q4 = NT // 4
            flat = acc[:, :, :].rearrange("p t d -> p (t d)")
            d = decay[:, :, :].rearrange("p t c -> p (t c)")
            dve.wait_ge(s["acc_done"], NT)
            for q in range(4):
                dve.wait_ge(res_in[q], 16 * TOPK)
                c = q * q4 * DM
                w = q4 * DM
                tt(flat[:, c:c + w], flat[:, c:c + w], d[:, c:c + w], ALU.add).then_inc(fin_a, 1)
                dve.wait_ge(fin_a, q + 1)
                tt(flat[:, c:c + w], flat[:, c:c + w], d[:, T + c:T + c + w], ALU.add).then_inc(fin_ready, 1)


_INS = ['L0_attn_u', 'L0_attn_W_in', 'L0_attn_W_out', 'L0_attn_dt_bias', 'L0_attn_B_bias', 'L0_attn_C_bias',
        'L0_attn_B_norm_w', 'L0_attn_C_norm_w', 'L0_attn_D', 'L0_ffn_Wr', 'L0_ffn_br', 'L0_ffn_W1', 'L0_ffn_W3',
        'L0_ffn_W2', 'L0_ffn_gamma', 'L0_ffn_beta']


def kernel(**inputs):
    import numpy as _np
    import concourse.bacc as _bacc
    from concourse import mybir as _mybir
    from concourse.bass_utils import run_bass_kernel_spmd as _run

    nc = _bacc.Bacc("TRN2", target_bir_lowering=False, num_devices=1)
    arrays, args = {}, []
    for name in _INS:
        a = _np.ascontiguousarray(inputs[name])
        arrays[f"in_{name}_dram"] = a
        args.append(nc.dram_tensor(f"in_{name}_dram", a.shape, _mybir.dt.from_np(a.dtype), kind="ExternalInput").ap())
    u = inputs['L0_attn_u']
    out = nc.dram_tensor("out_0_dram", tuple(u.shape), _mybir.dt.float32, kind="ExternalOutput").ap()
    build(nc, *args, out)
    r = _run(nc, [arrays], core_ids=[0])
    return r.results[0]["out_0_dram"]
```

```python
import concourse.bass as bass
from concourse import mybir
from contextlib import ExitStack


def build(nc, A_u, A_Win, A_Wout, A_dtb, A_Bb, A_Cb, A_Bw, A_Cw, A_D, A_Wr, A_br, A_W1, A_W3, A_W2,
          A_gamma, A_beta, A_out):
    fp32, bf16, i32 = mybir.dt.float32, mybir.dt.bfloat16, mybir.dt.int32
    ALU = mybir.AluOpType
    ACT = mybir.ActivationFunctionType
    X = mybir.AxisListType.X

    P = 128
    NBATCH, SEQ, DM = A_u.shape
    NT = NBATCH * SEQ // P
    TB = SEQ // P
    T = NT * P
    NH, DS = A_Bb.shape
    DI = A_Wout.shape[0]
    HD = DI // NH
    NA = (A_Win.shape[1] - 2 * DI - 2 * DS - 3 * NH)
    NE, _, F = A_W1.shape
    FC = F // P
    TOPK = 2
    ZX, BC = 2 * DI, 2 * DS
    NARROW = 3 * NH + NA + NE
    WIDE = ZX + BC
    NB = (TOPK * T - NE) // P + NE
    LOADED = NB + 2
    NROWS = LOADED * P
    ROW = DM + 2
    HALF = 3
    SLOTS = 2 * HALF
    PAIRS = (NT - 2) // 2
    BEFORE = 2 + HALF
    assert NT % 2 == 0 and NA == 32
    assert BEFORE + SLOTS * PAIRS == NB
    PRE = 8640
    WARM = 6
    WARM_ROUTING = 18
    EPS = 1e-5
    A_FLOOR = 1e-4
    MAGIC = 1.5 * 2.0 ** 23
    INV_2PI = 0.15915494309189535
    TWO_PI = 6.2831845
    HALF_PI = 1.5707963267948966
    TINY = 1e-37
    NEG = -1e30

    rows_dram = nc.dram_tensor("rows_dram", [NROWS, ROW], fp32, kind="Internal").ap()
    res_dram = nc.dram_tensor("res_dram", [TOPK * T + NROWS, DM], fp32, kind="Internal").ap()

    ctx = ExitStack()
    with ctx:
        def sb(name, shape, dt=fp32):
            return ctx.enter_context(nc.sbuf_tensor(name, shape, dt))

        def sem(name):
            return ctx.enter_context(nc.semaphore(name))

        def sems(name, n):
            return [sem(f"{name}{j}") for j in range(n)]

        bank = [ctx.enter_context(nc.psum_tensor(f"bank{i}", [P, 512], fp32)) for i in range(8)]

        w_up = sb("w_up", [P, HALF, 2, F])
        w2 = sb("w2", [P, NE, FC, DM])
        w_in = sb("w_in", [P, WIDE + NARROW])
        w_out = sb("w_out", [P, 2, DM])
        gam = sb("gam", [P, NE, DM])
        bias_kq = sb("bias_kq", [P, 2, NH, DS])
        nw_kq = sb("nw_kq", [P, 2, DS])
        br = sb("br", [P, NE])
        dtb = sb("dtb", [P, NH])
        dskip = sb("dskip", [P, NH])
        ident = sb("ident", [P, P])
        iota_e = sb("iota_e", [P, NE])
        iota_b = sb("iota_b", [1, LOADED])
        mhalf = sb("mhalf", [P, NT])
        half_pi = sb("half_pi", [P, 1])
        zero = sb("zero", [P, 1])

        acc = sb("acc", [P, NT, DM])
        xnT = sb("xnT", [P, T])
        xrow = sb("xrow", [P, NT, ROW])
        theta = sb("theta", [P, NT, NH * NA])
        decay = sb("decay", [P, NT, NH * P])
        rows0 = decay[:, :, :].rearrange("p t c -> p (t c)")[:, 0:LOADED * ROW]\
            .rearrange("p (b c) -> p b c", c=ROW)
        eL = sb("eL", [P, 3, NT, NH])
        own = sb("own", [P, NT, NH])
        lnw = sb("lnw", [P, NT, NH])
        wstate = sb("wstate", [P, NT, NH])
        slots_f = sb("slots_f", [P, TOPK, NT])
        slots = sb("slots", [P, TOPK, NT], i32)
        wtop = sb("wtop", [P, TOPK, NT])
        blk_e = sb("blk_e", [1, LOADED], i32)

        xt_s = sb("xt_s", [P, P])
        ms = sb("ms", [P, 2])
        rms = sb("rms", [P, 2])
        kq = sb("kq", [P, 2, NH, DS])
        ang = sb("ang", [P, NH * NA])
        trig = sb("trig", [P, 2, NH, NA])
        rot = sb("rot", [P, 4, 2, NH, NA])
        flat_rot = rot[:, :, :, :, :].rearrange("p r q h n -> p (r q h n)")
        kqT = sb("kqT", [P, 2, NH * P])
        sd = sb("sd", [P, NH, P])
        bn_kq = sd[:, 0:2, :]
        x_w = sb("x_w", [P, NH, HD])
        xs_w = sb("xs_w", [P, NH, HD])
        xd_w = sb("xd_w", [P, NH, HD])
        gate = sb("gate", [P, DI])
        ysum = sb("ysum", [P, NH, HD])
        yT = sb("yT", [P, DI])
        state = sb("state", [P, NH, HD])

        blk = sb("blk", [P, SLOTS, ROW])
        blkT = sb("blkT", [P, 2, P])
        rows_end = xrow[:, :, :].rearrange("p t c -> p (t c)")
        gl = rows_end[:, 0:F]
        hm = rows_end[:, F:3 * F].rearrange("p (s f) -> p s f", f=F)
        res = rows_end[:, 3 * F:3 * F + HALF * DM].rearrange("p (j d) -> p j d", d=DM)
        st6 = sb("st6", [P, 6])
        mv = sb("mv", [P, 2])
        rstd = sb("rstd", [P, 1])
        rw = sb("rw", [P, 1])
        yc = rows_end[:, 3 * F + HALF * DM:3 * F + (HALF + 1) * DM]

        flat_sd = sd[:, :, :].rearrange("p h i -> p (h i)")
        tri = flat_sd[:, 0:P]
        adt = flat_sd[:, P:P + NT * NH].rearrange("p (t h) -> p t h", h=NH)
        ident_h = flat_sd[:, P + NT * NH:2 * P].bitcast(bf16)
        neg_h = flat_sd[:, 2 * P:4 * P].bitcast(bf16).rearrange("p (h i) -> p h i", i=P)
        assert NT * NH == P // 2

        pre = sb("pre", [P, PRE])
        used = [0]

        def scratch(shape, dt=fp32):
            n = 1
            for s in shape[1:]:
                n *= s
            flat = pre[:, :]
            words = n if dt != bf16 else (n + 1) // 2
            v = flat[:, used[0]:used[0] + words]
            used[0] += words
            if dt != fp32:
                v = v.bitcast(dt)
            if len(shape) == 3:
                v = v.rearrange("p (a b) -> p a b", b=shape[2])
            if len(shape) == 4:
                v = v.rearrange("p (a b c) -> p a b c", b=shape[2], c=shape[3])
            return v

        low = scratch([P, P])
        ones = scratch([P, P])
        shift = scratch([P, P])
        wrap = scratch([P, P])
        tri_h = scratch([P, P], bf16)
        ones_h = scratch([P, P], bf16)
        stats = scratch([P, NT, 6])
        mvx = scratch([P, NT, 2])
        vx = scratch([P, NT])
        rx = scratch([P, NT])
        nar = scratch([P, NT, NARROW])
        turns = scratch([P, NT, NH * NA])
        tpre = scratch([P, NBATCH, TB - 1, NH * NA])
        lg, rt, sc1, posb, pick = (
            tpre.rearrange("p b j c -> p (b j c)")[:, n * NT * NE:(n + 1) * NT * NE]
            .rearrange("p (t e) -> p t e", e=NE) for n in range(5))
        cmpb = turns.rearrange("p t c -> p (t c)")[0:1, 0:LOADED * NE].rearrange("p (b e) -> p b e", e=NE)
        lnG = scratch([P, NT, NH])
        coefG = scratch([P, NT, NH])
        sp_x = scratch([P, 2, NT * NH])
        sp_e = scratch([P, 2, NT * NH])
        sp_u = scratch([P, 2, NT * NH])
        sp_l = scratch([P, 2, NT * NH])
        sp_r = scratch([P, 2, NT * NH])
        sp_t = scratch([P, 2, NT * NH])
        sp = scratch([P, 2, NT, NH])
        bet = scratch([P, NT, NH])
        bet_e = scratch([P, NT, NH])
        dtp = scratch([P, NT, NH])
        g_t = scratch([P, NT, NH])
        m1 = scratch([P, NT])
        m2 = scratch([P, NT])
        e2 = scratch([P, NT])
        oh1 = scratch([P, NT, NE])
        oh2 = scratch([P, NT, NE])
        comb = scratch([P, NT, NE])
        cnt_b = scratch([P, NE])
        ends = scratch([P, NE])
        base = scratch([P, NE])
        zer = scratch([P, NE])
        blkf = scratch([P, LOADED])[0:1]
        both_h = scratch([P, NT, NE], bf16)
        cut_ = scratch([P, TB * NH * NA])
        beta_e = scratch([P, DM])[0:NE]
        assert used[0] <= PRE, used[0]
        combT = sb("combT", [NE, 4, TB * P])

        x_in = sems("x_in", NBATCH)
        win_in, small_in, gam_in, w2_in = (sem(n) for n in (
            "win_in", "small_in", "gam_in", "w2_in"))
        rows0_set, rows0_out, consts_set, pool_step, dve_step = (sem(n) for n in (
            "rows0_set", "rows0_out", "consts_set", "pool_step", "dve_step"))
        var_ready, rstd_ready, xn_ready, xnT_psum, xnT_ready, nar_psum, nar_ready = (sem(n) for n in (
            "var_ready", "rstd_ready", "xn_ready", "xnT_psum", "xnT_ready", "nar_psum", "nar_ready"))
        e_in, e_out, l_in, l_out = (sem(n) for n in ("e_in", "e_out", "l_in", "l_out"))
        adt_ready, L_psum, L_exp, bet_ready, betn_psum, turns_ready, theta_psum, theta_ready = (sem(n) for n in (
            "adt_ready", "L_psum", "L_exp", "bet_ready", "betn_psum", "turns_ready", "theta_psum", "theta_ready"))
        top_in, top_out, both_ready, pos_psum, pos_used, slots_ready = (sem(n) for n in (
            "top_in", "top_out", "both_ready", "pos_psum", "pos_used", "slots_ready"))
        row_meta, sent, comb_ready, combT_psum, combT_ready, beta_psum, acc_ready, turns_cut = (sem(n) for n in (
            "row_meta", "sent", "comb_ready", "combT_psum", "combT_ready", "beta_psum", "acc_ready", "turns_cut"))
        zero_set, g_ready, lng_ready, lnw_ready, arm_psum, decay_ready, decay_done, blk_e_ready = (
            sem(n) for n in ("zero_set", "g_ready", "lng_ready", "lnw_ready", "arm_psum", "decay_ready", "decay_done",
                             "blk_e_ready"))
        names = ("xt_ready zx_psum bc_psum sq_done ms_ready rms_ready bn_ready k0_ready q0_ready ang_ready"
                 " trig_ready rot_dve rot_pool k_rot kT_psum qT_psum kT_ready qT_ready"
                 " score_psum sd_ready x_ready xd_ready xs_ready gate_ready inter_psum intra_psum state_psum"
                 " state_dec state_ready y1_ready y2_ready y3_ready y_ready yT_psum yT_ready out_psum acc_done")
        s = {n: sem(n) for n in names.split()}
        fnames = ("blkT_psum blkT_ready h1_psum h3_psum gl_ready hm_ready y_psum"
                  " st_ready mv_ready ve_ready rstd_ready rw_ready yc_ready res_ready")
        f = {n: sem("f_" + n) for n in fnames.split()}
        blk_in, up_in, res_out = sems("f_blk_in", SLOTS), sems("f_up_in", SLOTS), sems("f_res_out", SLOTS)
        res_in = sems("res_in", 4)
        fin_a, fin_ready, out_done = (sem(n) for n in ("fin_a", "fin_ready", "out_done"))

        PARTS = (0, 5, 10, 14, NT)
        SPARE = (4, 5, 0, 6)
        block = ctx.enter_context(nc.Block())

        def bc(ap, n, k):
            v = ap.unsqueeze(k + 1)
            shape = list(v.shape)
            shape[k + 1] = n
            return v.to_broadcast(shape)

        def num(blk_):
            j, i = blk_
            return SLOTS * i + (j + BEFORE)

        def cnt(blk_):
            j, i = blk_
            return SLOTS * i + (j + BEFORE + 1)

        def nth(blk_):
            j, i = blk_
            return i + 2 if j >= SLOTS - BEFORE else i + 1

        def shift_by(blk_, n):
            j, i = blk_
            return ((j + n) % SLOTS, i + (j + n) // SLOTS)

        def exists(blk_):
            n = num(blk_)
            return not isinstance(n, int) or 0 <= n < NB

        def loaded(blk_):
            n = num(blk_)
            return not isinstance(n, int) or 0 <= n < LOADED

        def again(eng, sem_, v):
            if not isinstance(v, int) or v > 0:
                eng.wait_ge(sem_, v)

        def weave(eng, iteration):
            iteration(0, [(SLOTS - BEFORE + j, -1) for j in range(BEFORE - HALF)])
            iteration(1, [(SLOTS - HALF + j, -1) for j in range(HALF)])
            with eng.Fori(0, PAIRS) as i:
                iteration(2 * i + 2, [(j, i) for j in range(HALF)])
                iteration(2 * i + 3, [(HALF + j, i) for j in range(HALF)])
            iteration(NT, [(j, PAIRS) for j in range(HALF)])

        def parts(t, blocks):
            first = not (isinstance(t, int) and t == NT)
            second = not (isinstance(t, int) and t == 0)
            return first, second, blocks + [None] * (HALF - len(blocks))

        def combT4(q):
            return combT[:, q, :]

        @block.sync
        def _(sp):
            x_v = A_u.rearrange("b (j p) d -> p (b j) d", p=P)
            for b in range(NBATCH):
                sp.dma_start(acc[:, b * TB:(b + 1) * TB, :], x_v[:, b * TB:(b + 1) * TB, :])\
                    .then_inc(x_in[b], 16)
            sp.dma_start(w_in[:, 0:WIDE + NARROW - NE], A_Win).then_inc(win_in, 16)
            sp.dma_start(w_in[:, WIDE + NARROW - NE:], A_Wr).then_inc(win_in, 16)
            sp.dma_start(w_out[:, :, :], A_Wout.rearrange("(c p) d -> p c d", p=P)).then_inc(small_in, 16)
            sp.dma_start(beta_e[:, :], A_beta).then_inc(small_in, 16)

            def spread(dst, src):
                sp.dma_start(dst, src.rearrange("(o n) -> o n", o=1).to_broadcast([P, src.shape[0]]))\
                    .then_inc(small_in, 16)
            spread(br[:, :], A_br)
            spread(dtb[:, :], A_dtb)
            spread(dskip[:, :], A_D)
            spread(bias_kq[:, 0, :, :].rearrange("p h n -> p (h n)"), A_Bb.rearrange("h n -> (h n)"))
            spread(bias_kq[:, 1, :, :].rearrange("p h n -> p (h n)"), A_Cb.rearrange("h n -> (h n)"))
            spread(nw_kq[:, 0, :], A_Bw)
            spread(nw_kq[:, 1, :], A_Cw)
            sp.wait_ge(rows0_set, 2)
            sp.dma_start(rows_dram.rearrange("(b p) c -> p b c", p=P), rows0).then_inc(rows0_out, 16)
            flat = A_gamma.rearrange("e d -> (e d)")
            sp.dma_start(gam[:, :, :].rearrange("p e d -> p (e d)"),
                         flat.rearrange("(o n) -> o n", o=1).to_broadcast([P, NE * DM])).then_inc(gam_in, 16)
            for q in range(4):
                e0, e1 = q * NE // 4, (q + 1) * NE // 4
                sp.dma_start(w2[:, e0:e1, :, :], A_W2[e0:e1].rearrange("e (c p) d -> p e c d", p=P))\
                    .then_inc(w2_in, 16)

            def load(blk_):
                b = num(blk_)
                sp.dma_start(blk[:, blk_[0], :], rows_dram[bass.ds(b * P, P), :]).then_inc(blk_in[blk_[0]], 16)

            def load_up(blk_):
                e = sp.value_load(blk_e[0:1, bass.ds(num(blk_), 1)], min_val=0, max_val=NE - 1)
                if exists(shift_by(blk_, -HALF)):
                    sp.wait_ge(f["h3_psum"], cnt(shift_by(blk_, -HALF)))
                for n, w in enumerate((A_W1, A_W3)):
                    sp.dma_start(w_up[:, blk_[0] % HALF, n, :], w[bass.ds(e, 1)].rearrange("o d f -> d (o f)"))\
                        .then_inc(up_in[blk_[0]], 16)
            sp.wait_ge(blk_e_ready, 1)
            for b in range(HALF):
                load_up(shift_by((SLOTS - BEFORE, -1), b))
            sp.wait_ge(sent, 16 * TOPK * NT)
            for b in range(SLOTS):
                load(shift_by((SLOTS - BEFORE, -1), b))
            for b in range(HALF, SLOTS):
                load_up(shift_by((SLOTS - BEFORE, -1), b))

            def refill(blk_):
                old = (blk_[0], blk_[1] - 1)
                sp.wait_ge(res_out[old[0]], 16 * nth(old))
                load(blk_)
                load_up(blk_)
            rounds = LOADED // SLOTS - 1
            with sp.Fori(0, rounds) as i:
                for j in range(SLOTS):
                    refill(shift_by((SLOTS - BEFORE, i), j))
            for j in range(LOADED % SLOTS):
                refill(shift_by((SLOTS - BEFORE, rounds), j))
            for q in range(4):
                if q == 0:
                    for b in range(NB - SLOTS, NB):
                        last_of = shift_by((SLOTS - BEFORE, -1), b)
                        sp.wait_ge(res_out[last_of[0]], 16 * nth(last_of))
                    sp.wait_ge(s["sd_ready"], NT)
                p0, p1 = PARTS[q], PARTS[q + 1]
                for k in range(TOPK):
                    rv = res_dram[k * T:(k + 1) * T, :].rearrange("(t p) d -> p t d", p=P)
                    dst = decay[:, :, :].rearrange("p t c -> p (t c)")[:, k * T:(k + 1) * T]\
                        .rearrange("p (t d) -> p t d", d=DM)
                    sp.dma_start(dst[:, p0:p1, :], rv[:, p0:p1, :]).then_inc(res_in[q], 16)
            out_v = A_out.rearrange("b (j p) d -> p (b j) d", p=P)
            for q in range(4):
                sp.wait_ge(fin_ready, q + 1)
                sp.dma_start(out_v[:, PARTS[q]:PARTS[q + 1], :], acc[:, PARTS[q]:PARTS[q + 1], :])\
                    .then_inc(out_done, 16)
            sp.wait_ge(out_done, 64)

        @block.gpsimd
        def _(pool):
            g = nc.gpsimd
            for m, v in ((ident, 0.0), (ones, 1.0), (tri, 1.0), (low, 1.0), (shift, 0.0), (wrap, 0.0),
                         (mhalf, -0.5), (ident_h, 0.0), (ones_h, 1.0), (tri_h, 1.0), (half_pi, HALF_PI)):
                g.memset(m[:, :], v).then_inc(pool_step, 1)
            g.memset(neg_h[:, :, :], 0.0).then_inc(pool_step, 1)
            g.iota(iota_e[:, :], [[1, NE]], base=0, channel_multiplier=0,
                   allow_small_or_imprecise_dtypes=True).then_inc(pool_step, 1)
            g.iota(iota_b[:, :], [[1, LOADED]], base=0, channel_multiplier=0,
                   allow_small_or_imprecise_dtypes=True).then_inc(pool_step, 1)
            pool.wait_ge(pool_step, 14)
            for m, cmp, fill, b0, cm, step in (
                    (ident, ALU.not_equal, 1.0, 0, 1, -1), (ident_h, ALU.not_equal, 1.0, 0, 1, -1),
                    (tri, ALU.is_ge, 0.0, 0, -1, 1), (tri_h, ALU.is_ge, 0.0, 0, -1, 1),
                    (low, ALU.is_gt, 0.0, 0, 1, -1), (shift, ALU.not_equal, 1.0, -1, 1, -1),
                    (wrap, ALU.not_equal, 1.0, P - 1, P, -1)):
                g.affine_select(out=m[:, :], in_=m[:, :], compare_op=cmp, fill=fill, base=b0,
                                pattern=[[step, P]], channel_multiplier=cm).then_inc(consts_set, 1)
            g.affine_select(out=neg_h[:, :, :], in_=neg_h[:, :, :], compare_op=ALU.is_gt, fill=NEG, base=0,
                            pattern=[[0, NH], [1, P]], channel_multiplier=-1).then_inc(consts_set, 1)
            for b in range(NBATCH):
                if b == 2:
                    pool.wait_ge(rows0_set, 1)
                    g.iota(rows0[:, :, ROW - 1:ROW].bitcast(i32), [[P, LOADED], [1, 1]], base=TOPK * T,
                           channel_multiplier=1).then_inc(rows0_set, 1)
                c = slice(b * TB, (b + 1) * TB)
                pool.wait_ge(var_ready, b + 1)
                g.tensor_tensor(rx[:, c], vx[:, c], mhalf[:, c], ALU.pow).then_inc(rstd_ready, 1)
            g.iota(xrow[:, :, ROW - 1:ROW].bitcast(i32), [[P, NT], [1, 1]], base=0, channel_multiplier=1)\
                .then_inc(row_meta, 1)
            pool.wait_ge(row_meta, 2)
            pool.wait_ge(slots_ready, 1)
            pool.wait_ge(xn_ready, NT)
            pool.wait_ge(rows0_out, 16)
            for k in range(TOPK):
                if k:
                    pool.wait_ge(sent, 16 * NT)
                    g.tensor_copy(xrow[:, :, DM:DM + 1].rearrange("p t o -> p (t o)"), wtop[:, 1, :])\
                        .then_inc(row_meta, 1)
                    g.iota(xrow[:, :, ROW - 1:ROW].bitcast(i32), [[P, NT], [1, 1]], base=k * T,
                           channel_multiplier=1).then_inc(row_meta, 1)
                    pool.wait_ge(row_meta, 4)
                    pool.wait_ge(slots_ready, 2)
                for t in range(NT):
                    g.indirect_dma_start(out=rows_dram, in_=xrow[:, t, :], in_offset=None,
                                         out_offset=bass.IndirectOffsetOnAxis(ap=slots[:, k, t:t + 1], axis=0))\
                        .then_inc(sent, 16)

            def skip_x(u):
                pool.wait_ge(s["x_ready"], u + 1)
                again(pool, s["y3_ready"], u)
                g.tensor_tensor(xd_w[:, :, :], x_w[:, :, :], bc(dskip[:, :], HD, 1), ALU.mult)\
                    .then_inc(s["xd_ready"], 1)

            def rms_pow(t):
                pool.wait_ge(s["ms_ready"], t + 1)
                again(pool, s["bn_ready"], t)
                g.tensor_tensor(rms[:, :], ms[:, :], mhalf[:, 0:2], ALU.pow).then_inc(s["rms_ready"], 1)

            def bias_k(t):
                pool.wait_ge(s["bn_ready"], t + 1)
                again(pool, s["state_psum"], t)
                g.tensor_tensor(kq[:, 0], bc(bn_kq[:, 0, :], NH, 0), bias_kq[:, 0], ALU.add)\
                    .then_inc(s["k0_ready"], 1)

            def rot_sine(t):
                pool.wait_ge(s["k0_ready"], t + 1)
                pool.wait_ge(s["q0_ready"], t + 1)
                pool.wait_ge(s["trig_ready"], t + 1)
                again(pool, s["k_rot"], 2 * t)
                sn = bc(trig[:, 0, :, :], 2, 0)
                x1, x2 = kq[:, :, :, 0:NA], kq[:, :, :, NA:2 * NA]
                g.tensor_tensor(rot[:, 1], x2, sn, ALU.mult).then_inc(s["rot_pool"], 1)
                g.tensor_tensor(rot[:, 3], x1, sn, ALU.mult).then_inc(s["rot_pool"], 1)

            def finish(b):
                if not exists(b):
                    return
                pool.wait_ge(blk_in[b[0]], 16)
                pool.wait_ge(f["ve_ready"], cnt(b))
                again(pool, f["rw_ready"], num(b))
                g.tensor_tensor(rstd[:, :], mv[:, 1:2], mhalf[:, 0:1], ALU.pow).then_inc(f["rstd_ready"], 1)
                pool.wait_ge(f["rstd_ready"], cnt(b))
                again(pool, f["res_ready"], num(b))
                g.tensor_tensor(rw[:, :], rstd[:, :], blk[:, b[0], DM:DM + 1], ALU.mult).then_inc(f["rw_ready"], 1)

            def store(b):
                if not exists(b):
                    return
                pool.wait_ge(blk_in[b[0]], 16)
                pool.wait_ge(f["res_ready"], cnt(b))
                g.indirect_dma_start(out=res_dram, in_=res[:, b[0] % HALF, :], in_offset=None,
                                     out_offset=bass.IndirectOffsetOnAxis(
                                         ap=blk[:, b[0], ROW - 1:ROW].bitcast(i32), axis=0))\
                    .then_inc(res_out[b[0]], 16)

            def iteration(t, blocks):
                first, second, (b0, b1, b2) = parts(t, blocks)
                if second and first:
                    skip_x(t - 1)
                if b0:
                    finish(shift_by(b0, -2))
                if first:
                    rms_pow(t)
                    bias_k(t)
                if b0:
                    store(shift_by(b0, -2))
                if first:
                    rot_sine(t)
                if b1:
                    finish(shift_by(b1, -2))
                if b1:
                    store(shift_by(b1, -2))
                if second and not first:
                    skip_x(t - 1)
                if b2:
                    finish(shift_by(b2, -2))
                    store(shift_by(b2, -2))
            weave(pool, iteration)

        @block.tensor
        def _(pe):
            m = nc.tensor.matmul
            pe.wait_ge(consts_set, 8)
            for _ in range(WARM):
                m(bank[7][:, :], ones_h[:, :], neg_h[:, :, :].rearrange("p h i -> p (h i)"), start=True, stop=True)
            per = NT // 2
            for b in range(NBATCH + 1):
                if b < NBATCH:
                    for j in range(TB):
                        t = b * TB + j
                        pe.wait_ge(xn_ready, t + 1)
                        nc.tensor.transpose(bank[b][:, j * P:(j + 1) * P], xrow[:, t, 0:DM], ident[:, :])\
                            .then_inc(xnT_psum, 1)
                if b:
                    pe.wait_ge(win_in, 32)
                    pe.wait_ge(xnT_ready, b)
                    for t in range((b - 1) * TB, b * TB):
                        c = (t % per) * NARROW
                        m(bank[4 + t // per][:, c:c + NARROW], xnT[:, t * P:(t + 1) * P], w_in[:, WIDE:],
                          start=True, stop=True).then_inc(nar_psum, 1)
            for _ in range(WARM_ROUTING):
                m(bank[7][:, :], ones_h[:, :], neg_h[:, :, :].rearrange("p h i -> p (h i)"), start=True, stop=True)
            pe.wait_ge(both_ready, 1)
            m(bank[0][:, 0:NT * NE], tri_h[:, :], both_h.rearrange("p t e -> p (t e)"),
              start=True, stop=False)
            for d in range(1, NT):
                m(bank[0][:, d * NE:NT * NE], ones_h[:, :],
                  both_h[:, 0:NT - d, :].rearrange("p t e -> p (t e)"), start=False, stop=(d == NT - 1))
            for t in range(NT):
                last = m(bank[1][:, 0:NE], ones_h[:, :], both_h[:, t, :], start=(t == 0), stop=(t == NT - 1))
            last.then_inc(pos_psum, 1)
            pe.wait_ge(comb_ready, 1)
            pe.wait_ge(pos_used, 1)
            pe.wait_ge(nar_ready, 2)
            pe.wait_ge(small_in, 16 * 9)
            for q in range(NBATCH):
                if q >= 2:
                    pe.wait_ge(combT_ready, q - 1)
                for c in range(TB):
                    nc.tensor.transpose(bank[q % 2][0:NE, c * P:(c + 1) * P], comb[:, q * TB + c, :], ident[:, :])\
                        .then_inc(combT_psum, 1)
            pe.wait_ge(adt_ready, 1)
            a_v = adt.rearrange("p t h -> p (t h)")
            W = NT * NH
            m(bank[2][:, 0:W], tri, a_v, start=True, stop=True)
            m(bank[2][:, W:2 * W], low, a_v, start=True, stop=True)
            m(bank[2][:, 2 * W:3 * W], ones, a_v, start=True, stop=True).then_inc(L_psum, 1)
            pe.wait_ge(bet_ready, 1)
            b4 = bet.rearrange("p (b j) h -> p b j h", j=TB)
            o4 = bank[3][:, 0:W].rearrange("p (b j h) -> p b j h", j=TB, h=NH)
            m(bank[3][:, 0:W], shift[:, :], bet.rearrange("p t h -> p (t h)"), start=True, stop=False)
            m(o4[:, :, 0:TB - 1, :], wrap[:, :], b4[:, :, 1:TB, :], start=False, stop=True).then_inc(betn_psum, 1)
            def sum_turns(b):
                pe.wait_ge(turns_ready, 1)
                if b >= 2:
                    pe.wait_ge(theta_ready, b - 1)
                v = turns[:, b * TB:(b + 1) * TB, :].rearrange("p j c -> p (j c)")
                q = tpre[:, b].rearrange("p j c -> p (j c)")
                m(bank[b % 2][:, :], tri, v, start=True, stop=False)
                m(bank[b % 2][:, P:], ones, q, start=False, stop=True).then_inc(theta_psum, 1)

            def sum_decays(t):
                out = bank[4 + t % 4]
                if t >= 4:
                    pe.wait_ge(decay_ready, NH * (t - 3))
                for h in range(NH):
                    m(out[:, h * P:(h + 1) * P], adt[:, t, h:h + 1].to_broadcast([P, P]), tri,
                      start=(h == 0), stop=False)
                m(out[:, :], ident_h[:, :], neg_h[:, :, :].rearrange("p h i -> p (h i)"),
                  start=False, stop=True).then_inc(arm_psum, 1)

            for t in range(NT):
                sum_decays(t)
                if t % 2 and 3 <= t < 3 + 2 * NBATCH:
                    sum_turns((t - 3) // 2)
            pe.wait_ge(theta_ready, NBATCH)

            def sum_betas(q):
                pe.wait_ge(combT_ready, q + 1)
                for c in range(TB):
                    m(bank[SPARE[q]][:, c * DM:(c + 1) * DM], combT4(q)[:, c * P:(c + 1) * P], beta_e[:, :],
                      start=True, stop=True).then_inc(beta_psum, 1)
            def project_zx(t):
                pe.wait_ge(s["xt_ready"], t + 1)
                again(pe, s["x_ready"], t)
                again(pe, s["xs_ready"], t)
                m(bank[0][:, :], xt_s[:, :], w_in[:, 0:ZX], start=True, stop=True).then_inc(s["zx_psum"], 1)

            def project_bc(t):
                again(pe, s["yT_ready"], t - 1)
                again(pe, s["state_ready"], t - 1)
                m(bank[1][:, 0:BC], xt_s[:, :], w_in[:, ZX:WIDE], start=True, stop=True).then_inc(s["bc_psum"], 1)

            def turn_kq(t):
                pe.wait_ge(s["k_rot"], 2 * (t + 1))
                again(pe, s["sd_ready"], t)
                for h in range(NH):
                    last = nc.tensor.transpose(bank[2][:, h * P:(h + 1) * P], kq[:, 0, h, :], ident[:, :])
                last.then_inc(s["kT_psum"], 1)
                again(pe, s["y2_ready"], t)
                for h in range(NH):
                    last = nc.tensor.transpose(bank[3][:, h * P:(h + 1) * P], kq[:, 1, h, :], ident[:, :])
                last.then_inc(s["qT_psum"], 1)

            def state_product(t):
                pe.wait_ge(s["xs_ready"], t + 1)
                again(pe, s["state_ready"], t)
                for h in range(NH):
                    last = m(bank[1][:, DI + h * HD:DI + (h + 1) * HD], kq[:, 0, h, :], xs_w[:, h, :],
                             start=True, stop=True)
                last.then_inc(s["state_psum"], 1)

            def scores(u):
                pe.wait_ge(s["kT_ready"], u + 1)
                pe.wait_ge(s["qT_ready"], u + 1)
                for h in range(NH):
                    last = m(bank[2][:, h * P:(h + 1) * P], kqT[:, 0, h * P:(h + 1) * P],
                             kqT[:, 1, h * P:(h + 1) * P], start=True, stop=True)
                last.then_inc(s["score_psum"], 1)

            def inter(u):
                again(pe, s["state_ready"], u)
                again(pe, s["acc_done"], u)
                for h in range(NH):
                    last = m(bank[3][:, DI + h * HD:DI + (h + 1) * HD], kqT[:, 1, h * P:(h + 1) * P],
                             state[:, h, :], start=True, stop=True)
                last.then_inc(s["inter_psum"], 1)

            def intra(u):
                pe.wait_ge(s["sd_ready"], u + 1)
                pe.wait_ge(s["x_ready"], u + 1)
                for h in range(NH):
                    last = m(bank[3][:, h * HD:(h + 1) * HD], sd[:, h, :], x_w[:, h, :], start=True, stop=True)
                last.then_inc(s["intra_psum"], 1)

            def turn_y(u):
                pe.wait_ge(s["y_ready"], u + 1)
                if not isinstance(u, int) or u + 1 < NT:
                    pe.wait_ge(s["state_ready"], u + 1)
                for c in range(2):
                    last = nc.tensor.transpose(
                        bank[1][:, c * P:(c + 1) * P],
                        ysum[:, :, :].rearrange("p h d -> p (h d)")[:, c * P:(c + 1) * P], ident[:, :])
                last.then_inc(s["yT_psum"], 1)

            def project_out(u):
                pe.wait_ge(s["yT_ready"], u + 1)
                if not isinstance(u, int) or u + 1 < NT:
                    pe.wait_ge(s["qT_ready"], u + 2)
                for c in range(2):
                    last = m(bank[3][:, 0:DM], yT[:, c * P:(c + 1) * P], w_out[:, c, :],
                             start=(c == 0), stop=(c == 1))
                last.then_inc(s["out_psum"], 1)

            def turn_block(b):
                if loaded(b):
                    pe.wait_ge(blk_in[b[0]], 16 * nth(b))
                    again(pe, f["blkT_ready"], num(b))
                    nc.tensor.transpose(bank[6][:, 0:P], blk[:, b[0], 0:DM], ident[:, :])\
                        .then_inc(f["blkT_psum"], 1)

            def expert_of(b):
                return pe.value_load(blk_e[0:1, bass.ds(num(b), 1)], min_val=0, max_val=NE - 1)

            def up(b, n, out, done):
                for c in range(FC):
                    last = m(bank[out][:, c * P:(c + 1) * P], w_up[:, b[0] % HALF, n, c * P:(c + 1) * P],
                             blkT[:, b[0] % 2, :], start=True, stop=True)
                last.then_inc(f[done], 1)

            def rise(b):
                if exists(b):
                    pe.wait_ge(f["blkT_ready"], cnt(b))
                    pe.wait_ge(up_in[b[0]], 32 * nth(b))
                    again(pe, f["gl_ready"], num(b))
                    up(b, 0, 4, "h1_psum")
                    again(pe, f["hm_ready"], num(b))
                    up(b, 1, 5, "h3_psum")

            def down(b, e):
                if not exists(b):
                    return
                pe.wait_ge(f["hm_ready"], cnt(b))
                again(pe, f["yc_ready"], num(b))
                w = w2[:, bass.ds(e, 1), :, :].rearrange("p o c d -> p (o c) d")
                for c in range(FC):
                    last = m(bank[7][:, 0:DM], hm[:, b[0] % 2, c * P:(c + 1) * P], w[:, c, :],
                             start=(c == 0), stop=(c == FC - 1))
                last.then_inc(f["y_psum"], 1)

            def begin(b):
                pe.wait_ge(lnw_ready, 1)
                pe.wait_ge(decay_ready, NH * NT)
                turn_block(b)
                turn_block(shift_by(b, 1))
                pe.wait_ge(blk_e_ready, 1)
                pe.wait_ge(w2_in, 16 * 4)

            def iteration(t, blocks):
                first, second, (b0, b1, b2) = parts(t, blocks)
                begins, ends_ = isinstance(t, int) and t == 0, isinstance(t, int) and t == NT
                ep = shift_by(b0, -1)
                ep = (ep, expert_of(ep) if exists(ep) else None)
                if first:
                    project_zx(t)
                if ends_:
                    down(*ep)
                if not isinstance(t, int) or t >= 2:
                    project_out(t - 2)
                if first:
                    project_bc(t)
                if begins:
                    begin(b0)
                if b0:
                    rise(b0)
                if second:
                    scores(t - 1)
                if b0 and not ends_:
                    down(*ep)
                    turn_block(shift_by(b0, 2))
                e0 = expert_of(b0) if b0 and exists(b0) else None
                if second:
                    inter(t - 1)
                if b1:
                    rise(b1)
                if second:
                    intra(t - 1)
                if b1:
                    down(shift_by(b1, -1), e0)
                    turn_block(shift_by(b1, 2))
                e1 = expert_of(b1) if b1 and exists(b1) else None
                if first:
                    turn_kq(t)
                if b2:
                    rise(b2)
                if b2:
                    down(shift_by(b2, -1), e1)
                    turn_block(shift_by(b2, 2))
                if first:
                    state_product(t)
                if ends_:
                    sum_betas(0)
                    sum_betas(1)
                if second:
                    turn_y(t - 1)
                if ends_:
                    sum_betas(2)
                    project_out(t - 1)
                    sum_betas(3)
            weave(pe, iteration)

        @block.scalar
        def _(act):
            a = nc.scalar.activation
            nc.scalar.preload_act_table_set("natural_log_exp_and_others")
            act.wait_ge(zero_set, 1)
            a(decay[:, :, :].rearrange("p t c -> p (t c)")[:, 0:LOADED * ROW],
              zero[:, :].to_broadcast([P, LOADED * ROW]), ACT.Copy).then_inc(rows0_set, 1)
            for b in range(NBATCH):
                act.wait_ge(xnT_psum, TB * (b + 1))
                a(xnT[:, b * SEQ:(b + 1) * SEQ], bank[b][:, :], ACT.Copy).then_inc(xnT_ready, 1)
            per = NT // 2
            for q in range(2):
                act.wait_ge(nar_psum, per * (q + 1))
                a(nar[:, q * per:(q + 1) * per, :].rearrange("p t c -> p (t c)"), bank[4 + q][:, 0:per * NARROW],
                  ACT.Copy).then_inc(nar_ready, 1)
            act.wait_ge(top_in, 1)
            a(e2, m2, ACT.Exp).then_inc(top_out, 1)
            act.wait_ge(e_in, 1)
            a(sp_e, sp_x, ACT.Exp, scale=-1.0).then_inc(e_out, 1)
            a(bet_e, nar[:, :, 2 * NH:3 * NH], ACT.Exp, scale=-1.0).then_inc(e_out, 1)
            for q in range(NBATCH):
                act.wait_ge(combT_psum, TB * (q + 1))
                a(combT4(q), bank[q % 2][0:NE, :], ACT.Copy).then_inc(combT_ready, 1)
            act.wait_ge(l_in, 1)
            a(sp_l, sp_u, ACT.Ln).then_inc(l_out, 1)
            act.wait_ge(L_psum, 1)
            a(eL[:, :, :, :].rearrange("p a t h -> p (a t h)"), bank[2][:, 0:3 * NT * NH], ACT.Exp)\
                .then_inc(L_exp, 1)
            act.wait_ge(g_ready, 1)
            a(lnG, g_t, ACT.Ln).then_inc(lng_ready, 1)
            act.wait_ge(rows0_out, 16)
            act.wait_ge(lnw_ready, 1)
            for t in range(NT):
                act.wait_ge(arm_psum, t + 1)
                for h in range(NH):
                    a(decay[:, t, h * P:(h + 1) * P], bank[4 + t % 4][:, h * P:(h + 1) * P], ACT.Exp,
                      bias=lnw[:, t, h:h + 1]).then_inc(decay_ready, 1)

            def sines(t):
                act.wait_ge(consts_set, 8)
                act.wait_ge(s["ang_ready"], t + 1)
                again(act, s["k_rot"], 2 * t)
                again(act, s["rot_pool"], 2 * t)
                a(trig[:, 0, :, :].rearrange("p h n -> p (h n)"), theta[:, bass.ds(t, 1), :].rearrange("p o c -> p (o c)"),
                  ACT.Sin, scale=TWO_PI)
                a(trig[:, 1, :, :].rearrange("p h n -> p (h n)"), ang[:, :], ACT.Sin, scale=-TWO_PI,
                  bias=half_pi[:, 0:1]).then_inc(s["trig_ready"], 1)

            def squares(t):
                act.wait_ge(s["bc_psum"], t + 1)
                again(act, s["k_rot"], 2 * t)
                for n in range(2):
                    a(flat_rot[:, n * DS:(n + 1) * DS], bank[1][:, n * DS:(n + 1) * DS], ACT.Square,
                      accum_out=ms[:, n:n + 1]).then_inc(s["sq_done"], 1)

            def out_kq(t):
                act.wait_ge(s["kT_psum"], t + 1)
                a(kqT[:, 0, :], bank[2][:, :], ACT.Copy).then_inc(s["kT_ready"], 1)
                act.wait_ge(s["qT_psum"], t + 1)
                a(kqT[:, 1, :], bank[3][:, :], ACT.Copy).then_inc(s["qT_ready"], 1)

            def gates(t):
                act.wait_ge(s["zx_psum"], t + 1)
                act.wait_ge(s["xs_ready"], t + 1)
                again(act, s["y_ready"], t)
                a(gate[:, :], bank[0][:, 0:DI], ACT.Silu).then_inc(s["gate_ready"], 1)
                again(act, s["intra_psum"], t)
                again(act, s["xd_ready"], t)
                a(x_w[:, :, :].rearrange("p h d -> p (h d)"), bank[0][:, DI:2 * DI], ACT.Copy)\
                    .then_inc(s["x_ready"], 1)

            def out_y(u):
                act.wait_ge(s["yT_psum"], u + 1)
                again(act, s["out_psum"], u)
                a(yT[:, :], bank[1][:, 0:DI], ACT.Copy).then_inc(s["yT_ready"], 1)

            def out_block(b):
                if loaded(b):
                    act.wait_ge(f["blkT_psum"], cnt(b))
                    a(blkT[:, b[0] % 2, :], bank[6][:, 0:P], ACT.Copy).then_inc(f["blkT_ready"], 1)

            def silu(b):
                if exists(b):
                    act.wait_ge(f["h1_psum"], cnt(b))
                    again(act, f["hm_ready"], num(b))
                    a(gl, bank[4][:, :], ACT.Silu).then_inc(f["gl_ready"], 1)

            def scale_y(b):
                if exists(b):
                    old = shift_by(b, -HALF)
                    act.wait_ge(f["rw_ready"], cnt(b))
                    act.wait_ge(f["yc_ready"], cnt(b))
                    if exists(old):
                        act.wait_ge(res_out[old[0]], 16 * nth(old))
                    a(res[:, b[0] % HALF, :], yc[:, :], ACT.Copy, scale=rw[:, 0:1]).then_inc(f["res_ready"], 1)

            def iteration(t, blocks):
                first, second, (b0, b1, b2) = parts(t, blocks)
                begins = isinstance(t, int) and t == 0
                if begins:
                    nc.scalar.preload_act_table_set("silu_and_others")
                    squares(t)
                    out_block(b0)
                    out_block(b1)
                if first:
                    sines(t)
                if begins:
                    gates(t)
                elif first:
                    squares(t)
                for b in (b0, b1):
                    if b:
                        if not (begins and b is b0):
                            out_block(shift_by(b, 1))
                        silu(b)
                        scale_y(shift_by(b, -2))
                if b2:
                    out_block(shift_by(b2, 1))
                if first:
                    out_kq(t)
                if b2:
                    silu(b2)
                if first and not begins:
                    gates(t)
                if b2:
                    scale_y(shift_by(b2, -2))
                if second:
                    out_y(t - 1)
            weave(act, iteration)

        @block.vector
        def _(dve):
            v = nc.vector
            tt, ts, stt = v.tensor_tensor, v.tensor_scalar, v.scalar_tensor_tensor
            n = [0]

            def link(ins):
                n[0] += 1
                ins.then_inc(dve_step, 1)
                dve.wait_ge(dve_step, n[0])

            v.memset(zero[:, :], 0.0).then_inc(zero_set, 1)
            v.memset(state[:, :, :], 0.0)
            v.memset(zer, 0.0)
            def of(b):
                return slice(b * TB, (b + 1) * TB)

            def moments(b):
                dve.wait_ge(x_in[b], 16)
                for t in range(b * TB, (b + 1) * TB):
                    last = v.bn_stats(stats[:, t, :], acc[:, t, :])
                link(last)
                for t in range(b * TB, (b + 1) * TB):
                    last = v.bn_aggr(mvx[:, t, :], stats[:, t, :])
                link(last)
                ts(vx[:, of(b)], mvx[:, of(b), 1], EPS, None, ALU.add).then_inc(var_ready, 1)

            def normalise(b):
                dve.wait_ge(rstd_ready, b + 1)
                for t in range(b * TB, (b + 1) * TB):
                    ts(xrow[:, t, 0:DM], acc[:, t, :], mvx[:, t, 0:1], rx[:, t:t + 1], ALU.subtract, ALU.mult)\
                        .then_inc(xn_ready, 1)
            moments(0)
            for b in range(1, NBATCH):
                moments(b)
                normalise(b - 1)
            normalise(NBATCH - 1)
            dve.wait_ge(small_in, 16 * 9)
            dve.wait_ge(nar_ready, 2)
            link(tt(lg, nar[:, :, NARROW - NE:], bc(br[:, :], NT, 0), ALU.add))
            link(v.tensor_reduce(m1, lg, X, ALU.max))

            def pick_top(src, mx, onehot):
                link(tt(rt, src, bc(mx, NE, 1), ALU.is_equal))
                link(stt(sc1, rt, -float(NE), bc(iota_e[:, :], NT, 0), ALU.mult, ALU.add))
                link(v.tensor_reduce(posb[:, 0, :], sc1, X, ALU.min))
                link(tt(onehot, sc1, bc(posb[:, 0, :], NE, 1), ALU.is_equal))
            pick_top(lg, m1, oh1)
            link(stt(lg, oh1, NEG, lg, ALU.mult, ALU.add))
            link(v.tensor_reduce(m2, lg, X, ALU.max))
            pick_top(lg, m2, oh2)
            tt(both_h, oh1, oh2, ALU.add).then_inc(both_ready, 1)
            tt(m2, m2, m1, ALU.subtract).then_inc(top_in, 1)
            sp4 = sp_t.rearrange("p a (t h) -> p a t h", h=NH)
            tt(sp4[:, 0], nar[:, :, 0:NH], bc(dtb[:, :], NT, 0), ALU.add)
            link(v.tensor_copy(sp4[:, 1], nar[:, :, NH:2 * NH]))
            stt(sp_x, sp_t, -1.0, sp_t, ALU.mult, ALU.max).then_inc(e_in, 1)
            dve.wait_ge(top_out, 1)
            link(ts(m1, e2, 1.0, None, ALU.add))
            link(v.reciprocal(wtop[:, 0, :], m1))
            link(tt(wtop[:, 1, :], wtop[:, 0, :], e2, ALU.mult))
            v.tensor_copy(xrow[:, :, DM:DM + 1].rearrange("p t o -> p (t o)"), wtop[:, 0, :]).then_inc(row_meta, 1)
            dve.wait_ge(pos_psum, 1)
            link(ts(cnt_b, bank[1][:, 0:NE], 1.0 / P, (P - 1) / P - (P - 1) / (2.0 * P), ALU.mult, ALU.add))
            link(ts(cnt_b, cnt_b, MAGIC, -MAGIC, ALU.add, ALU.add))
            link(v.tensor_tensor_scan(ends, cnt_b, zer, 0.0, ALU.add, ALU.add))
            link(tt(base, ends, cnt_b, ALU.subtract))
            link(ts(base, base, float(P), -1.0, ALU.mult, ALU.add))
            link(tt(posb, bank[0][:, 0:NT * NE].rearrange("p (t e) -> p t e", e=NE), bc(base, NT, 0), ALU.add))
            for k, oh in enumerate((oh1, oh2)):
                link(tt(pick, oh, posb, ALU.mult))
                link(v.tensor_reduce(slots_f[:, k, :], pick, X, ALU.add))
                v.tensor_copy(slots[:, k, :], slots_f[:, k, :]).then_inc(slots_ready, 1)
            link(tt(cmpb, bc(ends[0:1, :], LOADED, 0), bc(iota_b[:, :], NE, 1), ALU.is_le))
            link(v.tensor_reduce(blkf, cmpb, X, ALU.add))
            ts(blk_e[:, :], blkf, float(NE - 1), None, ALU.min).then_inc(blk_e_ready, 1)
            link(tt(comb, oh1, bc(wtop[:, 0, :], NE, 1), ALU.mult))
            link(tt(pick, oh2, bc(wtop[:, 1, :], NE, 1), ALU.mult))
            tt(comb, comb, pick, ALU.add).then_inc(comb_ready, 1)
            dve.wait_ge(comb_ready, 1)
            v.memset(base[0:1, 0:1], 0.0).then_inc(pos_used, 1)
            dve.wait_ge(e_out, 2)
            link(ts(sp_u, sp_e, 1.0, None, ALU.add))
            ts(sp_x, sp_u, 1.0, None, ALU.subtract).then_inc(l_in, 1)
            dve.wait_ge(l_in, 1)
            link(tt(sp_e, sp_e, sp_x, ALU.subtract))
            link(v.reciprocal(sp_r, sp_u))
            link(tt(sp_e, sp_e, sp_r, ALU.mult))
            link(stt(sp_e, sp_t, 0.0, sp_e, ALU.max, ALU.add))
            link(ts(bet_e, bet_e, 1.0, None, ALU.add))
            v.reciprocal(bet, bet_e).then_inc(bet_ready, 1)
            dve.wait_ge(bet_ready, 1)
            dve.wait_ge(l_out, 1)
            link(tt(sp.rearrange("p a t h -> p a (t h)"), sp_l, sp_e, ALU.add))
            dt_v = sp[:, 0]
            link(ts(g_t, sp[:, 1], -1.0, -A_FLOOR, ALU.mult, ALU.min))
            tt(adt, g_t, dt_v, ALU.mult).then_inc(adt_ready, 1)
            dve.wait_ge(betn_psum, 1)
            link(ts(g_t, bank[3][:, 0:NT * NH].rearrange("p (t h) -> p t h", h=NH), -1.0, 1.0, ALU.mult, ALU.add))
            link(tt(g_t, g_t, dt_v, ALU.mult))
            link(tt(own[:, :, :], bet, dt_v, ALU.mult))
            link(tt(coefG, own[:, :, :], g_t, ALU.add))
            ts(g_t, coefG, TINY, None, ALU.max).then_inc(g_ready, 1)
            dve.wait_ge(L_exp, 1)
            link(tt(wstate[:, :, :], coefG, eL[:, 1], ALU.mult))
            for z in (wstate[:, :, :], eL[:, 2]):
                for b in range(NBATCH):
                    last = v.memset(z[:, (b + 1) * TB - 1, :], 0.0)
            link(last)
            dve.wait_ge(lng_ready, 1)
            tt(lnw[:, :, :], lnG, bank[2][:, 0:NT * NH].rearrange("p (t h) -> p t h", h=NH), ALU.subtract)\
                .then_inc(lnw_ready, 1)
            def token(t):
                again(dve, s["zx_psum"], t)
                ts(xt_s[:, :], xnT[:, bass.ds(t * P, P)], 1.0, None, ALU.mult).then_inc(s["xt_ready"], 1)
                again(dve, s["trig_ready"], t)
                th = theta[:, bass.ds(t, 1), :].rearrange("p o c -> p (o c)")
                stt(ang[:, :], th, -1.0, th, ALU.mult, ALU.max).then_inc(s["ang_ready"], 1)

            def diagonal(t):
                dve.wait_ge(decay_ready, NH * (t + 1))
                for h in range(NH):
                    d_h = decay[:, t, h * P:(h + 1) * P]
                    stt(d_h, ident[:, :], own[:, t, h:h + 1], d_h, ALU.mult, ALU.add).then_inc(decay_done, 1)
            link(ts(dtp, dt_v, INV_2PI, None, ALU.mult))
            for t in range(NT):
                last = tt(turns[:, t, :].rearrange("p (h n) -> p h n", n=NA),
                          bc(nar[:, t, 3 * NH:3 * NH + NA], NH, 0), bc(dtp[:, t, :], NA, 1), ALU.mult)
            link(last)
            u4 = turns.rearrange("p (b j) c -> p b j c", j=TB)
            link(v.tensor_copy(tpre[:, :, 0], u4[:, :, 0]))
            for j in range(1, TB - 1):
                last = tt(tpre[:, :, j], tpre[:, :, j - 1], u4[:, :, j], ALU.add)
                if j < TB - 2:
                    link(last)
            last.then_inc(turns_ready, 1)

            def cut_turns(b):
                dve.wait_ge(theta_psum, b + 1)
                again(dve, theta_ready, b)
                ts(cut_, bank[b % 2][:, :], MAGIC, -MAGIC, ALU.add, ALU.add).then_inc(turns_cut, 1)
                dve.wait_ge(turns_cut, b + 1)
                tt(theta[:, b * TB:(b + 1) * TB, :].rearrange("p j c -> p (j c)"), bank[b % 2][:, :], cut_,
                   ALU.subtract).then_inc(theta_ready, 1)

            def add_betas(q):
                dve.wait_ge(beta_psum, TB * (q + 1))
                dve.wait_ge(s["acc_done"], TB * (q + 1))
                a4 = acc[:, q * TB:(q + 1) * TB, :].rearrange("p t d -> p (t d)")
                tt(a4, a4, bank[SPARE[q]][:, :], ALU.add).then_inc(acc_ready, 1)

            for t in range(NT):
                diagonal(t)
                if t == NT - 4:
                    token(0)
                if t % 2 and 3 <= t < 3 + 2 * NBATCH:
                    cut_turns((t - 3) // 2)

            def at(tile, t, k=None):
                x = tile[:, bass.ds(t, 1), :] if k is None else tile[:, k, bass.ds(t, 1), :]
                return x.rearrange("p o h -> p (o h)")

            def mean_square(t):
                dve.wait_ge(s["sq_done"], 2 * (t + 1))
                again(dve, s["rms_ready"], t)
                ts(ms[:, :], ms[:, :], 1.0 / DS, EPS, ALU.mult, ALU.add).then_inc(s["ms_ready"], 1)

            def weigh(t):
                dve.wait_ge(s["zx_psum"], t + 1)
                again(dve, s["state_psum"], t)
                tt(xs_w[:, :, :], bank[0][:, DI:2 * DI].rearrange("p (h d) -> p h d", d=HD),
                   bc(at(wstate, t), HD, 1), ALU.mult).then_inc(s["xs_ready"], 1)

            def norm_kq(t):
                dve.wait_ge(s["rms_ready"], t + 1)
                for q in range(2):
                    last = stt(bn_kq[:, q, :], bank[1][:, q * DS:(q + 1) * DS], rms[:, q:q + 1], nw_kq[:, q, :],
                               ALU.mult, ALU.mult)
                last.then_inc(s["bn_ready"], 1)
                dve.wait_ge(s["bn_ready"], t + 1)
                again(dve, s["state_psum"], t)
                tt(kq[:, 1], bc(bn_kq[:, 1, :], NH, 0), bias_kq[:, 1], ALU.add).then_inc(s["q0_ready"], 1)

            def rot_cosine(t):
                dve.wait_ge(s["k0_ready"], t + 1)
                dve.wait_ge(s["q0_ready"], t + 1)
                dve.wait_ge(s["trig_ready"], t + 1)
                cs = bc(trig[:, 1, :, :], 2, 0)
                x1, x2 = kq[:, :, :, 0:NA], kq[:, :, :, NA:2 * NA]
                tt(rot[:, 0], x1, cs, ALU.mult).then_inc(s["rot_dve"], 1)
                tt(rot[:, 2], x2, cs, ALU.mult).then_inc(s["rot_dve"], 1)

            def rotate(t):
                dve.wait_ge(s["rot_dve"], 2 * (t + 1))
                dve.wait_ge(s["rot_pool"], 2 * (t + 1))
                x1, x2 = kq[:, :, :, 0:NA], kq[:, :, :, NA:2 * NA]
                tt(x1, rot[:, 0], rot[:, 1], ALU.subtract).then_inc(s["k_rot"], 1)
                tt(x2, rot[:, 2], rot[:, 3], ALU.add).then_inc(s["k_rot"], 1)

            def mask(u):
                dve.wait_ge(decay_done, NH * NT)
                dve.wait_ge(s["score_psum"], u + 1)
                if not isinstance(u, int) or u + 1 < NT:
                    dve.wait_ge(s["k0_ready"], u + 2)
                    dve.wait_ge(s["q0_ready"], u + 2)
                tt(sd[:, :, :].rearrange("p h i -> p (h i)"), bank[2][:, :],
                   decay[:, bass.ds(u, 1), :].rearrange("p o c -> p (o c)"), ALU.mult).then_inc(s["sd_ready"], 1)

            def from_state(u):
                dve.wait_ge(s["inter_psum"], u + 1)
                dve.wait_ge(s["intra_psum"], u + 1)
                again(dve, s["yT_psum"], u)
                tt(ysum[:, :, :], bank[3][:, DI:2 * DI].rearrange("p (h d) -> p h d", d=HD),
                   bc(at(eL, u, 0), HD, 1), ALU.mult).then_inc(s["y1_ready"], 1)

            def fade(u):
                dve.wait_ge(s["inter_psum"], u + 1)
                tt(state[:, :, :], state[:, :, :], bc(at(eL, u, 2), HD, 1), ALU.mult).then_inc(s["state_dec"], 1)

            def carry(u):
                dve.wait_ge(s["state_psum"], u + 1)
                dve.wait_ge(s["state_dec"], u + 1)
                tt(state[:, :, :], state[:, :, :], bank[1][:, DI:2 * DI].rearrange("p (h d) -> p h d", d=HD), ALU.add)\
                    .then_inc(s["state_ready"], 1)

            def join(u):
                dve.wait_ge(s["intra_psum"], u + 1)
                dve.wait_ge(s["y1_ready"], u + 1)
                tt(ysum[:, :, :], ysum[:, :, :], bank[3][:, 0:DI].rearrange("p (h d) -> p h d", d=HD), ALU.add)\
                    .then_inc(s["y2_ready"], 1)

            def gate_y(u):
                dve.wait_ge(s["y2_ready"], u + 1)
                dve.wait_ge(s["xd_ready"], u + 1)
                tt(ysum[:, :, :], ysum[:, :, :], xd_w[:, :, :], ALU.add).then_inc(s["y3_ready"], 1)
                dve.wait_ge(s["y3_ready"], u + 1)
                dve.wait_ge(s["gate_ready"], u + 1)
                tt(ysum[:, :, :].rearrange("p h d -> p (h d)"), ysum[:, :, :].rearrange("p h d -> p (h d)"),
                   gate[:, :], ALU.mult).then_inc(s["y_ready"], 1)

            def add_out(u):
                dve.wait_ge(s["out_psum"], u + 1)
                o = acc[:, bass.ds(u, 1), :].rearrange("p o d -> p (o d)")
                tt(o, o, bank[3][:, 0:DM], ALU.add).then_inc(s["acc_done"], 1)

            def product(b):
                if not exists(b):
                    return
                dve.wait_ge(f["h3_psum"], cnt(b))
                dve.wait_ge(f["gl_ready"], cnt(b))
                if exists(shift_by(b, -2)):
                    dve.wait_ge(f["y_psum"], cnt(shift_by(b, -2)))
                tt(hm[:, b[0] % 2, :], gl, bank[5][:, :], ALU.mult).then_inc(f["hm_ready"], 1)

            def norm_y(b):
                if not exists(b):
                    return
                e = dve.value_load(blk_e[0:1, bass.ds(num(b), 1)], min_val=0, max_val=NE - 1)
                dve.wait_ge(f["y_psum"], cnt(b))
                v.bn_stats(st6[:, :], bank[7][:, 0:DM]).then_inc(f["st_ready"], 1)
                dve.wait_ge(gam_in, 16)
                dve.wait_ge(f["st_ready"], cnt(b))
                again(dve, f["rstd_ready"], num(b))
                v.bn_aggr(mv[:, :], st6[:, :]).then_inc(f["mv_ready"], 1)
                dve.wait_ge(f["mv_ready"], cnt(b))
                ts(mv[:, 1:2], mv[:, 1:2], EPS, None, ALU.add).then_inc(f["ve_ready"], 1)
                again(dve, f["res_ready"], num(b))
                stt(yc[:, :], bank[7][:, 0:DM], mv[:, 0:1], gam[:, bass.ds(e, 1), :].rearrange("p o d -> p (o d)"),
                    ALU.subtract, ALU.mult).then_inc(f["yc_ready"], 1)

            def iteration(t, blocks):
                first, second, (b0, b1, b2) = parts(t, blocks)
                if isinstance(t, int) and t == 1:
                    dve.wait_ge(blk_e_ready, 1)
                    dve.wait_ge(gam_in, 16)
                if first and not (isinstance(t, int) and t == 0):
                    token(t)
                if b0:
                    norm_y(shift_by(b0, -2))
                if not first:
                    norm_y(shift_by(b1, -2))
                if not isinstance(t, int) or t >= 2:
                    add_out(t - 2)
                if first:
                    weigh(t)
                    mean_square(t)
                    norm_kq(t)
                if b0:
                    product(b0)
                if second:
                    mask(t - 1)
                if b1 and first:
                    norm_y(shift_by(b1, -2))
                if first:
                    rot_cosine(t)
                if second and first:
                    fade(t - 1)
                if first:
                    rotate(t)
                if second:
                    from_state(t - 1)
                    join(t - 1)
                if b1:
                    product(b1)
                if b2:
                    norm_y(shift_by(b2, -2))
                if second:
                    gate_y(t - 1)
                if second and first:
                    carry(t - 1)
                if b2:
                    product(b2)
            weave(dve, iteration)
            d = decay[:, :, :].rearrange("p t c -> p (t c)")

            def add_results(q):
                dve.wait_ge(acc_ready, -(-PARTS[q + 1] // TB))
                dve.wait_ge(res_in[q], 16 * TOPK)
                c, w = PARTS[q] * DM, (PARTS[q + 1] - PARTS[q]) * DM
                a4 = acc[:, PARTS[q]:PARTS[q + 1], :].rearrange("p t d -> p (t d)")
                tt(a4, a4, d[:, c:c + w], ALU.add).then_inc(fin_a, 1)
                dve.wait_ge(fin_a, q + 1)
                tt(a4, a4, d[:, T + c:T + c + w], ALU.add).then_inc(fin_ready, 1)
            for q in range(NBATCH - 1):
                add_betas(q)
            add_results(0)
            add_out(NT - 1)
            add_betas(NBATCH - 1)
            for q in range(1, NBATCH):
                add_results(q)


_INS = ['L0_attn_u', 'L0_attn_W_in', 'L0_attn_W_out', 'L0_attn_dt_bias', 'L0_attn_B_bias', 'L0_attn_C_bias',
        'L0_attn_B_norm_w', 'L0_attn_C_norm_w', 'L0_attn_D', 'L0_ffn_Wr', 'L0_ffn_br', 'L0_ffn_W1', 'L0_ffn_W3',
        'L0_ffn_W2', 'L0_ffn_gamma', 'L0_ffn_beta']


def kernel(**inputs):
    import numpy as _np
    import concourse.bacc as _bacc
    from concourse import mybir as _mybir
    from concourse.bass_utils import run_bass_kernel_spmd as _run

    nc = _bacc.Bacc("TRN2", target_bir_lowering=False, num_devices=1)
    arrays, args = {}, []
    for name in _INS:
        a = _np.ascontiguousarray(inputs[name])
        arrays[f"in_{name}_dram"] = a
        args.append(nc.dram_tensor(f"in_{name}_dram", a.shape, _mybir.dt.from_np(a.dtype), kind="ExternalInput").ap())
    u = inputs['L0_attn_u']
    out = nc.dram_tensor("out_0_dram", tuple(u.shape), _mybir.dt.float32, kind="ExternalOutput").ap()
    build(nc, *args, out)
    r = _run(nc, [arrays], core_ids=[0])
    return r.results[0]["out_0_dram"]
```
